# Optimizing a Trainium2 kernel written in Bass

```python
import numpy as np
import jax
import jax.numpy as jnp

def _softmax(x, axis=-1):
    return jax.nn.softmax(x, axis=axis)

def _gelu(x):
    return jax.nn.gelu(x, approximate=True)

def _silu(x):
    return jax.nn.silu(x)

def _sigmoid(x):
    return jax.nn.sigmoid(x)

def _layernorm(x, axis=-1, eps=1e-05):
    m = jnp.mean(x, axis=axis, keepdims=True)
    v = jnp.var(x, axis=axis, keepdims=True)
    return (x - m) / jnp.sqrt(v + eps)

def _scatter_add(tgt, idx, src, axis=0):
    return tgt.at[idx].add(src)

def _segment_sum(src, seg, n):
    return jax.ops.segment_sum(src, seg, n)
kernel_name = 'mk_xattn_ffn_d4_seqx_r4_ac1889'

def setup_inputs(seed: int=0):
    np.random.seed(seed)
    _w = jnp.asarray

    def _rec_inputs():
        import jax
        import jax.numpy as jnp
        _rk = jax.random.key(seed)
        x = -0.0003929 + 0.9999 * jax.random.normal(jax.random.fold_in(_rk, 1), (16, 256, 256), jnp.float32)
        _lenS = 256 - jax.random.randint(jax.random.fold_in(_rk, 7), (16,), 0, max(1, 256 // 4) + 1, jnp.int32)
        _lenS2 = 120 - jax.random.randint(jax.random.fold_in(_rk, 8), (16,), 0, max(1, 120 // 4) + 1, jnp.int32)
        _ctx_768P = jax.random.normal(jax.random.fold_in(_rk, 11), (16, 16, 192), jnp.float32)
        _ctx_768c = jax.random.dirichlet(jax.random.fold_in(_rk, 511), 0.3 * jnp.ones((16,), jnp.float32), (16, 120))
        _ctx_768t = jnp.einsum('bsk,bkd->bsd', _ctx_768c, _ctx_768P)
        _ctx_768t = _ctx_768t * jax.lax.rsqrt(jnp.mean(jnp.square(_ctx_768t)) + 1e-12) * 0.953939
        ctx_768 = 2.09791e-05 + 1.00001 * (_ctx_768t + 0.3 * jax.random.normal(jax.random.fold_in(_rk, 611), (16, 120, 192), jnp.float32))
        _validS = jnp.arange(256)[None, :] < _lenS[:, None]
        _validS2 = jnp.arange(120)[None, :] < _lenS2[:, None]
        _causal = jnp.tril(jnp.ones((256, 256), dtype=bool))
        mask_BxS_bf1 = jnp.ones((16, 256), dtype=bool)
        mask_BxS2_bf1 = jnp.ones((16, 120), dtype=bool)
        return (x, ctx_768, mask_BxS_bf1, mask_BxS2_bf1)
    x, ctx_768, mask_BxS_bf1, mask_BxS2_bf1 = _rec_inputs()

    def _L0_xattn_setup():
        import jax, jax.numpy as jnp
        import numpy as np
        HEADS = 8
        DIM_HEAD = 64
        QUERY_DIM = 256
        CONTEXT_DIM = 192
        INNER = HEADS * DIM_HEAD
        key = jax.random.key(seed)
        ks = jax.random.split(key, 7)
        B, Sq, Skv = (4, 1024, 256)
        x = jax.random.normal(ks[0], (B, Sq, QUERY_DIM), dtype=jnp.float32)
        context = jax.random.normal(ks[1], (B, Skv, CONTEXT_DIM), dtype=jnp.float32)
        Wq = jax.random.normal(ks[2], (QUERY_DIM, INNER), dtype=jnp.float32) * QUERY_DIM ** (-0.5)
        Wk = jax.random.normal(ks[3], (CONTEXT_DIM, INNER), dtype=jnp.float32) * CONTEXT_DIM ** (-0.5)
        Wv = jax.random.normal(ks[4], (CONTEXT_DIM, INNER), dtype=jnp.float32) * CONTEXT_DIM ** (-0.5)
        Wo = jax.random.normal(ks[5], (INNER, QUERY_DIM), dtype=jnp.float32) * INNER ** (-0.5)
        bo = jax.random.normal(ks[6], (QUERY_DIM,), dtype=jnp.float32) * 0.01
        return {'x': x, 'context': context, 'Wq': Wq, 'Wk': Wk, 'Wv': Wv, 'Wo': Wo, 'bo': bo}
    _L0_xattn_all = _L0_xattn_setup()
    _L0_xattn_in = {k: v for k, v in _L0_xattn_all.items() if k in ('Wq', 'Wk', 'Wv', 'Wo', 'bo')}
    del _L0_xattn_all

    def _L0_ffn_setup():
        import jax, jax.numpy as jnp
        import numpy as np
        QMAX = 127.0
        EPS = 1e-08

        def _quantize_per_token(x):
            amax = jnp.clip(jnp.max(jnp.abs(x), axis=-1, keepdims=True), EPS, None)
            scale = amax / QMAX
            x_q = jnp.clip(jnp.round(x / scale), -128, 127)
            return (x_q, scale)

        def _quantize_per_channel(w):
            amax = jnp.clip(jnp.max(jnp.abs(w), axis=-1, keepdims=True), EPS, None)
            scale = amax / QMAX
            w_q = jnp.clip(jnp.round(w / scale), -128, 127)
            return (w_q, scale)
        key = jax.random.key(seed)
        k1, k2, k3 = jax.random.split(key, 3)
        B, S, DIN, DOUT = (8, 1024, 256, 256)
        x = jax.random.normal(k1, (B, S, DIN), dtype=jnp.float32)
        weight = jax.random.normal(k2, (DOUT, DIN), dtype=jnp.float32) * 0.02
        bias = jax.random.normal(k3, (DOUT,), dtype=jnp.float32)
        return {'x': x, 'weight': weight, 'bias': bias}
    _L0_ffn_all = _L0_ffn_setup()
    _L0_ffn_in = {k: v for k, v in _L0_ffn_all.items() if k in ('weight', 'bias')}
    del _L0_ffn_all

    def _L1_xattn_setup():
        import jax, jax.numpy as jnp
        import numpy as np
        N_HEADS = 16
        DIMS = 256
        D_CTX = 192
        HEAD = DIMS // N_HEADS
        key = jax.random.key(seed)
        ks = jax.random.split(key, 10)
        s_q = 1.0 / np.sqrt(DIMS)
        s_c = 1.0 / np.sqrt(D_CTX)
        return {'x': jax.random.normal(ks[0], (2, 512, DIMS), jnp.float32), 'context': jax.random.normal(ks[1], (2, 512, D_CTX), jnp.float32), 'w_q': jax.random.normal(ks[2], (DIMS, DIMS), jnp.float32) * s_q, 'b_q': jax.random.normal(ks[3], (DIMS,), jnp.float32) * 0.01, 'w_k': jax.random.normal(ks[4], (D_CTX, DIMS), jnp.float32) * s_c, 'b_k': jax.random.normal(ks[5], (DIMS,), jnp.float32) * 0.01, 'w_v': jax.random.normal(ks[6], (D_CTX, DIMS), jnp.float32) * s_c, 'b_v': jax.random.normal(ks[7], (DIMS,), jnp.float32) * 0.01, 'w_o': jax.random.normal(ks[8], (DIMS, DIMS), jnp.float32) * s_q, 'b_o': jax.random.normal(ks[9], (DIMS,), jnp.float32) * 0.01}
    _L1_xattn_all = _L1_xattn_setup()
    _L1_xattn_in = {k: v for k, v in _L1_xattn_all.items() if k in ('w_q', 'b_q', 'w_k', 'b_k', 'w_v', 'b_v', 'w_o', 'b_o')}
    del _L1_xattn_all

    def _L1_ffn_setup():
        import jax, jax.numpy as jnp
        import numpy as np
        B, S, H, E = (2, 512, 256, 16)
        key = jax.random.key(seed)
        k0, k1, k2, k3 = jax.random.split(key, 4)
        tokens = jax.random.normal(k0, (B, S, H), dtype=jnp.float32)
        gate_w = jax.random.normal(k1, (E, H), dtype=jnp.float32) * H ** (-0.5)
        expert_w = jax.random.normal(k2, (E, H, H), dtype=jnp.float32) * H ** (-0.5)
        expert_b = jax.random.normal(k3, (E, H), dtype=jnp.float32) * 0.01
        return {'tokens': tokens, 'gate_w': gate_w, 'expert_w': expert_w, 'expert_b': expert_b}
    _L1_ffn_all = _L1_ffn_setup()
    _L1_ffn_in = {k: v for k, v in _L1_ffn_all.items() if k in ('gate_w', 'expert_w', 'expert_b')}
    del _L1_ffn_all

    def _L2_xattn_setup():
        import jax, jax.numpy as jnp
        import numpy as np
        HEADS = 8
        DIM_HEAD = 128
        ATTN_MATRIX_SCALE = 1.5
        SCALE = DIM_HEAD ** (-0.5)

        def _split_heads(t):
            b, n, _ = t.shape
            t = t.reshape(b, n, HEADS, DIM_HEAD)
            return t.transpose(2, 0, 1, 3).reshape(HEADS, b * n, DIM_HEAD)
        key = jax.random.key(seed)
        ks = jax.random.split(key, 7)
        b, n, m = (2, 512, 512)
        qd, cd, inner = (256, 192, HEADS * DIM_HEAD)
        x = jax.random.normal(ks[0], (b, n, qd), dtype=jnp.float32)
        context = jax.random.normal(ks[1], (b, m, cd), dtype=jnp.float32)
        Wq = jax.random.normal(ks[2], (qd, inner), dtype=jnp.float32) * qd ** (-0.5)
        Wk = jax.random.normal(ks[3], (cd, inner), dtype=jnp.float32) * cd ** (-0.5)
        Wv = jax.random.normal(ks[4], (cd, inner), dtype=jnp.float32) * cd ** (-0.5)
        Wout = jax.random.normal(ks[5], (inner, qd), dtype=jnp.float32) * inner ** (-0.5)
        bout = jnp.zeros((qd,), dtype=jnp.float32)
        return {'x': x, 'context': context, 'Wq': Wq, 'Wk': Wk, 'Wv': Wv, 'Wout': Wout, 'bout': bout}
    _L2_xattn_all = _L2_xattn_setup()
    _L2_xattn_in = {k: v for k, v in _L2_xattn_all.items() if k in ('Wq', 'Wk', 'Wv', 'Wout', 'bout')}
    del _L2_xattn_all

    def _L2_ffn_setup():
        import jax, jax.numpy as jnp
        import numpy as np
        B, S, D_IN, D_OUT = (16, 1024, 256, 256)
        ACT_BITS = 8
        QB = float(2 ** (ACT_BITS - 1) - 1)
        key = jax.random.key(seed)
        k1, k2, k3 = jax.random.split(key, 3)
        x = jax.random.normal(k1, (B, S, D_IN), dtype=jnp.float32)
        ternary_weight = jax.random.randint(k2, (D_OUT, D_IN), 0, 3, dtype=jnp.int32)
        bias = jax.random.normal(k3, (D_OUT,), dtype=jnp.float32)
        act_scale = (jnp.max(jnp.abs(x)) / QB).astype(jnp.float32)
        return {'x': x, 'ternary_weight': ternary_weight, 'bias': bias, 'act_scale': act_scale}
    _L2_ffn_all = _L2_ffn_setup()
    _L2_ffn_in = {k: v for k, v in _L2_ffn_all.items() if k in ('ternary_weight', 'bias', 'act_scale')}
    del _L2_ffn_all

    def _L3_xattn_setup():
        import jax, jax.numpy as jnp
        import numpy as np
        B, T, DT, G, DV = (16, 128, 256, 144, 192)
        H, DH = (4, 32)
        INNER = H * DH
        HID = 4 * DT
        N_STATE = 64
        K_TOP = 32

        def layernorm(x, g, b, eps=1e-05):
            m = x.mean(-1, keepdims=True)
            v = x.var(-1, keepdims=True)
            return (x - m) * jax.lax.rsqrt(v + eps) * g + b

        def s4d(x, log_dt, A_re, A_im, C_re, C_im, D_skip):
            Bb, L, D = x.shape
            dt = jnp.exp(log_dt)
            A = A_re + 1j * A_im
            C = C_re + 1j * C_im
            dtA = dt[:, None] * A
            dC = C * (jnp.exp(dtA) - 1.0) / A
            powers = jnp.exp(dtA[:, :, None] * jnp.arange(L))
            K = 2.0 * jnp.einsum('dn,dnl->dl', dC, powers).real
            n = 2 * L
            Kf = jnp.fft.rfft(K, n=n, axis=-1)
            xf = jnp.fft.rfft(x, n=n, axis=1)
            y = jnp.fft.irfft(xf * Kf.T[None], n=n, axis=1)[:, :L]
            return y + x * D_skip
        key = jax.random.key(seed)
        ks = jax.random.split(key, 16)
        s = 0.02
        inp = {'x_text': jax.random.normal(ks[0], (B, T, DT), jnp.float32), 'x_vision': jax.random.normal(ks[1], (B, G, DV), jnp.float32), 'text_mask': jnp.ones((B, T), bool), 'vision_mask': jnp.ones((B, G), bool), 'Wq': jax.random.normal(ks[2], (DT, INNER), jnp.float32) * s, 'Wk': jax.random.normal(ks[3], (DV, INNER), jnp.float32) * s, 'Wv': jax.random.normal(ks[4], (DV, DT), jnp.float32) * s, 'W_film_in': jax.random.normal(ks[5], (DT, 2 * DT), jnp.float32) * s, 'b_film_in': jnp.zeros((2 * DT,), jnp.float32), 'W_film_out': jax.random.normal(ks[6], (DT, 2 * DT), jnp.float32) * s, 'b_film_out': jnp.zeros((2 * DT,), jnp.float32), 'g_norm_in': jnp.ones((DT,), jnp.float32), 'b_norm_in': jnp.zeros((DT,), jnp.float32), 'g_norm_out': jnp.ones((DT,), jnp.float32), 'b_norm_out': jnp.zeros((DT,), jnp.float32), 'g_ffn': jnp.ones((DT,), jnp.float32), 'b_ffn': jnp.zeros((DT,), jnp.float32), 'W1': jax.random.normal(ks[7], (DT, HID), jnp.float32) * s, 'b1': jnp.zeros((HID,), jnp.float32), 'W2': jax.random.normal(ks[8], (HID, DT), jnp.float32) * s, 'b2': jnp.zeros((DT,), jnp.float32), 'log_dt': jnp.log(0.001) + jax.random.uniform(ks[9], (DT,), jnp.float32) * (jnp.log(0.1) - jnp.log(0.001)), 'A_re': -0.5 * jnp.ones((DT, N_STATE), jnp.float32), 'A_im': jnp.tile(jnp.pi * jnp.arange(N_STATE, dtype=jnp.float32), (DT, 1)), 'C_re': jax.random.normal(ks[10], (DT, N_STATE), jnp.float32) * 0.5 ** 0.5, 'C_im': jax.random.normal(ks[11], (DT, N_STATE), jnp.float32) * 0.5 ** 0.5, 'D_skip': jax.random.normal(ks[12], (DT,), jnp.float32), 'mod_gate': jnp.array(0.5, jnp.float32)}
        return inp
    _L3_xattn_all = _L3_xattn_setup()
    _L3_xattn_in = {k: v for k, v in _L3_xattn_all.items() if k in ('Wq', 'Wk', 'Wv', 'W_film_in', 'b_film_in', 'W_film_out', 'b_film_out', 'g_norm_in', 'b_norm_in', 'g_norm_out', 'b_norm_out', 'g_ffn', 'b_ffn', 'W1', 'b1', 'W2', 'b2', 'log_dt', 'A_re', 'A_im', 'C_re', 'C_im', 'D_skip', 'mod_gate')}
    del _L3_xattn_all

    def _L3_ffn_setup():
        import math
        import jax, jax.numpy as jnp
        import numpy as np
        E = 8
        H = 256
        HP = 128
        SPARSITY = 8
        N_ROTATE = 64
        ROPE_BASE = 10000.0

        def _rope(x, pos):
            half = N_ROTATE // 2
            inv_freq = 1.0 / ROPE_BASE ** (jnp.arange(half, dtype=jnp.float32) * 2.0 / N_ROTATE)
            ang = pos.astype(jnp.float32)[..., None] * inv_freq
            sin, cos = (jnp.sin(ang), jnp.cos(ang))
            x1, x2 = (x[..., :half], x[..., half:])
            return jnp.concatenate([x1 * cos - x2 * sin, x2 * cos + x1 * sin], axis=-1)
        key = jax.random.key(seed)
        k1, k2, k3, k4 = jax.random.split(key, 4)
        B, T = (4, 2048)
        X = jax.random.normal(k1, (B, T, H), dtype=jnp.float32)
        Wr = jax.random.uniform(k2, (E, H), minval=-1 / math.sqrt(H), maxval=1 / math.sqrt(H), dtype=jnp.float32)
        bq = 1 / math.sqrt(3 * HP)
        Wqkv = jax.random.uniform(k3, (E, H, 3 * HP), minval=-bq, maxval=bq, dtype=jnp.float32)
        bo = 1 / math.sqrt(H * E)
        Wo = jax.random.uniform(k4, (E, HP, H), minval=-bo, maxval=bo, dtype=jnp.float32)
        return {'X': X, 'Wr': Wr, 'Wqkv': Wqkv, 'Wo': Wo}
    _L3_ffn_all = _L3_ffn_setup()
    _L3_ffn_in = {k: v for k, v in _L3_ffn_all.items() if k in ('Wr', 'Wqkv', 'Wo')}
    del _L3_ffn_all
    return {'x': x, 'ctx_768': ctx_768, 'mask_BxS_bf1': mask_BxS_bf1, 'mask_BxS2_bf1': mask_BxS2_bf1, 'L0_xattn_Wq': _L0_xattn_in['Wq'], 'L0_xattn_Wk': _L0_xattn_in['Wk'], 'L0_xattn_Wv': _L0_xattn_in['Wv'], 'L0_xattn_Wo': _L0_xattn_in['Wo'], 'L0_xattn_bo': _L0_xattn_in['bo'], 'L0_ffn_weight': _L0_ffn_in['weight'], 'L0_ffn_bias': _L0_ffn_in['bias'], 'L1_xattn_w_q': _L1_xattn_in['w_q'], 'L1_xattn_b_q': _L1_xattn_in['b_q'], 'L1_xattn_w_k': _L1_xattn_in['w_k'], 'L1_xattn_b_k': _L1_xattn_in['b_k'], 'L1_xattn_w_v': _L1_xattn_in['w_v'], 'L1_xattn_b_v': _L1_xattn_in['b_v'], 'L1_xattn_w_o': _L1_xattn_in['w_o'], 'L1_xattn_b_o': _L1_xattn_in['b_o'], 'L1_ffn_gate_w': _L1_ffn_in['gate_w'], 'L1_ffn_expert_w': _L1_ffn_in['expert_w'], 'L1_ffn_expert_b': _L1_ffn_in['expert_b'], 'L2_xattn_Wq': _L2_xattn_in['Wq'], 'L2_xattn_Wk': _L2_xattn_in['Wk'], 'L2_xattn_Wv': _L2_xattn_in['Wv'], 'L2_xattn_Wout': _L2_xattn_in['Wout'], 'L2_xattn_bout': _L2_xattn_in['bout'], 'L2_ffn_ternary_weight': _L2_ffn_in['ternary_weight'], 'L2_ffn_bias': _L2_ffn_in['bias'], 'L2_ffn_act_scale': _L2_ffn_in['act_scale'], 'L3_xattn_Wq': _L3_xattn_in['Wq'], 'L3_xattn_Wk': _L3_xattn_in['Wk'], 'L3_xattn_Wv': _L3_xattn_in['Wv'], 'L3_xattn_W_film_in': _L3_xattn_in['W_film_in'], 'L3_xattn_b_film_in': _L3_xattn_in['b_film_in'], 'L3_xattn_W_film_out': _L3_xattn_in['W_film_out'], 'L3_xattn_b_film_out': _L3_xattn_in['b_film_out'], 'L3_xattn_g_norm_in': _L3_xattn_in['g_norm_in'], 'L3_xattn_b_norm_in': _L3_xattn_in['b_norm_in'], 'L3_xattn_g_norm_out': _L3_xattn_in['g_norm_out'], 'L3_xattn_b_norm_out': _L3_xattn_in['b_norm_out'], 'L3_xattn_g_ffn': _L3_xattn_in['g_ffn'], 'L3_xattn_b_ffn': _L3_xattn_in['b_ffn'], 'L3_xattn_W1': _L3_xattn_in['W1'], 'L3_xattn_b1': _L3_xattn_in['b1'], 'L3_xattn_W2': _L3_xattn_in['W2'], 'L3_xattn_b2': _L3_xattn_in['b2'], 'L3_xattn_log_dt': _L3_xattn_in['log_dt'], 'L3_xattn_A_re': _L3_xattn_in['A_re'], 'L3_xattn_A_im': _L3_xattn_in['A_im'], 'L3_xattn_C_re': _L3_xattn_in['C_re'], 'L3_xattn_C_im': _L3_xattn_in['C_im'], 'L3_xattn_D_skip': _L3_xattn_in['D_skip'], 'L3_xattn_mod_gate': _L3_xattn_in['mod_gate'], 'L3_ffn_Wr': _L3_ffn_in['Wr'], 'L3_ffn_Wqkv': _L3_ffn_in['Wqkv'], 'L3_ffn_Wo': _L3_ffn_in['Wo']}

def reference(x, ctx_768, mask_BxS_bf1, mask_BxS2_bf1, L0_xattn_Wq, L0_xattn_Wk, L0_xattn_Wv, L0_xattn_Wo, L0_xattn_bo, L0_ffn_weight, L0_ffn_bias, L1_xattn_w_q, L1_xattn_b_q, L1_xattn_w_k, L1_xattn_b_k, L1_xattn_w_v, L1_xattn_b_v, L1_xattn_w_o, L1_xattn_b_o, L1_ffn_gate_w, L1_ffn_expert_w, L1_ffn_expert_b, L2_xattn_Wq, L2_xattn_Wk, L2_xattn_Wv, L2_xattn_Wout, L2_xattn_bout, L2_ffn_ternary_weight, L2_ffn_bias, L2_ffn_act_scale, L3_xattn_Wq, L3_xattn_Wk, L3_xattn_Wv, L3_xattn_W_film_in, L3_xattn_b_film_in, L3_xattn_W_film_out, L3_xattn_b_film_out, L3_xattn_g_norm_in, L3_xattn_b_norm_in, L3_xattn_g_norm_out, L3_xattn_b_norm_out, L3_xattn_g_ffn, L3_xattn_b_ffn, L3_xattn_W1, L3_xattn_b1, L3_xattn_W2, L3_xattn_b2, L3_xattn_log_dt, L3_xattn_A_re, L3_xattn_A_im, L3_xattn_C_re, L3_xattn_C_im, L3_xattn_D_skip, L3_xattn_mod_gate, L3_ffn_Wr, L3_ffn_Wqkv, L3_ffn_Wo):
    import jax
    import jax.numpy as jnp

    def _L0_xattn_ref(x, context, Wq, Wk, Wv, Wo, bo):
        import jax, jax.numpy as jnp
        import numpy as np
        HEADS = 8
        DIM_HEAD = 64
        QUERY_DIM = 256
        CONTEXT_DIM = 192
        INNER = HEADS * DIM_HEAD
        B, Sq, _ = x.shape
        h, d = (HEADS, DIM_HEAD)
        scale = d ** (-0.5)
        q = (x @ Wq).reshape(B, Sq, h, d).transpose(0, 2, 1, 3)
        k = (context @ Wk).reshape(B, -1, h, d).transpose(0, 2, 1, 3)
        v = (context @ Wv).reshape(B, -1, h, d).transpose(0, 2, 1, 3)
        scores = jnp.einsum('bhid,bhjd->bhij', q, k) * scale
        attn = jax.nn.softmax(scores, axis=-1)
        out = jnp.einsum('bhij,bhjd->bhid', attn, v)
        out = out.transpose(0, 2, 1, 3).reshape(B, Sq, h * d)
        return out @ Wo + bo

    def _L0_ffn_ref(x, weight, bias):
        import jax, jax.numpy as jnp
        import numpy as np
        QMAX = 127.0
        EPS = 1e-08

        def _quantize_per_token(x):
            amax = jnp.clip(jnp.max(jnp.abs(x), axis=-1, keepdims=True), EPS, None)
            scale = amax / QMAX
            x_q = jnp.clip(jnp.round(x / scale), -128, 127)
            return (x_q, scale)

        def _quantize_per_channel(w):
            amax = jnp.clip(jnp.max(jnp.abs(w), axis=-1, keepdims=True), EPS, None)
            scale = amax / QMAX
            w_q = jnp.clip(jnp.round(w / scale), -128, 127)
            return (w_q, scale)
        B, S, DIN = x.shape
        w_q, w_scale = _quantize_per_channel(weight.astype(jnp.float32))
        x_flat = x.reshape(-1, DIN).astype(jnp.float32)
        x_q, x_scale = _quantize_per_token(x_flat)
        out = jnp.matmul(x_q, w_q.T) * x_scale * w_scale.T
        out = out.reshape(B, S, -1) + bias
        return out.astype(x.dtype)

    def _L1_xattn_ref(x, context, w_q, b_q, w_k, b_k, w_v, b_v, w_o, b_o):
        import jax, jax.numpy as jnp
        import numpy as np
        N_HEADS = 16
        DIMS = 256
        D_CTX = 192
        HEAD = DIMS // N_HEADS
        B, Lq, D = x.shape
        q = x @ w_q + b_q
        k = context @ w_k + b_k
        v = context @ w_v + b_v
        q = q.reshape(B, Lq, N_HEADS, HEAD)
        k = k.reshape(B, -1, N_HEADS, HEAD)
        v = v.reshape(B, -1, N_HEADS, HEAD)
        scale = 1.0 / np.sqrt(HEAD).astype(np.float32)
        scores = jnp.einsum('bqhd,bkhd->bhqk', q, k) * scale
        weights = jax.nn.softmax(scores, axis=-1)
        out = jnp.einsum('bhqk,bkhd->bqhd', weights, v).reshape(B, Lq, D)
        return out @ w_o + b_o

    def _L1_ffn_ref(tokens, gate_w, expert_w, expert_b):
        import jax, jax.numpy as jnp
        import numpy as np
        B, S, H, E = (2, 512, 256, 16)
        b, s, h = tokens.shape
        logits = jnp.einsum('bsh,eh->bse', tokens, gate_w)
        weights = jax.nn.softmax(logits, axis=-1)
        top2_w, top2_idx = jax.lax.top_k(weights, 2)
        flat = tokens.reshape(b * s, h)
        flat_w = top2_w.reshape(b * s, 2)
        flat_idx = top2_idx.reshape(b * s, 2)
        y = jax.nn.relu(jnp.einsum('nh,edh->ned', flat, expert_w) + expert_b[None, :, :])
        sel = jnp.take_along_axis(y, flat_idx[:, :, None], axis=1)
        out = jnp.sum(sel * flat_w[:, :, None], axis=1)
        return out.reshape(b, s, h)

    def _L2_xattn_ref(x, context, Wq, Wk, Wv, Wout, bout):
        import jax, jax.numpy as jnp
        import numpy as np
        HEADS = 8
        DIM_HEAD = 128
        ATTN_MATRIX_SCALE = 1.5
        SCALE = DIM_HEAD ** (-0.5)

        def _split_heads(t):
            b, n, _ = t.shape
            t = t.reshape(b, n, HEADS, DIM_HEAD)
            return t.transpose(2, 0, 1, 3).reshape(HEADS, b * n, DIM_HEAD)
        b, n, _ = x.shape
        qh = _split_heads(jnp.einsum('bnq,qi->bni', x, Wq))
        kh = _split_heads(jnp.einsum('bmc,ci->bmi', context, Wk))
        vh = _split_heads(jnp.einsum('bmc,ci->bmi', context, Wv))
        sim = jnp.einsum('hid,hjd->hij', qh, kh) * SCALE
        mean = jnp.mean(sim, axis=-1, keepdims=True)
        sim = (sim - mean) * ATTN_MATRIX_SCALE + mean
        attn = jax.nn.softmax(sim, axis=-1)
        out = jnp.einsum('hij,hjd->hid', attn, vh)
        out = out.reshape(HEADS, b, n, DIM_HEAD).transpose(1, 2, 0, 3)
        out = out.reshape(b, n, HEADS * DIM_HEAD)
        return jnp.einsum('bni,iq->bnq', out, Wout) + bout

    def _L2_ffn_ref(x, ternary_weight, bias, act_scale):
        import jax, jax.numpy as jnp
        import numpy as np
        B, S, D_IN, D_OUT = (16, 1024, 256, 256)
        ACT_BITS = 8
        QB = float(2 ** (ACT_BITS - 1) - 1)
        scale = jnp.maximum(act_scale, 1e-05)
        x_int = jnp.clip(jnp.round(x / scale), -QB, QB)
        x_dq = jnp.nan_to_num(x_int * scale, nan=0.0, posinf=10000.0, neginf=-10000.0)
        w = ternary_weight.astype(jnp.float32) - 1.0
        return jnp.einsum('bsi,oi->bso', x_dq, w) + bias

    def _L3_xattn_ref(x_text, x_vision, text_mask, vision_mask, Wq, Wk, Wv, W_film_in, b_film_in, W_film_out, b_film_out, g_norm_in, b_norm_in, g_norm_out, b_norm_out, g_ffn, b_ffn, W1, b1, W2, b2, log_dt, A_re, A_im, C_re, C_im, D_skip, mod_gate):
        import jax, jax.numpy as jnp
        import numpy as np
        B, T, DT, G, DV = (16, 128, 256, 144, 192)
        H, DH = (4, 32)
        INNER = H * DH
        HID = 4 * DT
        N_STATE = 64
        K_TOP = 32

        def layernorm(x, g, b, eps=1e-05):
            m = x.mean(-1, keepdims=True)
            v = x.var(-1, keepdims=True)
            return (x - m) * jax.lax.rsqrt(v + eps) * g + b

        def s4d(x, log_dt, A_re, A_im, C_re, C_im, D_skip):
            Bb, L, D = x.shape
            dt = jnp.exp(log_dt)
            A = A_re + 1j * A_im
            C = C_re + 1j * C_im
            dtA = dt[:, None] * A
            dC = C * (jnp.exp(dtA) - 1.0) / A
            powers = jnp.exp(dtA[:, :, None] * jnp.arange(L))
            K = 2.0 * jnp.einsum('dn,dnl->dl', dC, powers).real
            n = 2 * L
            Kf = jnp.fft.rfft(K, n=n, axis=-1)
            xf = jnp.fft.rfft(x, n=n, axis=1)
            y = jnp.fft.irfft(xf * Kf.T[None], n=n, axis=1)[:, :L]
            return y + x * D_skip
        Bb, Tt, D = x_text.shape
        Gg = x_vision.shape[1]
        Q = (x_text @ Wq).reshape(Bb, Tt, H, DH)
        K = (x_vision @ Wk).reshape(Bb, Gg, H, DH)
        scores = jnp.einsum('bthd,bghd->bhtg', Q, K) / np.sqrt(DH).astype(np.float32)
        scores = jnp.where(vision_mask[:, None, None, :], scores, -jnp.inf)
        topv, topi = jax.lax.top_k(scores, K_TOP)
        probs = jax.nn.softmax(topv, axis=-1)
        bi = jnp.arange(Bb)[:, None, None, None]
        hi = jnp.arange(H)[None, :, None, None]
        ti = jnp.arange(Tt)[None, None, :, None]
        attn = jnp.zeros_like(scores).at[bi, hi, ti, topi].set(probs)
        attn_mean = attn.mean(axis=1)
        V = x_vision @ Wv
        c_t = jnp.einsum('btg,bgd->btd', attn_mean, V)
        c_t = c_t * text_mask[..., None]
        x = layernorm(x_text, g_norm_in, b_norm_in)
        scale_in, shift_in = jnp.split(c_t @ W_film_in + b_film_in, 2, axis=-1)
        x = x * (1.0 + mod_gate * scale_in) + mod_gate * shift_in
        y = s4d(x, log_dt, A_re, A_im, C_re, C_im, D_skip)
        scale_out, shift_out = jnp.split(c_t @ W_film_out + b_film_out, 2, axis=-1)
        y = y * (1.0 + mod_gate * scale_out) + mod_gate * shift_out
        xt = x_text + y
        h = layernorm(xt, g_ffn, b_ffn)
        h = jax.nn.gelu(h @ W1 + b1, approximate=False) @ W2 + b2
        xt = xt + h
        return layernorm(xt, g_norm_out, b_norm_out)

    def _L3_ffn_ref(X, Wr, Wqkv, Wo):
        import math
        import jax, jax.numpy as jnp
        import numpy as np
        E = 8
        H = 256
        HP = 128
        SPARSITY = 8
        N_ROTATE = 64
        ROPE_BASE = 10000.0

        def _rope(x, pos):
            half = N_ROTATE // 2
            inv_freq = 1.0 / ROPE_BASE ** (jnp.arange(half, dtype=jnp.float32) * 2.0 / N_ROTATE)
            ang = pos.astype(jnp.float32)[..., None] * inv_freq
            sin, cos = (jnp.sin(ang), jnp.cos(ang))
            x1, x2 = (x[..., :half], x[..., half:])
            return jnp.concatenate([x1 * cos - x2 * sin, x2 * cos + x1 * sin], axis=-1)
        B, T, _ = X.shape
        k = min(max(T // SPARSITY, 2), T)
        logits = jax.nn.sigmoid(jnp.einsum('bth,eh->bte', X, Wr))
        topk_vals, topk_I = jax.lax.top_k(logits.transpose(0, 2, 1), k)
        idx_flat = topk_I.reshape(B, E * k)
        Xg = jnp.take_along_axis(X, idx_flat[:, :, None], axis=1).reshape(B, E, k, H)
        QKV = jnp.einsum('beki,eij->bekj', Xg, Wqkv)
        Q, K, V = jnp.split(QKV, 3, axis=-1)
        Q = jnp.concatenate([_rope(Q[..., :N_ROTATE], topk_I), Q[..., N_ROTATE:]], axis=-1)
        K = jnp.concatenate([_rope(K[..., :N_ROTATE], topk_I), K[..., N_ROTATE:]], axis=-1)
        M = topk_I[..., :, None] >= topk_I[..., None, :]
        scores = jnp.einsum('bekd,bemd->bekm', Q, K) / math.sqrt(HP)
        scores = jnp.where(M, scores, -jnp.inf)
        A = jax.nn.softmax(scores, axis=-1)
        AV = jnp.einsum('bekm,bemd->bekd', A, V)
        AV = AV * topk_vals[..., None]
        Xpre = jnp.einsum('bekj,eji->beki', AV, Wo)
        out = jnp.zeros((B, T, H), dtype=X.dtype)
        out = out.at[jnp.arange(B)[:, None], idx_flat].add(Xpre.reshape(B, E * k, H))
        return out
    x = x + _L0_xattn_ref(_layernorm(x, axis=-1), ctx_768, L0_xattn_Wq, L0_xattn_Wk, L0_xattn_Wv, L0_xattn_Wo, L0_xattn_bo)
    x = x + _L0_ffn_ref(_layernorm(x, axis=-1), L0_ffn_weight, L0_ffn_bias)
    x = x + _L1_xattn_ref(_layernorm(x, axis=-1), ctx_768, L1_xattn_w_q, L1_xattn_b_q, L1_xattn_w_k, L1_xattn_b_k, L1_xattn_w_v, L1_xattn_b_v, L1_xattn_w_o, L1_xattn_b_o)
    x = x + _L1_ffn_ref(_layernorm(x, axis=-1), L1_ffn_gate_w, L1_ffn_expert_w, L1_ffn_expert_b)
    x = x + _L2_xattn_ref(_layernorm(x, axis=-1), ctx_768, L2_xattn_Wq, L2_xattn_Wk, L2_xattn_Wv, L2_xattn_Wout, L2_xattn_bout)
    x = x + _L2_ffn_ref(_layernorm(x, axis=-1), L2_ffn_ternary_weight, L2_ffn_bias, L2_ffn_act_scale)
    x = x + _L3_xattn_ref(_layernorm(x, axis=-1), ctx_768, mask_BxS_bf1, mask_BxS2_bf1, L3_xattn_Wq, L3_xattn_Wk, L3_xattn_Wv, L3_xattn_W_film_in, L3_xattn_b_film_in, L3_xattn_W_film_out, L3_xattn_b_film_out, L3_xattn_g_norm_in, L3_xattn_b_norm_in, L3_xattn_g_norm_out, L3_xattn_b_norm_out, L3_xattn_g_ffn, L3_xattn_b_ffn, L3_xattn_W1, L3_xattn_b1, L3_xattn_W2, L3_xattn_b2, L3_xattn_log_dt, L3_xattn_A_re, L3_xattn_A_im, L3_xattn_C_re, L3_xattn_C_im, L3_xattn_D_skip, L3_xattn_mod_gate)
    x = x + _L3_ffn_ref(_layernorm(x, axis=-1), L3_ffn_Wr, L3_ffn_Wqkv, L3_ffn_Wo)
    return x

_drawn_inputs = setup_inputs


def setup_inputs(seed=0):
    import zlib

    import numpy as np

    out = dict(_drawn_inputs(seed))
    spreads = {'L2_xattn_bout': (0.0, 0.1),
     'L3_xattn_b_film_in': (0.0, 0.8),
     'L3_xattn_b_film_out': (0.0, 0.8),
     'L3_xattn_g_norm_in': (1.0, 0.6),
     'L3_xattn_b_norm_in': (0.0, 0.8),
     'L3_xattn_g_norm_out': (1.0, 0.6),
     'L3_xattn_b_norm_out': (0.0, 0.8),
     'L3_xattn_g_ffn': (1.0, 0.6),
     'L3_xattn_b_ffn': (0.0, 0.8),
     'L3_xattn_b1': (0.0, 0.8),
     'L3_xattn_b2': (0.0, 0.8),
     'L3_xattn_A_re': (-0.5, 0.6)}
    factors = {'L0_xattn_bo': 4.354,
     'L1_xattn_b_q': 8.0,
     'L1_xattn_b_k': 8.0,
     'L1_xattn_b_v': 4.497,
     'L1_xattn_b_o': 4.39,
     'L1_ffn_expert_b': 8.0,
     'L3_xattn_Wq': 8.0,
     'L3_xattn_Wk': 8.0,
     'L3_xattn_Wv': 8.0,
     'L3_xattn_W_film_in': 8.0,
     'L3_xattn_W_film_out': 8.0,
     'L3_xattn_W1': 8.0,
     'L3_xattn_W2': 8.0,
     'L3_ffn_Wr': 8.0,
     'L3_ffn_Wqkv': 8.0,
     'L3_ffn_Wo': 8.0}
    for name, (base, spread) in spreads.items():
        noise = np.random.default_rng([zlib.crc32(name.encode()), seed]).standard_normal(out[name].shape)
        drawn = base * np.exp(spread * noise) if base else spread * noise
        out[name] = jnp.asarray(drawn.astype(out[name].dtype))
    for name, factor in factors.items():
        out[name] = (out[name] * factor).astype(out[name].dtype)
    return out
```

```python
from contextlib import ExitStack

import numpy as np

import concourse.bass as bass
from concourse import mybir

F32 = mybir.dt.float32
BF16 = mybir.dt.bfloat16
I32 = mybir.dt.int32
U32 = mybir.dt.uint32
U8 = mybir.dt.uint8
ALU = mybir.AluOpType
ACT = mybir.ActivationFunctionType
AX = mybir.AxisListType

P = 128
B, S, D = 16, 256, 256
NCTX, DC = 120, 192
LANES = S // P
TILES = B * LANES
DK = D // P
CP = DC // 2
LN_EPS = 1e-5
ROUND = 1.5 * 2.0 ** 23


class Counter:

    def __init__(self, sem):
        self.sem, self.base = sem, 0

    def count(self, n):
        return self.base + n + 1


class Chain:

    def __init__(self, eng, sem):
        self.eng, self.sem, self.n = eng, sem, 0

    def restart(self):
        if self.n:
            self.eng.sem_clear(self.sem)
        self.n = 0

    def restart_always(self):
        self.eng.sem_clear(self.sem)
        self.n = 0

    def link(self, instruction):
        self.n += 1
        instruction.then_inc(self.sem, 1)
        self.eng.wait_ge(self.sem, self.n)


def program(nc, io, out, stages):
    with ExitStack() as ctx:
        whole = Whole(nc, io, ctx)
        load_x(nc, whole)
        for stage in stages:
            with ExitStack() as stage_ctx:
                stage(nc, whole, stage_ctx)
        store_x(nc, whole, out)


class Whole:

    def __init__(self, nc, io, ctx):
        self.nc, self.io = nc, io
        self.x_res = ctx.enter_context(nc.sbuf_tensor("x_res", [P, TILES + 1, D], F32))
        self.ident = ctx.enter_context(nc.sbuf_tensor("ident", [P, P], F32))
        self.ident16 = ctx.enter_context(nc.sbuf_tensor("ident16", [P, P], BF16))
        self.ones = ctx.enter_context(nc.sbuf_tensor("ones", [P, P], F32))
        self.neg_half = ctx.enter_context(nc.sbuf_tensor("neg_half", [P, LANES], F32))
        self.eps = ctx.enter_context(nc.sbuf_tensor("eps", [P, LANES], F32))
        self.stats = ctx.enter_context(nc.sbuf_tensor("stats", [P, LANES, 6], F32))
        self.mean_var = ctx.enter_context(nc.sbuf_tensor("mean_var", [P, LANES, 2], F32))
        self.rstd = ctx.enter_context(nc.sbuf_tensor("rstd", [P, LANES], F32))
        self.psum = ctx.enter_context(nc.psum_tensor("psum", [P, 8, 512], F32))
        self.counters = {}
        self.ctx = ctx
        self.chains = {e: ctx.enter_context(nc.semaphore(f"{e}_chain")) for e in ("dve", "pool", "act")}

    def counter(self, name):
        if name not in self.counters:
            self.counters[name] = Counter(self.ctx.enter_context(self.nc.semaphore(name)))
        return self.counters[name]

    def lane(self, s):
        return self.psum[:, 4 * s:4 * s + 4, :]

    def advance(self, **events):
        for name, n in events.items():
            self.counters[name].base += n


LOOKED_BACK = ("x_updated", "kv_ready", "exped", "attn_ready", "gated_used", "prob_t_psum", "prob_t_ready",
               "prob_t_ready2", "film_out_ready", "xn_kept", "xn_t_psum", "gather_psum", "gather_kept", "rope_kept")


def load_x(nc, w):
    loaded = w.counter("inputs_loaded")
    for name in LOOKED_BACK:
        w.counter(name).base = 1
    with nc.Block() as block:
        @block.sync
        def _(sp):
            for name in LOOKED_BACK:
                sp.sem_inc(w.counter(name).sem, 1)
            x_tiles = w.io["x"].rearrange("b (l p) d -> p (b l) d", p=P)
            step = TILES // 4
            for c in range(4):
                sp.dma_start(w.x_res[:, c * step:(c + 1) * step, :],
                             x_tiles[:, c * step:(c + 1) * step, :]).then_inc(loaded.sem, 16)
            sp.dma_start(w.ident[:, :], w.io["ident"]).then_inc(loaded.sem, 16)
            sp.wait_ge(loaded.sem, 16 * 5)

        @block.vector
        def _(dve):
            dve.memset(w.ones[:, :], 1.0)
            dve.memset(w.x_res[:, TILES, :], 0.0)
            dve.memset(w.neg_half[:, :], -0.5)
            dve.memset(w.eps[:, :], LN_EPS)
            dve.wait_ge(loaded.sem, 16 * 5)
            dve.tensor_copy(w.ident16[:, :], w.ident[:, :])
    loaded.base += 16 * 5


def store_x(nc, w, out):
    stored = w.counter("output_stored")
    with nc.Block() as block:
        @block.sync
        def _(sp):
            out_tiles = out.rearrange("b (l p) d -> p (b l) d", p=P)
            step = TILES // 4
            for c in range(4):
                sp.dma_start(out_tiles[:, c * step:(c + 1) * step, :],
                             w.x_res[:, c * step:(c + 1) * step, :]).then_inc(stored.sem, 16)
            sp.wait_ge(stored.sem, 16 * 4)



def layernorm_stats(dve, w, chain, u, s):
    chain.link(dve.bn_stats(w.stats[:, s, :], w.x_res[:, u, :]))
    dve.bn_aggr(w.mean_var[:, s, :], w.stats[:, s, :]).then_inc(w.counter("stats_ready").sem, 1)


def layernorm_rstd(pool, w, chain, u, s):
    pool.wait_ge(w.counter("stats_ready").sem, w.counter("stats_ready").count(u))
    chain.link(pool.tensor_tensor(w.rstd[:, s:s + 1], w.mean_var[:, s, 1:2], w.eps[:, 0:1], ALU.add))
    pool.tensor_tensor(w.rstd[:, s:s + 1], w.rstd[:, s:s + 1], w.neg_half[:, 0:1],
                       ALU.pow).then_inc(w.counter("rstd_ready").sem, 1)


def layernorm_apply(dve, w, xn, u, s):
    dve.wait_ge(w.counter("rstd_ready").sem, w.counter("rstd_ready").count(u))
    return dve.tensor_scalar(xn, w.x_res[:, u, :], w.mean_var[:, s, 0:1], w.rstd[:, s:s + 1],
                             ALU.subtract, ALU.mult)


def transpose_tile(pe, w, xn, bank, ident):
    for k in range(DK):
        last = pe.transpose(bank[:, k * P:(k + 1) * P], xn[:, k * P:(k + 1) * P], ident)
    return last



def attention_stage(tag, heads, dim, q_w, k_w, v_w, o_w, o_b, q_b=None, k_b=None, v_b=None):
    pad = max(dim, 32)
    inner = heads * pad
    parts = inner // P
    per = P // pad
    scale = float(dim) ** -0.5

    def stage(nc, w, ctx):
        io = w.io

        def sb(name, shape, dt=F32):
            return ctx.enter_context(nc.sbuf_tensor(f"{tag}_{name}", shape, dt))

        wq = sb("wq", [P, DK, inner])
        wk = sb("wk", [CP, 2, inner])
        wv = sb("wv", [CP, 2, inner])
        wo = sb("wo", [P, parts, D])
        bo = sb("bo", [1, D])
        ctx_t = sb("ctx_t", [CP, 2, B, NCTX])
        ctx_b = sb("ctx_b", [CP, 2, NCTX])
        bq = sb("bq", [P, parts])
        bk = sb("bk", [P, parts])
        bv = sb("bv", [1, inner])
        k_t = sb("k_t", [P, parts, NCTX])
        v = sb("v", [NCTX, inner])
        xn = sb("xn", [P, LANES, D])
        xn_t = sb("xn_t", [P, LANES, DK, P])
        q_t = sb("q_t", [P, LANES, parts, P])
        top = sb("top", [P, LANES, per, parts])
        total = sb("total", [P, LANES, per, parts])
        prob = sb("prob", [P, LANES, per, parts, NCTX])
        prob_t = sb("prob_t", [NCTX, LANES, per, parts, P])
        attn_t = sb("attn_t", [P, LANES, parts, P])

        padded = pad != dim
        biased = q_b is not None
        cleared = w.counter("weights_cleared")
        loaded = w.counter("weights_loaded")
        loads = []
        if padded:
            for k in range(DK):
                loads.append((wq[:, k, :].rearrange("p (h e) -> p h e", e=pad)[:, :, 0:dim],
                              io[q_w][k * P:(k + 1) * P, :].rearrange("p (h e) -> p h e", e=dim)))
            for k in range(2):
                for dst, src in ((wk, io[k_w]), (wv, io[v_w])):
                    loads.append((dst[:, k, :].rearrange("p (h e) -> p h e", e=pad)[:, :, 0:dim],
                                  src[k * CP:(k + 1) * CP, :].rearrange("p (h e) -> p h e", e=dim)))
            for r in range(per):
                loads.append((wo[r * pad:r * pad + dim, :, :],
                              io[o_w].rearrange("(k r e) n -> r e k n", r=per, e=dim)[r]))
        else:
            loads.append((wq[:, :, :], io[q_w].rearrange("(k p) n -> p k n", p=P)))
            loads.append((wk[:, :, :], io[k_w].rearrange("(k p) n -> p k n", p=CP)))
            loads.append((wv[:, :, :], io[v_w].rearrange("(k p) n -> p k n", p=CP)))
            loads.append((wo[:, :, :], io[o_w].rearrange("(k p) n -> p k n", p=P)))
        if biased:
            for r in range(per):
                for dst, src in ((bq, io[q_b]), (bk, io[k_b])):
                    loads.append((dst[r * pad:r * pad + dim, :],
                                  src.rearrange("(k r e) -> r e k", r=per, e=dim)[r]))
            loads.append((bv[:, :].rearrange("p (h e) -> p h e", e=pad)[:, :, 0:dim],
                          io[v_b].rearrange("(a h e) -> a h e", a=1, e=dim)))
        loads.append((bo[:, :], io[o_b].rearrange("(a n) -> a n", a=1)))
        loads.append((ctx_t[:, :, :, :], io["ctx_t"].rearrange("(k p) b j -> p k b j", p=CP)))
        all_loaded = loaded.base + 16 * len(loads)

        sig = w.counter
        ctx_copied, kv_ready, kv_copied = sig("ctx_copied"), sig("kv_ready"), sig("kv_copied")
        xn_ready, xn_t_psum, xn_t_ready = sig("xn_ready"), sig("xn_t_psum"), sig("xn_t_ready")
        q_psum, q_ready = sig("q_psum"), sig("q_ready")
        scores_psum, shifted, exped = sig("scores_psum"), sig("shifted"), sig("exped")
        inverse_ready, normalised = sig("inverse_ready"), sig("normalised")
        prob_t_psum, prob_t_ready = sig("prob_t_psum"), sig("prob_t_ready")
        attn_psum, attn_ready = sig("attn_psum"), sig("attn_ready")
        out_psum, x_updated = sig("out_psum"), sig("x_updated")

        def blocks_of(bank_view):
            return bank_view[:, 0:per, 0:parts * NCTX].rearrange("p r (k j) -> p r k j", j=NCTX)

        with nc.allow_non_contiguous_dma(reason="padded weights"), nc.Block() as block:
            @block.sync
            def _(sp):
                if padded:
                    sp.wait_ge(cleared.sem, cleared.count(0))
                for dst, src in loads:
                    sp.dma_start(dst, src).then_inc(loaded.sem, 16)
                sp.wait_ge(loaded.sem, all_loaded)

            @block.gpsimd
            def _(pool):
                chain = Chain(pool, w.chains["pool"])
                if padded:
                    for t in (wq, wk, wv, wo):
                        pool.memset(t[:, :, :], 0.0)
                    for t in (bq, bk):
                        pool.memset(t[:, :], 0.0)
                    pool.memset(bv[:, :], 0.0).then_inc(cleared.sem, 1)
                pool.wait_ge(loaded.sem, all_loaded)
                with pool.Fori(0, B) as i:
                    pool.wait_ge(kv_ready.sem, kv_ready.count(i - 1))
                    pool.tensor_copy(ctx_b[:, :, :], ctx_t[:, :, i, :]).then_inc(ctx_copied.sem, 1)
                    for s in range(LANES):
                        layernorm_rstd(pool, w, chain, i * LANES + s, s)
                    chain.restart()
                    for s in range(LANES):
                        u = i * LANES + s
                        pool.wait_ge(inverse_ready.sem, inverse_ready.count(u))
                        pool.tensor_tensor(
                            prob[:, s, :, :, :], prob[:, s, :, :, :],
                            total[:, s, :, :].unsqueeze(3).to_broadcast([P, per, parts, NCTX]),
                            ALU.mult).then_inc(normalised.sem, 1)

            @block.vector
            def _(dve):
                chain = Chain(dve, w.chains["dve"])
                dve.wait_ge(loaded.sem, all_loaded)
                with dve.Fori(0, B) as i:
                    for s in range(LANES):
                        layernorm_stats(dve, w, chain, i * LANES + s, s)
                    for s in range(LANES):
                        u = i * LANES + s
                        layernorm_apply(dve, w, xn[:, s, :], u, s).then_inc(xn_ready.sem, 1)
                    dve.wait_ge(kv_ready.sem, kv_ready.count(i))
                    dve.tensor_copy(v[:, :], w.lane(1)[0:NCTX, 3, 0:inner]).then_inc(kv_copied.sem, 1)
                    for s in range(LANES):
                        u = i * LANES + s
                        dve.wait_ge(q_psum.sem, q_psum.count(u))
                        src = w.lane(s)[:, 1, 0:parts * P].rearrange("p (k t) -> p k t", t=P)
                        if biased:
                            dve.tensor_tensor(q_t[:, s, :, :], src,
                                              bq[:, :].unsqueeze(2).to_broadcast([P, parts, P]),
                                              ALU.add).then_inc(q_ready.sem, 1)
                        else:
                            dve.tensor_copy(q_t[:, s, :, :], src).then_inc(q_ready.sem, 1)
                    for s in range(LANES):
                        u = i * LANES + s
                        dve.wait_ge(scores_psum.sem, scores_psum.count(u))
                        scores = blocks_of(w.lane(s))
                        chain.link(dve.tensor_reduce(top[:, s, :, :], scores, AX.X, ALU.max))
                        dve.tensor_tensor(
                            prob[:, s, :, :, :], scores,
                            top[:, s, :, :].unsqueeze(3).to_broadcast([P, per, parts, NCTX]),
                            ALU.subtract).then_inc(shifted.sem, 1)
                    for s in range(LANES):
                        u = i * LANES + s
                        dve.wait_ge(exped.sem, exped.count(u))
                        chain.link(dve.tensor_reduce(total[:, s, :, :], prob[:, s, :, :, :], AX.X, ALU.add))
                        dve.reciprocal(total[:, s, :, :], total[:, s, :, :]).then_inc(inverse_ready.sem, 1)
                    for s in range(LANES):
                        u = i * LANES + s
                        dve.wait_ge(prob_t_psum.sem, prob_t_psum.count(u))
                        dve.tensor_copy(prob_t[:, s, :, :, :],
                                        w.lane(s)[0:NCTX, 0:per, 0:parts * P]
                                        .rearrange("p r (k t) -> p r k t", t=P)).then_inc(prob_t_ready.sem, 1)
                    for s in range(LANES):
                        u = i * LANES + s
                        dve.wait_ge(out_psum.sem, out_psum.count(u))
                        dve.tensor_tensor(w.x_res[:, u, :], w.lane(s)[:, 1, 0:D], w.x_res[:, u, :],
                                          ALU.add).then_inc(x_updated.sem, 1)
                    chain.restart()

            @block.scalar
            def _(act):
                act.wait_ge(loaded.sem, all_loaded)
                with act.Fori(0, B) as i:
                    act.wait_ge(kv_ready.sem, kv_ready.count(i))
                    k_psum = w.lane(0)[:, 3, 0:parts * NCTX].rearrange("p (k j) -> p k j", j=NCTX)
                    for k in range(parts):
                        last = act.activation(k_t[:, k, :], k_psum[:, k, :], ACT.Identity,
                                              bias=bk[:, k:k + 1] if biased else 0.0)
                    last.then_inc(kv_copied.sem, 1)
                    for s in range(LANES):
                        u = i * LANES + s
                        act.wait_ge(xn_t_psum.sem, xn_t_psum.count(u))
                        act.activation(xn_t[:, s, :, :],
                                       w.lane(s)[:, 0, 0:D].rearrange("p (k t) -> p k t", t=P),
                                       ACT.Copy).then_inc(xn_t_ready.sem, 1)
                    for s in range(LANES):
                        u = i * LANES + s
                        act.wait_ge(shifted.sem, shifted.count(u))
                        act.activation(prob[:, s, :, :, :], prob[:, s, :, :, :], ACT.Exp,
                                       scale=scale).then_inc(exped.sem, 1)
                    for s in range(LANES):
                        u = i * LANES + s
                        act.wait_ge(attn_psum.sem, attn_psum.count(u))
                        act.activation(attn_t[:, s, :, :],
                                       w.lane(s)[:, 0, 0:parts * P].rearrange("p (k t) -> p k t", t=P),
                                       ACT.Copy).then_inc(attn_ready.sem, 1)

            @block.tensor
            def _(pe):
                pe.wait_ge(loaded.sem, all_loaded)
                with pe.Fori(0, B) as i:
                    pe.wait_ge(ctx_copied.sem, ctx_copied.count(i))
                    pe.wait_ge(x_updated.sem, x_updated.count(i * LANES - 1))
                    for m in range(parts):
                        for k in range(2):
                            pe.matmul(w.lane(0)[:, 3, m * NCTX:(m + 1) * NCTX], wk[:, k, m * P:(m + 1) * P],
                                      ctx_b[:, k, :], start=(k == 0), stop=(k == 1))
                    for k in range(2):
                        last = pe.matmul(w.lane(1)[0:NCTX, 3, 0:inner], ctx_b[:, k, :], wv[:, k, :],
                                         start=(k == 0), stop=(k == 1 and not biased))
                    if biased:
                        last = pe.matmul(w.lane(1)[0:NCTX, 3, 0:inner], w.ones[0:1, 0:NCTX], bv[:, :],
                                         start=False, stop=True)
                    last.then_inc(kv_ready.sem, 1)
                    for s in range(LANES):
                        pe.wait_ge(xn_ready.sem, xn_ready.count(i * LANES + s))
                        transpose_tile(pe, w, xn[:, s, :], w.lane(s)[:, 0, :],
                                       w.ident[:, :]).then_inc(xn_t_psum.sem, 1)
                    for s in range(LANES):
                        pe.wait_ge(xn_t_ready.sem, xn_t_ready.count(i * LANES + s))
                        for m in range(parts):
                            for k in range(DK):
                                last = pe.matmul(w.lane(s)[:, 1, m * P:(m + 1) * P],
                                                 wq[:, k, m * P:(m + 1) * P], xn_t[:, s, k, :],
                                                 start=(k == 0), stop=(k == DK - 1))
                        last.then_inc(q_psum.sem, 1)
                    pe.wait_ge(kv_copied.sem, kv_copied.base + 2 * i + 2)
                    for s in range(LANES):
                        pe.wait_ge(q_ready.sem, q_ready.count(i * LANES + s))
                        for r in range(per):
                            for k in range(parts):
                                rows = slice(r * pad, (r + 1) * pad)
                                last = pe.matmul(w.lane(s)[:, r, k * NCTX:(k + 1) * NCTX],
                                                 q_t[rows, s, k, :], k_t[rows, k, :], start=True, stop=True)
                        last.then_inc(scores_psum.sem, 1)
                    for s in range(LANES):
                        pe.wait_ge(normalised.sem, normalised.count(i * LANES + s))
                        for r in range(per):
                            for k in range(parts):
                                last = pe.transpose(w.lane(s)[0:NCTX, r, k * P:(k + 1) * P],
                                                    prob[:, s, r, k, :], w.ident[:, :])
                        last.then_inc(prob_t_psum.sem, 1)
                    for s in range(LANES):
                        pe.wait_ge(prob_t_ready.sem, prob_t_ready.count(i * LANES + s))
                        for k in range(parts):
                            for r in range(per):
                                h = k * per + r
                                last = pe.matmul(w.lane(s)[r * pad:(r + 1) * pad, 0, k * P:(k + 1) * P],
                                                 v[:, h * pad:(h + 1) * pad], prob_t[:, s, r, k, :],
                                                 start=True, stop=True)
                        last.then_inc(attn_psum.sem, 1)
                    for s in range(LANES):
                        pe.wait_ge(attn_ready.sem, attn_ready.count(i * LANES + s))
                        for k in range(parts):
                            pe.matmul(w.lane(s)[:, 1, 0:D], attn_t[:, s, k, :], wo[:, k, :],
                                      start=(k == 0), stop=False)
                        pe.matmul(w.lane(s)[:, 1, 0:D], w.ones[0:1, :], bo[:, :], start=False,
                                  stop=True).then_inc(out_psum.sem, 1)

        loaded.base = all_loaded
        if padded:
            cleared.base += 1
        w.advance(ctx_copied=B, kv_ready=B, kv_copied=2 * B)
        w.advance(**{name: TILES for name in (
            "stats_ready", "rstd_ready", "xn_ready", "xn_t_psum", "xn_t_ready", "q_psum", "q_ready",
            "scores_psum", "shifted", "exped", "inverse_ready", "normalised", "prob_t_psum",
            "prob_t_ready", "attn_psum", "attn_ready", "out_psum", "x_updated")})
    return stage



def quantised_stage(tag, prepare):
    per_token = tag == "int8"

    def stage(nc, w, ctx):
        io = w.io

        def sb(name, shape, dt=F32):
            return ctx.enter_context(nc.sbuf_tensor(f"{tag}_{name}", shape, dt))

        w_t = sb("w_t", [P, DK, D], BF16)
        w_scale = sb("w_scale", [P, D])
        bias = sb("bias", [P, D])
        prepare(nc, w, sb, w_t, w_scale, bias)
        xn = sb("xn", [P, LANES, D])
        x_scale = sb("x_scale", [P, LANES])
        x_inv = sb("x_inv", [P, LANES])
        x_q = sb("x_q", [P, LANES, D], BF16)
        x_qt = sb("x_qt", [P, LANES, DK, P], BF16)
        x_bias = sb("x_bias", [P, LANES, D])
        scaled = sb("scaled", [P, LANES, D])

        sig = w.counter
        xn_ready, xn_t_psum, xn_t_ready = sig("xn_ready"), sig("xn_t_psum"), sig("xn_t_ready")
        out_psum, x_updated, x_biased = sig("out_psum"), sig("x_updated"), sig("x_biased")

        with nc.Block() as block:
            @block.gpsimd
            def _(pool):
                chain = Chain(pool, w.chains["pool"])
                with pool.Fori(0, B) as i:
                    for s in range(LANES):
                        layernorm_rstd(pool, w, chain, i * LANES + s, s)
                    chain.restart()
                    for s in range(LANES):
                        u = i * LANES + s
                        pool.wait_ge(x_updated.sem, x_updated.count(i * LANES - 1))
                        pool.tensor_tensor(x_bias[:, s, :], w.x_res[:, u, :], bias[:, :],
                                           ALU.add).then_inc(x_biased.sem, 1)

            @block.vector
            def _(dve):
                chain = Chain(dve, w.chains["dve"])
                with dve.Fori(0, B) as i:
                    for s in range(LANES):
                        layernorm_stats(dve, w, chain, i * LANES + s, s)
                    for s in range(LANES):
                        u = i * LANES + s
                        chain.link(layernorm_apply(dve, w, xn[:, s, :], u, s))
                        if per_token:
                            chain.link(dve.tensor_reduce(x_scale[:, s:s + 1], xn[:, s, :], AX.X, ALU.max,
                                                         apply_absolute_value=True))
                            chain.link(dve.tensor_scalar(x_scale[:, s:s + 1], x_scale[:, s:s + 1], 1e-8,
                                                         1.0 / 127.0, ALU.max, ALU.mult))
                            chain.link(dve.reciprocal(x_inv[:, s:s + 1], x_scale[:, s:s + 1]))
                            inverse = x_inv[:, s:s + 1]
                        else:
                            inverse = w_scale[:, 1:2]
                        chain.link(dve.tensor_scalar(xn[:, s, :], xn[:, s, :], inverse, ROUND,
                                                     ALU.mult, ALU.add))
                        low = -128.0 if per_token else -127.0
                        chain.link(dve.tensor_scalar(xn[:, s, :], xn[:, s, :], ROUND, low,
                                                     ALU.subtract, ALU.max))
                        dve.tensor_scalar(x_q[:, s, :], xn[:, s, :], 127.0, None,
                                          ALU.min).then_inc(xn_ready.sem, 1)
                    for s in range(LANES):
                        u = i * LANES + s
                        dve.wait_ge(out_psum.sem, out_psum.count(u))
                        y = w.lane(s)[:, 1, 0:D]
                        dve.wait_ge(x_biased.sem, x_biased.count(u))
                        if per_token:
                            chain.link(dve.scalar_tensor_tensor(scaled[:, s, :], y, x_scale[:, s:s + 1],
                                                                w_scale[:, :], ALU.mult, ALU.mult))
                            chain.link(dve.tensor_tensor(w.x_res[:, u, :], scaled[:, s, :],
                                                         x_bias[:, s, :], ALU.add))
                        else:
                            chain.link(dve.scalar_tensor_tensor(w.x_res[:, u, :], y, w_scale[:, 0:1],
                                                                x_bias[:, s, :], ALU.mult, ALU.add))
                        dve.engine_nop().then_inc(x_updated.sem, 1)
                    chain.restart()

            @block.scalar
            def _(act):
                with act.Fori(0, B) as i:
                    for s in range(LANES):
                        u = i * LANES + s
                        act.wait_ge(xn_t_psum.sem, xn_t_psum.count(u))
                        act.activation(x_qt[:, s, :, :],
                                       w.lane(s)[:, 0, 0:P].bitcast(BF16).rearrange("p (k t) -> p k t", t=P),
                                       ACT.Copy).then_inc(xn_t_ready.sem, 1)

            @block.tensor
            def _(pe):
                with pe.Fori(0, B) as i:
                    for s in range(LANES):
                        pe.wait_ge(xn_ready.sem, xn_ready.count(i * LANES + s))
                        transpose_tile(pe, w, x_q[:, s, :], w.lane(s)[:, 0, 0:P].bitcast(BF16),
                                       w.ident16[:, :]).then_inc(xn_t_psum.sem, 1)
                    for s in range(LANES):
                        u = i * LANES + s
                        pe.wait_ge(xn_t_ready.sem, xn_t_ready.count(u))
                        for k in range(DK):
                            last = pe.matmul(w.lane(s)[:, 1, 0:D], x_qt[:, s, k, :], w_t[:, k, :],
                                             start=(k == 0), stop=(k == DK - 1))
                        last.then_inc(out_psum.sem, 1)

        w.advance(**{name: TILES for name in (
            "stats_ready", "rstd_ready", "xn_ready", "xn_t_psum", "xn_t_ready", "out_psum",
            "x_updated", "x_biased")})
    return stage


def prepare_int8(nc, w, sb, w_t, w_scale, bias):
    weight = sb("weight", [P, DK, D])
    amax = sb("amax", [P, DK])
    inverse = sb("inverse", [P, DK])
    w_q = sb("w_q", [P, DK, D], BF16)
    diag = sb("diag", [P, DK, P])
    loaded, quantised, turned = w.counter("weights_loaded"), w.counter("w_quantised"), w.counter("w_turned")
    all_loaded = loaded.base + 32
    with nc.Block() as block:
        @block.sync
        def _(sp):
            sp.dma_start(weight[:, :, :], w.io["L0_ffn_weight"].rearrange("(m p) n -> p m n", p=P)
                         ).then_inc(loaded.sem, 16)
            sp.dma_start(bias[:, :], w.io["L0_ffn_bias"].partition_broadcast(P)).then_inc(loaded.sem, 16)
            sp.wait_ge(loaded.sem, all_loaded)

        @block.vector
        def _(dve):
            chain = Chain(dve, w.chains["dve"])
            dve.wait_ge(loaded.sem, all_loaded)
            chain.link(dve.tensor_reduce(amax[:, :], weight[:, :, :], AX.X, ALU.max,
                                         apply_absolute_value=True))
            chain.link(dve.tensor_scalar(amax[:, :], amax[:, :], 1e-8, 1.0 / 127.0, ALU.max, ALU.mult))
            chain.link(dve.reciprocal(inverse[:, :], amax[:, :]))
            for m in range(DK):
                chain.link(dve.tensor_scalar(weight[:, m, :], weight[:, m, :], inverse[:, m:m + 1], ROUND,
                                             ALU.mult, ALU.add))
                chain.link(dve.tensor_scalar(weight[:, m, :], weight[:, m, :], ROUND, -128.0,
                                             ALU.subtract, ALU.max))
                chain.link(dve.tensor_scalar(w_q[:, m, :], weight[:, m, :], 127.0, None, ALU.min))
                chain.link(dve.tensor_scalar(diag[:, m, :], w.ident[:, :], amax[:, m:m + 1], None, ALU.mult))
            dve.engine_nop().then_inc(quantised.sem, 1)
            dve.wait_ge(turned.sem, turned.count(0))
            dve.tensor_copy(w_t[:, :, :], w.psum[:, 0, 0:D].bitcast(BF16).rearrange("p (k m) -> p k m", k=DK))
            dve.tensor_copy(w_scale[:, :], w.psum[:, 1, 0:D])
            chain.link(dve.engine_nop())
            chain.restart()

        @block.tensor
        def _(pe):
            pe.wait_ge(quantised.sem, quantised.count(0))
            weights_t = w.psum[:, 0, 0:D].bitcast(BF16).rearrange("p (k m) -> p k m", k=DK)
            for m in range(DK):
                for k in range(DK):
                    pe.transpose(weights_t[:, k, m * P:(m + 1) * P], w_q[:, m, k * P:(k + 1) * P],
                                 w.ident16[:, :])
            for m in range(DK):
                last = pe.matmul(w.psum[:, 1, m * P:(m + 1) * P], w.ones[:, :], diag[:, m, :],
                                 start=True, stop=True)
            last.then_inc(turned.sem, 1)
    loaded.base = all_loaded
    w.advance(w_quantised=1, w_turned=1)


def prepare_ternary(nc, w, sb, w_t, w_scale, bias):
    weight = sb("weight", [P, DK, D], I32)
    loaded = w.counter("weights_loaded")
    all_loaded = loaded.base + 48
    with nc.Block() as block:
        @block.sync
        def _(sp):
            sp.dma_start(weight[:, :, :], w.io["ternary_t"].rearrange("(k p) n -> p k n", p=P)
                         ).then_inc(loaded.sem, 16)
            sp.dma_start(bias[:, :], w.io["L2_ffn_bias"].partition_broadcast(P)).then_inc(loaded.sem, 16)
            sp.dma_start(w_scale[:, 0:1], w.io["act_scale"].partition_broadcast(P)).then_inc(loaded.sem, 16)
            sp.wait_ge(loaded.sem, all_loaded)

        @block.vector
        def _(dve):
            chain = Chain(dve, w.chains["dve"])
            dve.wait_ge(loaded.sem, all_loaded)
            chain.link(dve.tensor_scalar(w_scale[:, 0:1], w_scale[:, 0:1], 1e-5, None, ALU.max))
            chain.link(dve.reciprocal(w_scale[:, 1:2], w_scale[:, 0:1]))
            chain.link(dve.tensor_scalar(w_t[:, :, :], weight[:, :, :], -1.0, None, ALU.add))
            chain.restart()
    loaded.base = all_loaded



EXPERTS = 16
PAIRS = EXPERTS // 2


def experts_stage(nc, w, ctx):
    io = w.io

    def sb(name, shape, dt=F32):
        return ctx.enter_context(nc.sbuf_tensor(f"moe_{name}", shape, dt))

    gate = sb("gate", [P, DK, EXPERTS])
    we = sb("we", [P, DK, EXPERTS, D])
    be = sb("be", [1, EXPERTS, D])
    iota = sb("iota", [P, EXPERTS])
    xn = sb("xn", [P, LANES, D])
    xn_t = sb("xn_t", [P, LANES, DK, P])
    top = sb("top", [P, LANES])
    e = sb("e", [P, LANES, EXPERTS])
    total = sb("total", [P, LANES])
    best = sb("best", [P, LANES, 8])
    best_at = sb("best_at", [P, LANES, 8], U32)
    at = sb("at", [P, LANES, 2])
    pick = sb("pick", [P, LANES, 2, EXPERTS])
    weight = sb("weight", [P, LANES, EXPERTS])
    RING = 3
    gated = sb("gated", [P, RING, 2, D])

    sig = w.counter
    loaded = sig("weights_loaded")
    n_loads = 5
    all_loaded = loaded.base + 16 * n_loads
    xn_ready, xn_t_psum, xn_t_ready = sig("xn_ready"), sig("xn_t_psum"), sig("xn_t_ready")
    gate_psum, shifted, exped = sig("scores_psum"), sig("shifted"), sig("exped")
    weights_ready = sig("inverse_ready")
    expert_psum, gated_ready, gated_used = sig("expert_psum"), sig("gated_ready"), sig("gated_used")

    with nc.Block() as block:
        @block.sync
        def _(sp):
            sp.dma_start(gate[:, :, :], io["gate_t"].rearrange("(k p) e -> p k e", p=P)).then_inc(loaded.sem, 16)
            for k in range(DK):
                sp.dma_start(we[:, k, :, :], io["expert_t"][k * P:(k + 1) * P, :, :]).then_inc(loaded.sem, 16)
            sp.dma_start(be[:, :, :], io["L1_ffn_expert_b"].rearrange("(a e) n -> a e n", a=1)
                         ).then_inc(loaded.sem, 16)
            sp.dma_start(iota[:, :], io["iota"][0:EXPERTS].partition_broadcast(P)).then_inc(loaded.sem, 16)
            sp.wait_ge(loaded.sem, all_loaded)

        @block.gpsimd
        def _(pool):
            chain = Chain(pool, w.chains["pool"])
            with pool.Fori(0, B) as i:
                for s in range(LANES):
                    layernorm_rstd(pool, w, chain, i * LANES + s, s)
                chain.restart()

        @block.vector
        def _(dve):
            chain = Chain(dve, w.chains["dve"])
            dve.wait_ge(loaded.sem, all_loaded)
            with dve.Fori(0, B) as i:
                for s in range(LANES):
                    layernorm_stats(dve, w, chain, i * LANES + s, s)
                for s in range(LANES):
                    u = i * LANES + s
                    layernorm_apply(dve, w, xn[:, s, :], u, s).then_inc(xn_ready.sem, 1)
                for s in range(LANES):
                    u = i * LANES + s
                    logits = w.lane(s)[:, 0, 0:EXPERTS]
                    dve.wait_ge(gate_psum.sem, gate_psum.count(u))
                    chain.link(dve.tensor_reduce(top[:, s:s + 1], logits, AX.X, ALU.max))
                    dve.tensor_scalar(e[:, s, :], logits, top[:, s:s + 1], None,
                                      ALU.subtract).then_inc(shifted.sem, 1)
                for s in range(LANES):
                    u = i * LANES + s
                    dve.wait_ge(exped.sem, exped.count(u))
                    chain.link(dve.tensor_reduce(total[:, s:s + 1], e[:, s, :], AX.X, ALU.add))
                    chain.link(dve.reciprocal(total[:, s:s + 1], total[:, s:s + 1]))
                    chain.link(dve.max(best[:, s, :], e[:, s, :]))
                    chain.link(dve.max_index(best_at[:, s, :], best[:, s, :], e[:, s, :]))
                    chain.link(dve.tensor_copy(at[:, s, :], best_at[:, s, 0:2]))
                    for n in range(2):
                        chain.link(dve.tensor_scalar(pick[:, s, n, :], iota[:, :], at[:, s, n:n + 1],
                                                     best[:, s, n:n + 1], ALU.is_equal, ALU.mult))
                    chain.link(dve.tensor_tensor(weight[:, s, :], pick[:, s, 0, :], pick[:, s, 1, :], ALU.add))
                    dve.tensor_scalar(weight[:, s, :], weight[:, s, :], total[:, s:s + 1], None,
                                      ALU.mult).then_inc(weights_ready.sem, 1)
                for s in range(LANES):
                    u = i * LANES + s
                    for p in range(PAIRS):
                        n = u * PAIRS + p
                        if p > 0:
                            dve.wait_ge(gated_used.sem, gated_used.count(n - 1))
                        dve.wait_ge(gated_ready.sem, gated_ready.count(n))
                        slot = (s * PAIRS + p) % RING
                        chain.link(dve.tensor_tensor(w.x_res[:, u, :], w.x_res[:, u, :],
                                                     gated[:, slot, 0, :], ALU.add))
                        ins = dve.tensor_tensor(w.x_res[:, u, :], w.x_res[:, u, :], gated[:, slot, 1, :],
                                                ALU.add)
                        ins.then_inc(gated_used.sem, 1)
                chain.restart()

        @block.scalar
        def _(act):
            with act.Fori(0, B) as i:
                for s in range(LANES):
                    u = i * LANES + s
                    act.wait_ge(xn_t_psum.sem, xn_t_psum.count(u))
                    act.activation(xn_t[:, s, :, :], w.lane(s)[:, 0, 0:D].rearrange("p (k t) -> p k t", t=P),
                                   ACT.Copy).then_inc(xn_t_ready.sem, 1)
                for s in range(LANES):
                    u = i * LANES + s
                    act.wait_ge(shifted.sem, shifted.count(u))
                    act.activation(e[:, s, :], e[:, s, :], ACT.Exp).then_inc(exped.sem, 1)
                for s in range(LANES):
                    u = i * LANES + s
                    act.wait_ge(weights_ready.sem, weights_ready.count(u))
                    for p in range(PAIRS):
                        n = u * PAIRS + p
                        local = s * PAIRS + p
                        act.wait_ge(expert_psum.sem, expert_psum.count(n))
                        back = RING if local >= RING else local % RING + 1
                        act.wait_ge(gated_used.sem, gated_used.count(n - back))
                        for h in range(2):
                            x = 2 * p + h
                            last = act.activation(gated[:, local % RING, h, :],
                                                  w.lane(s)[:, 1 + p % 3, h * D:(h + 1) * D], ACT.Relu,
                                                  scale=weight[:, s, x:x + 1])
                        last.then_inc(gated_ready.sem, 1)

        @block.tensor
        def _(pe):
            pe.wait_ge(loaded.sem, all_loaded)
            with pe.Fori(0, B) as i:
                for s in range(LANES):
                    pe.wait_ge(xn_ready.sem, xn_ready.count(i * LANES + s))
                    transpose_tile(pe, w, xn[:, s, :], w.lane(s)[:, 0, :],
                                   w.ident[:, :]).then_inc(xn_t_psum.sem, 1)
                for s in range(LANES):
                    pe.wait_ge(xn_t_ready.sem, xn_t_ready.count(i * LANES + s))
                    for k in range(DK):
                        last = pe.matmul(w.lane(s)[:, 0, 0:EXPERTS], xn_t[:, s, k, :], gate[:, k, :],
                                         start=(k == 0), stop=(k == DK - 1))
                    last.then_inc(gate_psum.sem, 1)
                for s in range(LANES):
                    u = i * LANES + s
                    for p in range(PAIRS):
                        n = u * PAIRS + p
                        bank = w.lane(s)[:, 1 + p % 3, :]
                        if p >= 3:
                            pe.wait_ge(gated_ready.sem, gated_ready.count(n - 3))
                        for k in range(DK):
                            pe.matmul(bank, xn_t[:, s, k, :], we[:, k, 2 * p:2 * p + 2, :],
                                      start=(k == 0), stop=False)
                        pe.matmul(bank, w.ones[0:1, :], be[:, 2 * p:2 * p + 2, :], start=False,
                                  stop=True).then_inc(expert_psum.sem, 1)

    loaded.base = all_loaded
    w.advance(**{name: TILES for name in (
        "stats_ready", "rstd_ready", "xn_ready", "xn_t_psum", "xn_t_ready", "scores_psum", "shifted",
        "exped", "inverse_ready")})
    w.advance(expert_psum=TILES * PAIRS, gated_ready=TILES * PAIRS, gated_used=TILES * PAIRS)



def global_attention_stage(nc, w, ctx):
    heads, dim = 8, 128
    inner = heads * dim
    scale = 1.5 * float(dim) ** -0.5
    chunk = 4 * NCTX
    chunks = B // 4
    TURN = 4
    NORM_AT, TURN_AT, QUERY_AT = 2, 3, 5
    io = w.io

    def sb(name, shape, dt=F32):
        return ctx.enter_context(nc.sbuf_tensor(f"global_{name}", shape, dt))

    KEYS = B * NCTX
    KT = KEYS // P
    k_t = sb("k_t", [P, heads, KEYS])
    v = sb("v", [P, KT, inner])
    sig = w.counter
    loaded, projected, copied = sig("weights_loaded"), sig("kv_ready"), sig("kv_copied")

    with ExitStack() as once, nc.Block() as block:
        wk = once.enter_context(nc.sbuf_tensor("global_wk", [CP, 2, inner], F32))
        wv = once.enter_context(nc.sbuf_tensor("global_wv", [CP, 2, inner], F32))
        ctx_t = once.enter_context(nc.sbuf_tensor("global_ctx_t", [CP, 2, KEYS], F32))
        all_loaded = loaded.base + 48
        groups = [("k", h, c) for h in range(heads) for c in range(chunks)]
        groups += [("v", t, c) for t in range(KT) for c in range(inner // 512)]

        @block.sync
        def _(sp):
            for dst, src in ((wk[:, :, :], io["L2_xattn_Wk"].rearrange("(k p) n -> p k n", p=CP)),
                             (ctx_t[:, :, :], io["ctx_t"].rearrange("(k p) b j -> p k (b j)", p=CP)),
                             (wv[:, :, :], io["L2_xattn_Wv"].rearrange("(k p) n -> p k n", p=CP))):
                sp.dma_start(dst, src).then_inc(loaded.sem, 16)

        @block.tensor
        def _(pe):
            pe.wait_ge(loaded.sem, all_loaded)
            for n, (what, a, c) in enumerate(groups):
                if n >= 8:
                    used = sig("kv_copied2") if n % 2 else copied
                    pe.wait_ge(used.sem, used.count((n - 8) // 2))
                for k in range(2):
                    if what == "k":
                        last = pe.matmul(w.psum[:, n % 8, 0:chunk], wk[:, k, a * dim:(a + 1) * dim],
                                         ctx_t[:, k, c * chunk:(c + 1) * chunk], start=(k == 0), stop=(k == 1))
                    else:
                        last = pe.matmul(w.psum[:, n % 8, :], ctx_t[:, k, a * P:(a + 1) * P],
                                         wv[:, k, c * 512:(c + 1) * 512], start=(k == 0), stop=(k == 1))
                last.then_inc(projected.sem, 1)

        def place(n):
            what, a, c = groups[n]
            if what == "k":
                return k_t[:, a, c * chunk:(c + 1) * chunk], w.psum[:, n % 8, 0:chunk]
            return v[:, a, c * 512:(c + 1) * 512], w.psum[:, n % 8, :]

        @block.vector
        def _(dve):
            for n in range(0, len(groups), 2):
                dve.wait_ge(projected.sem, projected.count(n))
                dve.tensor_copy(*place(n)).then_inc(copied.sem, 1)

        @block.scalar
        def _(act):
            for n in range(1, len(groups), 2):
                act.wait_ge(projected.sem, projected.count(n))
                act.activation(*place(n), ACT.Copy).then_inc(sig("kv_copied2").sem, 1)
    loaded.base = all_loaded
    w.advance(kv_ready=len(groups), kv_copied=(len(groups) + 1) // 2, kv_copied2=len(groups) // 2)

    wq = sb("wq", [P, DK, inner])
    wo = sb("wo", [P, heads, D])
    xn = sb("xn", [P, D])
    xn_t = sb("xn_t", [P, DK, P])
    q_t = sb("q_t", [P, heads, P])
    top = sb("top", [P, chunks])
    bias = sb("bias", [P, 2])
    part_sum = sb("part_sum", [P, heads, chunks])
    inverse = sb("inverse", [P, 2])
    prob = sb("prob", [P, 2, KEYS])
    prob_t = sb("prob_t", [P, 2, TURN, P])
    attn_t = sb("attn_t", [P, 2, P])
    all_loaded = loaded.base + 32

    turns = [list(range(t * TURN, min((t + 1) * TURN, KT))) for t in range(chunks)]

    xn_ready, xn_t_psum, xn_t_ready = sig("xn_ready"), sig("xn_t_psum"), sig("xn_t_ready")
    q_psum, q_ready = sig("q_psum"), sig("q_ready")
    scores_psum, bias_ready, exped = sig("scores_psum"), sig("shifted"), sig("exped")
    prob_t_psum, even_ready, odd_ready = sig("prob_t_psum"), sig("prob_t_ready"), sig("prob_t_ready2")
    attn_psum, attn_ready = sig("attn_psum"), sig("attn_ready")
    out_psum, x_updated = sig("out_psum"), sig("x_updated")


    with nc.Block() as block:
        @block.sync
        def _(sp):
            for dst, src in ((wq[:, :, :], io["L2_xattn_Wq"].rearrange("(k p) n -> p k n", p=P)),
                             (wo[:, :, :], io["L2_xattn_Wout"].rearrange("(h p) n -> p h n", p=P))):
                sp.dma_start(dst, src).then_inc(loaded.sem, 16)

        @block.gpsimd
        def _(pool):
            chain = Chain(pool, w.chains["pool"])
            with pool.Fori(0, TILES + 1) as u:
                chain.restart_always()
                layernorm_rstd(pool, w, chain, u, 0)
            chain.restart_always()

        @block.vector
        def _(dve):
            chain = Chain(dve, w.chains["dve"])
            dve.wait_ge(loaded.sem, all_loaded)

            def maximum(n, h):
                for c in range(chunks):
                    dve.wait_ge(scores_psum.sem, scores_psum.count(n * chunks + c))
                    ins = dve.tensor_reduce(top[:, c:c + 1], w.psum[:, c, 0:chunk], AX.X, ALU.max)
                chain.link(ins)
                chain.link(dve.tensor_reduce(bias[:, h % 2:h % 2 + 1], top[:, :], AX.X, ALU.max))
                dve.tensor_scalar(bias[:, h % 2:h % 2 + 1], bias[:, h % 2:h % 2 + 1], -scale, None,
                                  ALU.mult).then_inc(bias_ready.sem, 1)

            def turn(n, t):
                dve.wait_ge(prob_t_psum.sem, prob_t_psum.count(n * chunks + t))
                size = len(turns[t])
                dve.tensor_copy(prob_t[:, t % 2, 0:size, :],
                                w.psum[:, 4 + t % 2, 0:size * P].rearrange("p (k t) -> p k t", t=P)
                                ).then_inc((odd_ready if t % 2 else even_ready).sem, 1)

            def output(u, h):
                n = u * heads + h
                chain.link(dve.tensor_reduce(inverse[:, h % 2:h % 2 + 1], part_sum[:, h, :], AX.X, ALU.add))
                chain.link(dve.reciprocal(inverse[:, h % 2:h % 2 + 1], inverse[:, h % 2:h % 2 + 1]))
                if h > 0:
                    dve.wait_ge(x_updated.sem, x_updated.count(n - 1))
                dve.wait_ge(out_psum.sem, out_psum.count(n))
                dve.scalar_tensor_tensor(w.x_res[:, u, :], w.psum[:, 7, 0:D], inverse[:, h % 2:h % 2 + 1],
                                         w.x_res[:, u, :], ALU.mult, ALU.add).then_inc(x_updated.sem, 1)

            def queries(u, c):
                dve.wait_ge(q_psum.sem, q_psum.count(2 * u + c))
                dve.tensor_copy(q_t[:, 4 * c:4 * c + 4, :],
                                w.psum[:, 4, :].rearrange("p (k t) -> p k t", t=P)).then_inc(q_ready.sem, 1)

            def normalise(u):
                layernorm_stats(dve, w, chain, u, 0)
                layernorm_apply(dve, w, xn[:, :], u, 0).then_inc(xn_ready.sem, 1)

            chain.restart_always()
            normalise(0)
            queries(0, 0)
            queries(0, 1)
            maximum(0, 0)
            with dve.Fori(0, TILES) as u:
                for h in range(heads):
                    n = u * heads + h
                    if h == 0:
                        chain.restart_always()
                    turn(n, 0)
                    maximum(n + 1, h + 1)
                    if h == NORM_AT:
                        normalise(u + 1)
                    if h > 0:
                        output(u, h - 1)
                    turn(n, 2)
                    turn(n, 3)
                    if h == QUERY_AT:
                        queries(u + 1, 0)
                    if h == heads - 1:
                        queries(u + 1, 1)
                output(u, heads - 1)
            chain.restart_always()

        @block.scalar
        def _(act):
            act.wait_ge(loaded.sem, all_loaded)

            def exponential(n, h):
                act.wait_ge(bias_ready.sem, bias_ready.count(n))
                for c in range(chunks):
                    act.activation(prob[:, h % 2, c * chunk:(c + 1) * chunk], w.psum[:, c, 0:chunk], ACT.Exp,
                                   bias=bias[:, h % 2:h % 2 + 1], scale=scale,
                                   accum_out=part_sum[:, h % heads, c:c + 1]).then_inc(exped.sem, 1)

            def normalised(u):
                act.wait_ge(xn_t_psum.sem, xn_t_psum.count(u))
                act.activation(xn_t[:, :, :], w.psum[:, 4, 0:D].rearrange("p (k t) -> p k t", t=P),
                               ACT.Copy).then_inc(xn_t_ready.sem, 1)

            normalised(0)
            exponential(0, 0)
            with act.Fori(0, TILES) as u:
                for h in range(heads):
                    n = u * heads + h
                    act.wait_ge(prob_t_psum.sem, prob_t_psum.count(n * chunks + 1))
                    act.activation(prob_t[:, 1, :, :], w.psum[:, 5, :].rearrange("p (k t) -> p k t", t=P),
                                   ACT.Copy).then_inc(odd_ready.sem, 1)
                    exponential(n + 1, h + 1)
                    if h == TURN_AT:
                        normalised(u + 1)
                    act.wait_ge(attn_psum.sem, attn_psum.count(n))
                    act.activation(attn_t[:, h % 2, :], w.psum[:, 6, 0:P], ACT.Copy).then_inc(attn_ready.sem, 1)

        @block.tensor
        def _(pe):
            pe.wait_ge(loaded.sem, all_loaded)

            def scores(n, h, first=False):
                for c in range(chunks):
                    if not first:
                        pe.wait_ge(exped.sem, exped.count((n - 1) * chunks + c))
                    pe.matmul(w.psum[:, c, 0:chunk], q_t[:, h, :], k_t[:, h, c * chunk:(c + 1) * chunk],
                              start=True, stop=True).then_inc(scores_psum.sem, 1)

            def turn(n, h, t):
                if t == 0:
                    pe.wait_ge(exped.sem, exped.count(n * chunks + chunks - 1))
                ready = odd_ready if t % 2 else even_ready
                pe.wait_ge(ready.sem, ready.count(n * 2 + t // 2 - 1))
                for j, kt in enumerate(turns[t]):
                    last = pe.transpose(w.psum[:, 4 + t % 2, j * P:(j + 1) * P],
                                        prob[:, h % 2, kt * P:(kt + 1) * P], w.ident[:, :])
                last.then_inc(prob_t_psum.sem, 1)

            def weigh(n, h, t):
                if t == 0:
                    pe.wait_ge(attn_ready.sem, attn_ready.count(n - 1))
                ready = odd_ready if t % 2 else even_ready
                pe.wait_ge(ready.sem, ready.count(n * 2 + t // 2))
                for j, kt in enumerate(turns[t]):
                    last = pe.matmul(w.psum[:, 6, 0:P], v[:, kt, h * dim:(h + 1) * dim], prob_t[:, t % 2, j, :],
                                     start=(kt == 0), stop=(kt == KT - 1))
                if t == chunks - 1:
                    last.then_inc(attn_psum.sem, 1)

            def output(u, h):
                n = u * heads + h
                pe.wait_ge(attn_ready.sem, attn_ready.count(n))
                pe.wait_ge(x_updated.sem, x_updated.count(n - 1))
                pe.matmul(w.psum[:, 7, 0:D], attn_t[:, h % 2, :], wo[:, h, :], start=True,
                          stop=True).then_inc(out_psum.sem, 1)

            def normalised(u):
                pe.wait_ge(xn_ready.sem, xn_ready.count(u))
                transpose_tile(pe, w, xn[:, :], w.psum[:, 4, :], w.ident[:, :]).then_inc(xn_t_psum.sem, 1)

            def queries(u, c):
                pe.wait_ge(xn_t_ready.sem, xn_t_ready.count(u))
                if c == 1:
                    pe.wait_ge(q_ready.sem, q_ready.count(2 * u))
                for m in range(4):
                    h = 4 * c + m
                    for k in range(DK):
                        last = pe.matmul(w.psum[:, 4, m * P:(m + 1) * P], wq[:, k, h * dim:(h + 1) * dim],
                                         xn_t[:, k, :], start=(k == 0), stop=(k == DK - 1))
                last.then_inc(q_psum.sem, 1)

            normalised(0)
            queries(0, 0)
            queries(0, 1)
            pe.wait_ge(q_ready.sem, q_ready.count(1))
            scores(0, 0, first=True)
            with pe.Fori(0, TILES) as u:
                for h in range(heads):
                    n = u * heads + h
                    if h == TURN_AT + 1:
                        pe.wait_ge(xn_t_ready.sem, xn_t_ready.count(u + 1))
                    if h == QUERY_AT + 1:
                        pe.wait_ge(q_ready.sem, q_ready.count(2 * (u + 1)))
                    if h == 0:
                        pe.wait_ge(q_ready.sem, q_ready.count(2 * u + 1))
                    turn(n, h, 0)
                    turn(n, h, 1)
                    scores(n + 1, (h + 1) % heads)
                    weigh(n, h, 0)
                    if h > 0:
                        output(u, h - 1)
                    turn(n, h, 2)
                    weigh(n, h, 1)
                    turn(n, h, 3)
                    weigh(n, h, 2)
                    if h == TURN_AT:
                        normalised(u + 1)
                    if h == QUERY_AT:
                        queries(u + 1, 0)
                    if h == heads - 1:
                        queries(u + 1, 1)
                    weigh(n, h, 3)
                output(u, heads - 1)

    loaded.base = all_loaded
    n_heads = TILES * heads
    w.advance(**{name: TILES + 1 for name in ("stats_ready", "rstd_ready", "xn_ready", "xn_t_psum", "xn_t_ready")})
    w.advance(q_psum=2 * TILES + 2, q_ready=2 * TILES + 2, shifted=n_heads + 1)
    w.advance(scores_psum=(n_heads + 1) * chunks, exped=(n_heads + 1) * chunks)
    w.advance(**{name: n_heads for name in ("attn_psum", "attn_ready", "out_psum", "x_updated")})
    w.advance(prob_t_psum=n_heads * chunks, prob_t_ready=n_heads * 2, prob_t_ready2=n_heads * 2)

    bout = sb("bout", [P, D])
    with nc.Block() as block:
        @block.sync
        def _(sp):
            sp.dma_start(bout[:, :], io["L2_xattn_bout"].partition_broadcast(P)).then_inc(loaded.sem, 16)

        @block.vector
        def _(dve):
            dve.wait_ge(loaded.sem, loaded.base + 16)
            dve.tensor_tensor(w.x_res[:, 0:TILES, :], w.x_res[:, 0:TILES, :],
                              bout[:, :].unsqueeze(1).to_broadcast([P, TILES, D]), ALU.add)
    loaded.base += 16



N_STATE = 64
SEQ_A, SEQ_B = 16, 16
FREQ = 2 * S
GROUP = P // SEQ_A
TWO_PI = 6.283185


def spectral_kernel(nc, w, ctx):
    io = w.io

    def keep(name, shape):
        return ctx.enter_context(nc.sbuf_tensor(f"ssm_{name}", shape, F32))

    by_cos, by_sin, by_last = (keep(n, [P, DK, D]) for n in ("by_cos", "by_sin", "by_last"))
    sig = w.counter
    loaded, gathered = sig("weights_loaded"), sig("lags_gathered")
    made, turned, spectra = sig("states_made"), sig("states_tanh"), sig("spectra_psum")
    lag_psum, lag_copied = sig("lag_psum"), sig("lag_copied")
    dve_done, act_done = sig("ssm_dve"), sig("ssm_act")

    with ExitStack() as once, nc.Block() as block:
        def sb(name, shape):
            return once.enter_context(nc.sbuf_tensor(f"ssm_{name}", shape, F32))

        a_re, a_im, c_re, c_im, log_dt = (sb(n, [P, D]) for n in ("a_re", "a_im", "c_re", "c_im", "log_dt"))
        phase = sb("phase", [P, 4])
        steps = sb("steps", [P, 2, SEQ_A])
        transform = sb("transform", [SEQ_A, SEQ_B, 5 * P])
        r, turn, tan, cos, sin, half = (sb(n, [P, D]) for n in ("r", "turn", "tan", "cos", "sin", "half"))
        e_re, e_im, n_re, n_im, t1, t2 = (sb(n, [P, D]) for n in ("e_re", "e_im", "n_re", "n_im", "t1", "t2"))
        angle = sb("angle", [P, 3, D])
        whole = sb("whole", [P, 3, D])
        big = [sb(f"big{n}", [P, D, SEQ_A]) for n in range(5)]
        lags = sb("lags", [SEQ_A, GROUP, D // GROUP, SEQ_B])
        n_loads = 12
        all_loaded = loaded.base + 16 * n_loads

        @block.sync
        def _(sp):
            for dst, name in ((a_re, "a_re_t"), (a_im, "a_im_t"), (c_re, "c_re_t"), (c_im, "c_im_t")):
                for c in range(2):
                    sp.dma_start(dst[c * N_STATE:(c + 1) * N_STATE, :], io[name]).then_inc(loaded.sem, 16)
            sp.dma_start(log_dt[:, :], io["L3_xattn_log_dt"].partition_broadcast(P)).then_inc(loaded.sem, 16)
            sp.dma_start(phase[:, :], io["phase"]).then_inc(loaded.sem, 16)
            sp.dma_start(steps[:, :, :], io["steps"].partition_broadcast(P)).then_inc(loaded.sem, 16)
            sp.dma_start(transform[:, :, :], io["lag_transform"]).then_inc(loaded.sem, 16)
            sp.wait_ge(lag_copied.sem, lag_copied.count(0))
            blocks = big[0][:, :, :].rearrange("p (g e) b -> p g e b", e=GROUP)
            for e in range(GROUP):
                sp.dma_start(lags[:, e, :, :], blocks[e * SEQ_A:(e + 1) * SEQ_A, :, e, :]
                             ).then_inc(gathered.sem, 16)

        @block.scalar
        def _(act):
            chain = Chain(act, w.chains["act"])
            chain.restart()
            act.wait_ge(loaded.sem, all_loaded)
            act.activation(log_dt[:, :], log_dt[:, :], ACT.Exp).then_inc(act_done.sem, 1)
            act.wait_ge(dve_done.sem, dve_done.count(0))
            act.activation(tan[:, :], r[:, :], ACT.Tanh, scale=0.5).then_inc(act_done.sem, 1)
            act.activation(big[1][:, :, :], big[1][:, :, :], ACT.Exp)
            act.activation(big[2][:, :, :], big[2][:, :, :], ACT.Exp).then_inc(act_done.sem, 1)
            for n, t in enumerate((sin, cos, half)):
                ins = act.activation(t[:, :], angle[:, n, :], ACT.Sin, scale=TWO_PI)
            ins.then_inc(act_done.sem, 1)
            for n in range(3):
                act.wait_ge(dve_done.sem, dve_done.count(1 + n))
                t = (big[0], big[3], big[4])[n]
                act.activation(t[:, :, :], t[:, :, :], ACT.Sin, scale=TWO_PI).then_inc(act_done.sem, 1)

        @block.vector
        def _(dve):
            chain = Chain(dve, w.chains["dve"])
            chain.restart()
            dve.wait_ge(loaded.sem, all_loaded)
            dve.wait_ge(act_done.sem, act_done.count(0))
            link = chain.link

            def wide(t):
                return t.unsqueeze(2).to_broadcast([P, D, SEQ_A])

            def stepped(n):
                return steps[:, n, :].unsqueeze(1).to_broadcast([P, D, SEQ_A])

            def fraction(x, whole_part):
                link(dve.tensor_scalar(whole_part, x, ROUND, -ROUND, ALU.add, ALU.add))
                return dve.tensor_tensor(x, x, whole_part, ALU.subtract)

            link(dve.tensor_tensor(r[:, :], log_dt[:, :], a_re[:, :], ALU.mult))
            link(dve.tensor_tensor(turn[:, :], log_dt[:, :], a_im[:, :], ALU.mult))
            link(dve.tensor_scalar(turn[:, :], turn[:, :], 1.0 / (2.0 * np.pi), None, ALU.mult))
            for n in range(2):
                link(dve.tensor_tensor(big[1 + n][:, :, :], wide(r[:, :]), stepped(n), ALU.mult))
            link(dve.tensor_copy(angle[:, 0, :], turn[:, :]))
            link(dve.tensor_scalar(angle[:, 1, :], turn[:, :], 0.25, None, ALU.add))
            link(dve.tensor_scalar(angle[:, 2, :], turn[:, :], 0.5, None, ALU.mult))
            link(fraction(angle[:, :, :], whole[:, :, :]))
            dve.engine_nop().then_inc(dve_done.sem, 1)
            link(dve.tensor_copy(turn[:, :], angle[:, 0, :]))
            for n, (t, step) in enumerate(((big[0], 0), (big[3], 0), (big[4], 1))):
                link(dve.tensor_tensor(t[:, :, :], wide(turn[:, :]), stepped(step), ALU.mult))
                link(dve.tensor_scalar(t[:, :, :], t[:, :, :], phase[:, n:n + 1], None, ALU.add))
                scratch = (big[3], big[4], None)[n]
                if scratch is None:
                    break
                link(fraction(t[:, :, :], scratch[:, :, :]))
                dve.engine_nop().then_inc(dve_done.sem, 1)
            dve.wait_ge(act_done.sem, act_done.count(3))
            link(dve.tensor_scalar(t1[:, :], tan[:, :], -1.0, 1.0, ALU.mult, ALU.add))
            link(dve.reciprocal(t1[:, :], t1[:, :]))
            link(dve.scalar_tensor_tensor(t1[:, :], tan[:, :], 2.0, t1[:, :], ALU.mult, ALU.mult))
            link(dve.tensor_tensor(e_re[:, :], t1[:, :], cos[:, :], ALU.mult))
            link(dve.scalar_tensor_tensor(e_im[:, :], t1[:, :], 1.0, sin[:, :], ALU.add, ALU.mult))
            link(dve.scalar_tensor_tensor(t2[:, :], half[:, :], 2.0, half[:, :], ALU.mult, ALU.mult))
            link(dve.tensor_tensor(e_re[:, :], e_re[:, :], t2[:, :], ALU.subtract))

            def complex_product(re, im, x_re, x_im, y_re, y_im, sign):
                link(dve.tensor_tensor(t1[:, :], x_re[:, :], y_re[:, :], ALU.mult))
                link(dve.tensor_tensor(t2[:, :], x_im[:, :], y_im[:, :], ALU.mult))
                link(dve.scalar_tensor_tensor(re[:, :], t2[:, :], -sign, t1[:, :], ALU.mult, ALU.add))
                link(dve.tensor_tensor(t1[:, :], x_im[:, :], y_re[:, :], ALU.mult))
                link(dve.tensor_tensor(t2[:, :], x_re[:, :], y_im[:, :], ALU.mult))
                link(dve.scalar_tensor_tensor(im[:, :], t2[:, :], sign, t1[:, :], ALU.mult, ALU.add))

            complex_product(n_re, n_im, c_re, c_im, e_re, e_im, 1.0)
            complex_product(e_re, e_im, n_re, n_im, a_re, a_im, -1.0)
            link(dve.tensor_tensor(t1[:, :], a_re[:, :], a_re[:, :], ALU.mult))
            link(dve.tensor_tensor(t2[:, :], a_im[:, :], a_im[:, :], ALU.mult))
            link(dve.tensor_tensor(t1[:, :], t1[:, :], t2[:, :], ALU.add))
            link(dve.reciprocal(t1[:, :], t1[:, :]))
            link(dve.tensor_tensor(e_re[:, :], e_re[:, :], t1[:, :], ALU.mult))
            link(dve.tensor_tensor(e_im[:, :], e_im[:, :], t1[:, :], ALU.mult))
            dve.wait_ge(act_done.sem, act_done.count(5))
            link(dve.tensor_tensor(big[0][:, :, :], big[0][:, :, :], wide(e_re[:, :]), ALU.mult))
            link(dve.tensor_tensor(big[3][:, :, :], big[3][:, :, :], wide(e_im[:, :]), ALU.mult))
            link(dve.tensor_tensor(big[0][:, :, :], big[0][:, :, :], big[3][:, :, :], ALU.add))
            link(dve.tensor_tensor(big[1][:, :, :], big[1][:, :, :], big[0][:, :, :], ALU.mult))
            link(fraction(big[4][:, :, :], big[3][:, :, :]))
            dve.engine_nop().then_inc(dve_done.sem, 1)
            dve.wait_ge(act_done.sem, act_done.count(6))
            link(dve.tensor_tensor(big[2][:, :, :], big[2][:, :, :], big[4][:, :, :], ALU.mult))
            dve.engine_nop().then_inc(made.sem, 1)
            dve.wait_ge(lag_psum.sem, lag_psum.count(0))
            dve.tensor_copy(big[0][:, :, :].rearrange("p (g e) b -> p g (e b)", g=8),
                            w.psum[:, :, :]).then_inc(lag_copied.sem, 1)
            dve.wait_ge(spectra.sem, spectra.count(0))
            dve.tensor_copy(by_cos[:, :, :], w.psum[:, 0, :].rearrange("p (k d) -> p k d", d=D))
            dve.tensor_copy(by_sin[:, :, :], w.psum[:, 1, :].rearrange("p (k d) -> p k d", d=D))
            dve.tensor_copy(by_last[:, 0, :], w.psum[:, 2, 0:D])
            dve.tensor_copy(by_last[:, 1, :], w.psum[:, 0, D:2 * D])

        @block.tensor
        def _(pe):
            pe.wait_ge(made.sem, made.count(0))
            for g in range(D // GROUP):
                lanes = slice(g * GROUP, (g + 1) * GROUP)
                last = pe.matmul(w.psum[:, g // 4, (g % 4) * P:(g % 4 + 1) * P], big[1][:, lanes, :],
                                 big[2][:, lanes, :], start=True, stop=True)
            last.then_inc(lag_psum.sem, 1)
            pe.wait_ge(gathered.sem, gathered.base + 16 * GROUP)
            for t in range(5):
                for b in range(SEQ_B):
                    last = pe.matmul(w.psum[:, t // 2, (t % 2) * D:(t % 2 + 1) * D],
                                     transform[:, b, t * P:(t + 1) * P],
                                     lags[:, :, :, b].rearrange("a e g -> a g e"),
                                     start=(b == 0), stop=(b == SEQ_B - 1))
            last.then_inc(spectra.sem, 1)

    loaded.base = all_loaded
    gathered.base += 16 * GROUP
    w.advance(ssm_dve=4, ssm_act=7, states_made=1, lag_psum=1, lag_copied=1, spectra_psum=1)
    return by_cos, by_sin, by_last


def selective_stage(nc, w, ctx):
    heads, dim, top_k = 4, 32, 32
    hidden = 4 * D
    HT = hidden // P
    scale = float(dim) ** -0.5
    io = w.io
    by_cos, by_sin, by_last = spectral_kernel(nc, w, ctx)

    def sb(name, shape, dt=F32):
        return ctx.enter_context(nc.sbuf_tensor(f"sel_{name}", shape, dt))

    wq = sb("wq", [P, DK, heads * dim])
    wk = sb("wk", [CP, 2, heads * dim])
    wv = sb("wv", [CP, 2, D])
    film = [sb(f"film{n}", [P, DK, 2 * D]) for n in range(2)]
    film_b = [sb(f"film_b{n}", [1, 2 * D]) for n in range(2)]
    rows = {n: sb(n, [P, D]) for n in ("g_norm_in", "b_norm_in", "g_ffn", "b_ffn", "g_norm_out", "b_norm_out",
                                       "b2", "D_skip")}
    gate = sb("gate", [P, 1])
    w1 = sb("w1", [P, DK, hidden])
    b1 = sb("b1", [P, HT])
    w2 = sb("w2", [P, HT, D])
    forward = sb("forward", [P, LANES, 4 * P])
    backward = sb("backward", [P, 4, LANES, P])
    text_u8 = sb("text_u8", [P, TILES], U8)
    text = sb("text", [P, TILES])
    vision_u8 = sb("vision_u8", [P, B, NCTX], U8)
    vision = sb("vision", [P, B, NCTX])
    ctx_t = sb("ctx_t", [CP, 2, B, NCTX])
    ctx_b = sb("ctx_b", [CP, 2, NCTX])
    k_t = sb("k_t", [P, NCTX])
    v = sb("v", [NCTX, D])
    xl_t = sb("xl_t", [P, DK, LANES, P])
    q_t = sb("q_t", [P, LANES, P])
    score = sb("score", [P, heads, LANES, NCTX])
    rest = sb("rest", [P, heads, LANES, NCTX])
    top = sb("top", [P, heads, LANES])
    best = sb("best", [P, heads, LANES, 8])
    total = sb("total", [P, heads, LANES])
    mean = sb("mean", [P, LANES, NCTX])
    mean_t = sb("mean_t", [NCTX, LANES, P])
    c_t = sb("c_t", [P, DK, LANES, P])
    mods_in = sb("mods_in", [P, LANES, 2 * D])
    xl = [sb(f"xl{n}", [P, LANES, D]) for n in range(2)]
    u_in = [sb(f"u_in{n}", [P, LANES, D]) for n in range(2)]
    u_skip = [sb(f"u_skip{n}", [P, LANES, D]) for n in range(2)]
    mods_out = [sb(f"mods_out{n}", [P, LANES, 2 * D]) for n in range(2)]
    prod = [sb(f"prod{n}", [P, DK, D]) for n in range(4)]
    spectrum = sb("spectrum", [P, 2 * DK, D])
    y = sb("y", [P, LANES, D])
    xt = sb("xt", [P, LANES, D])
    h = sb("h", [P, LANES, D])
    h_t = sb("h_t", [P, DK, LANES, P])
    hid = sb("hid", [P, HT, LANES, P])
    norms = {half: (sb(f"stats_{half}", [P, LANES, 6]), sb(f"mean_var_{half}", [P, LANES, 2]),
                    sb(f"rstd_{half}", [P, LANES])) for half in "ab"}

    sig = w.counter
    loaded = sig("weights_loaded")
    loads = [(wq[:, :, :], io["L3_xattn_Wq"].rearrange("(k p) n -> p k n", p=P)),
             (wk[:, :, :], io["L3_xattn_Wk"].rearrange("(k p) n -> p k n", p=CP)),
             (wv[:, :, :], io["L3_xattn_Wv"].rearrange("(k p) n -> p k n", p=CP)),
             (ctx_t[:, :, :, :], io["ctx_t"].rearrange("(k p) b j -> p k b j", p=CP)),
             (text_u8[:, :], io["text_mask_t"]),
             (vision_u8[:, :, :], io["vision_mask"].partition_broadcast(P)),
             (gate[:, :], io["mod_gate"].partition_broadcast(P)),
             (w1[:, :, :], io["L3_xattn_W1"].rearrange("(k p) n -> p k n", p=P)),
             (b1[:, :], io["L3_xattn_b1"].rearrange("(k p) -> p k", p=P)),
             (w2[:, :, :], io["L3_xattn_W2"].rearrange("(k p) n -> p k n", p=P)),
             (forward[:, :, :], io["forward"].rearrange("(k p) n -> p k n", p=P)),
             (backward[:, :, :, :], io["backward"].rearrange("(k p) (l t) -> p k l t", p=P, t=P))]
    for n, end in enumerate(("in", "out")):
        loads.append((film[n][:, :, :], io[f"L3_xattn_W_film_{end}"].rearrange("(k p) n -> p k n", p=P)))
        loads.append((film_b[n][:, :], io[f"L3_xattn_b_film_{end}"].rearrange("(a n) -> a n", a=1)))
    for name, t in rows.items():
        loads.append((t[:, :], io[f"L3_xattn_{name}"].partition_broadcast(P)))
    all_loaded = loaded.base + 16 * len(loads)

    once = ("ctx_copied", "kv_ready", "kv_copied", "xl_ready", "xl_t_psum", "xl_t_ready", "q_psum", "q_ready",
            "u_normed", "u_affine", "scores_psum", "shifted", "exped", "mean_ready", "mean_t_psum",
            "mean_t_ready", "c_psum", "c_ready", "film_psum", "film_ready", "u_ready", "skip_ready",
            "freq_psum", "prods_ready", "spec_ready", "y_psum", "h_normed", "h_affine", "h_t_psum",
            "h_t_ready", "ffn_psum", "out_normed", "out_affine", "x_updated")
    c_ = {n: sig(n) for n in once}

    def before(eng, name, n):
        eng.wait_ge(c_[name].sem, c_[name].count(n))

    def norm_events(half, i, which):
        n = 2 * i + which
        return sig(f"stats_{half}"), sig(f"rstd_{half}"), n

    def interleave(a, b):
        def run(nxt, now):
            for step in range(5):
                if now is not None:
                    b(step, *now)
                if nxt is not None:
                    a(step, *nxt)

        return run

    def over_batches(eng, a, b):
        run = interleave(a, b)
        run((0, 0), None)
        with eng.Fori(0, B // 2 - 1) as t:
            run((2 * t + 1, 1), (2 * t, 0))
            run((2 * t + 2, 0), (2 * t + 1, 1))
        run((B - 1, 1), (B - 2, 0))
        run(None, (B - 1, 1))

    def scale_rows(pool, chain, half, i, which):
        stats, rstd, n = norm_events(half, i, which)
        _, mean_var, r = norms[half]
        pool.wait_ge(stats.sem, stats.count(n))
        chain.link(pool.tensor_tensor(r[:, :], mean_var[:, :, 1], w.eps[:, :], ALU.add))
        pool.tensor_tensor(r[:, :], r[:, :], w.neg_half[:, :], ALU.pow).then_inc(rstd.sem, 1)

    def affine(pool, chain, t, gain, shift):
        chain.link(pool.tensor_tensor(t[:, :, :], t[:, :, :],
                                      rows[gain][:, :].unsqueeze(1).to_broadcast([P, LANES, D]), ALU.mult))
        return pool.tensor_tensor(t[:, :, :], t[:, :, :],
                                  rows[shift][:, :].unsqueeze(1).to_broadcast([P, LANES, D]), ALU.add)

    with nc.allow_non_contiguous_dma(reason="biases by partition"), nc.Block() as block:
        @block.sync
        def _(sp):
            for dst, src in loads:
                sp.dma_start(dst, src).then_inc(loaded.sem, 16)

        @block.gpsimd
        def _(pool):
            chain = Chain(pool, w.chains["pool"])
            pool.wait_ge(loaded.sem, all_loaded)

            def a(step, i, par):
                if step == 0:
                    chain.restart_always()
                    before(pool, "kv_ready", i - 1)
                    pool.tensor_copy(ctx_b[:, :, :], ctx_t[:, :, i, :]).then_inc(c_["ctx_copied"].sem, 1)
                    scale_rows(pool, chain, "a", i, 0)
                if step == 1:
                    scale_rows(pool, chain, "a", i, 1)
                if step == 2:
                    before(pool, "u_normed", i)
                    affine(pool, chain, u_in[par], "g_norm_in", "b_norm_in").then_inc(c_["u_affine"].sem, 1)
                if step == 4:
                    before(pool, "u_ready", i)
                    pool.tensor_tensor(u_skip[par][:, :, :], u_in[par][:, :, :],
                                       rows["D_skip"][:, :].unsqueeze(1).to_broadcast([P, LANES, D]),
                                       ALU.mult).then_inc(c_["skip_ready"].sem, 1)

            def b(step, i, par):
                if step == 0:
                    before(pool, "prods_ready", i)
                    pool.tensor_tensor(spectrum[:, 0:DK, :], prod[0][:, :, :], prod[1][:, :, :], ALU.subtract)
                    pool.tensor_tensor(spectrum[:, DK:2 * DK, :], prod[2][:, :, :], prod[3][:, :, :],
                                       ALU.add).then_inc(c_["spec_ready"].sem, 1)
                if step == 1:
                    scale_rows(pool, chain, "b", i, 0)
                if step == 2:
                    before(pool, "h_normed", i)
                    affine(pool, chain, h, "g_ffn", "b_ffn").then_inc(c_["h_affine"].sem, 1)
                if step == 4:
                    scale_rows(pool, chain, "b", i, 1)
                    before(pool, "out_normed", i)
                    affine(pool, chain, y, "g_norm_out", "b_norm_out").then_inc(c_["out_affine"].sem, 1)

            over_batches(pool, a, b)

        @block.vector
        def _(dve):
            chain = Chain(dve, w.chains["dve"])
            dve.wait_ge(loaded.sem, all_loaded)
            dve.tensor_copy(text[:, :], text_u8[:, :])
            chain.restart_always()
            chain.link(dve.tensor_scalar(vision[:, :, :], vision_u8[:, :, :], -1.0, 3.0e38, ALU.add, ALU.mult))
            chain.link(dve.tensor_scalar(vision[:, :, :], vision[:, :, :], 3.0e38, None, ALU.mult))
            chain.link(dve.tensor_scalar(text[:, :], text[:, :], 1.0 / heads, None, ALU.mult))
            link = chain.link

            def stats(half, i, which, x):
                st, mean_var, _ = norms[half]
                for s in range(LANES):
                    ins = dve.bn_stats(st[:, s, :], x(s))
                link(ins)
                for s in range(LANES):
                    ins = dve.bn_aggr(mean_var[:, s, :], st[:, s, :])
                ins.then_inc(norm_events(half, i, which)[0].sem, 1)

            def normalise(half, i, which, x, to):
                _, mean_var, r = norms[half]
                _, rstd, n = norm_events(half, i, which)
                dve.wait_ge(rstd.sem, rstd.count(n))
                for s in range(LANES):
                    ins = dve.tensor_scalar(to[:, s, :], x(s), mean_var[:, s, 0:1], r[:, s:s + 1],
                                            ALU.subtract, ALU.mult)
                return ins

            def a(step, i, par):
                if step == 0:
                    chain.restart_always()
                    stats("a", i, 0, lambda s: w.x_res[:, i * LANES + s, :])
                    link(normalise("a", i, 0, lambda s: w.x_res[:, i * LANES + s, :], xl[par]))
                    dve.engine_nop().then_inc(c_["xl_ready"].sem, 1)
                    stats("a", i, 1, lambda s: xl[par][:, s, :])
                if step == 1:
                    normalise("a", i, 1, lambda s: xl[par][:, s, :], u_in[par]).then_inc(c_["u_normed"].sem, 1)
                    before(dve, "kv_ready", i)
                    dve.tensor_copy(k_t[:, :], w.psum[:, 0, 0:NCTX])
                    dve.tensor_copy(v[:, :], w.psum[0:NCTX, 0, P:P + D]).then_inc(c_["kv_copied"].sem, 1)
                if step == 2:
                    before(dve, "q_psum", i)
                    dve.tensor_copy(q_t[:, :, :], w.psum[:, 2, 0:LANES * P].rearrange(
                        "p (l t) -> p l t", t=P)).then_inc(c_["q_ready"].sem, 1)
                if step == 3:
                    before(dve, "scores_psum", i)
                    shape = [P, heads, LANES, NCTX]
                    for s in range(LANES):
                        ins = dve.tensor_tensor(score[:, :, s, :], w.psum[:, 0:heads, s * NCTX:(s + 1) * NCTX],
                                                vision[:, i, :].unsqueeze(1).to_broadcast([P, heads, NCTX]),
                                                ALU.add)
                    link(ins)
                    link(dve.tensor_reduce(top[:, :, :], score[:, :, :, :], AX.X, ALU.max))
                    link(dve.tensor_tensor(score[:, :, :, :], score[:, :, :, :],
                                           top[:, :, :].unsqueeze(3).to_broadcast(shape), ALU.subtract))
                    lanes = [(hd, s) for hd in range(heads) for s in range(LANES)]
                    for turn in range(top_k // 8):
                        src = score if turn == 0 else rest
                        for hd, s in lanes:
                            ins = dve.max(best[:, hd, s, :], src[:, hd, s, :])
                        link(ins)
                        for hd, s in lanes:
                            ins = dve.match_replace(rest[:, hd, s, :], best[:, hd, s, :], src[:, hd, s, :],
                                                    -1.0e30)
                        link(ins)
                    dve.engine_nop().then_inc(c_["shifted"].sem, 1)
                if step == 4:
                    before(dve, "exped", i)
                    link(dve.tensor_tensor(score[:, :, :, :], score[:, :, :, :], rest[:, :, :, :],
                                           ALU.subtract))
                    link(dve.tensor_reduce(total[:, :, :], score[:, :, :, :], AX.X, ALU.add))
                    link(dve.reciprocal(total[:, :, :], total[:, :, :]))
                    link(dve.tensor_tensor(total[:, :, :], total[:, :, :],
                                           text[:, bass.ds(i * LANES, LANES)].unsqueeze(1)
                                           .to_broadcast([P, heads, LANES]), ALU.mult))
                    for s in range(LANES):
                        ins = dve.tensor_scalar(mean[:, s, :], score[:, 0, s, :], total[:, 0, s:s + 1], None,
                                                ALU.mult)
                    link(ins)
                    for hd in range(1, heads):
                        for s in range(LANES):
                            ins = dve.scalar_tensor_tensor(mean[:, s, :], score[:, hd, s, :],
                                                           total[:, hd, s:s + 1], mean[:, s, :],
                                                           ALU.mult, ALU.add)
                        if hd < heads - 1:
                            link(ins)
                    ins.then_inc(c_["mean_ready"].sem, 1)
                    before(dve, "u_affine", i)
                    before(dve, "film_ready", i)
                    link(dve.scalar_tensor_tensor(u_in[par][:, :, :], mods_in[:, :, 0:D], 1.0,
                                                  u_in[par][:, :, :], ALU.add, ALU.mult))
                    dve.tensor_tensor(u_in[par][:, :, :], u_in[par][:, :, :], mods_in[:, :, D:2 * D],
                                      ALU.add).then_inc(c_["u_ready"].sem, 1)

            def b(step, i, par):
                if step == 0:
                    before(dve, "freq_psum", i)
                    x_cos = w.psum[:, 4, :].rearrange("p (k d) -> p k d", d=D)
                    x_sin = w.psum[:, 5, :].rearrange("p (k d) -> p k d", d=D)
                    dve.tensor_tensor(prod[0][:, :, :], x_cos, by_cos[:, :, :], ALU.mult)
                    dve.tensor_tensor(prod[1][:, :, :], x_sin, by_sin[:, :, :], ALU.mult)
                    dve.tensor_tensor(prod[2][:, :, :], x_cos, by_sin[:, :, :], ALU.mult)
                    dve.tensor_tensor(prod[3][:, :, :], x_sin, by_last[:, :, :],
                                      ALU.mult).then_inc(c_["prods_ready"].sem, 1)
                if step == 1:
                    before(dve, "skip_ready", i)
                    dve.wait_ge(sig("film_out_ready").sem, sig("film_out_ready").count(i))
                    before(dve, "y_psum", i)
                    link(dve.tensor_tensor(y[:, :, :], w.psum[:, 6, :].rearrange("p (l d) -> p l d", d=D),
                                           u_skip[par][:, :, :], ALU.add))
                    link(dve.scalar_tensor_tensor(y[:, :, :], mods_out[par][:, :, 0:D], 1.0, y[:, :, :],
                                                  ALU.add, ALU.mult))
                    link(dve.tensor_tensor(y[:, :, :], y[:, :, :], mods_out[par][:, :, D:2 * D], ALU.add))
                    link(dve.tensor_tensor(xt[:, :, :], xl[par][:, :, :], y[:, :, :], ALU.add))
                    stats("b", i, 0, lambda s: xt[:, s, :])
                if step == 2:
                    normalise("b", i, 0, lambda s: xt[:, s, :], h).then_inc(c_["h_normed"].sem, 1)
                    before(dve, "h_normed", i)
                    link(dve.tensor_tensor(xt[:, :, :], xt[:, :, :],
                                           rows["b2"][:, :].unsqueeze(1).to_broadcast([P, LANES, D]), ALU.add))
                if step == 4:
                    before(dve, "ffn_psum", i)
                    link(dve.tensor_tensor(xt[:, :, :], w.psum[:, 4, :].rearrange("p (l d) -> p l d", d=D),
                                           xt[:, :, :], ALU.add))
                    stats("b", i, 1, lambda s: xt[:, s, :])
                    normalise("b", i, 1, lambda s: xt[:, s, :], y).then_inc(c_["out_normed"].sem, 1)
                    before(dve, "out_affine", i)
                    tiles = w.x_res[:, bass.ds(i * LANES, LANES), :]
                    dve.tensor_tensor(tiles, tiles, y[:, :, :], ALU.add).then_inc(c_["x_updated"].sem, 1)

            over_batches(dve, a, b)

        @block.scalar
        def _(act):
            act.wait_ge(loaded.sem, all_loaded)

            def a(step, i, par):
                if step == 1:
                    before(act, "xl_t_psum", i)
                    act.activation(xl_t[:, :, :, :], w.psum[:, 1, :].rearrange("p (k l t) -> p k l t", k=DK, t=P),
                                   ACT.Copy).then_inc(c_["xl_t_ready"].sem, 1)
                if step == 4:
                    before(act, "shifted", i)
                    act.activation(score[:, :, :, :], score[:, :, :, :], ACT.Exp, scale=scale)
                    act.activation(rest[:, :, :, :], rest[:, :, :, :], ACT.Exp,
                                   scale=scale).then_inc(c_["exped"].sem, 1)
                    before(act, "mean_t_psum", i)
                    act.activation(mean_t[:, :, :], w.psum[0:NCTX, 0, 0:LANES * P].rearrange(
                        "p (l t) -> p l t", t=P), ACT.Copy).then_inc(c_["mean_t_ready"].sem, 1)
                    before(act, "c_psum", i)
                    act.activation(c_t[:, :, :, :], w.psum[:, 1, :].rearrange("p (k l t) -> p k l t", k=DK, t=P),
                                   ACT.Copy).then_inc(c_["c_ready"].sem, 1)
                    before(act, "film_psum", i)
                    act.activation(mods_in[:, :, :], w.psum[:, 0:2, :], ACT.Copy, scale=gate[:, 0:1]
                                   ).then_inc(c_["film_ready"].sem, 1)
                    act.activation(mods_out[par][:, :, :], w.psum[:, 2:4, :], ACT.Copy, scale=gate[:, 0:1]
                                   ).then_inc(sig("film_out_ready").sem, 1)

            def b(step, i, par):
                if step == 2:
                    before(act, "h_t_psum", i)
                    act.activation(h_t[:, :, :, :], w.psum[:, 7, :].rearrange("p (k l t) -> p k l t", k=DK, t=P),
                                   ACT.Copy).then_inc(c_["h_t_ready"].sem, 1)
                if step == 3:
                    for c in range(4):
                        act.wait_ge(sig("hid_psum").sem, sig("hid_psum").count(i * 4 + c))
                        for m in range(2):
                            j = 2 * c + m
                            ins = act.activation(hid[:, j, :, :], w.psum[:, 4 + c, m * D:(m + 1) * D]
                                                 .rearrange("p (l t) -> p l t", t=P),
                                                 ACT.Gelu, bias=b1[:, j:j + 1])
                        ins.then_inc(sig("hid_ready").sem, 1)

            over_batches(act, a, b)

        @block.tensor
        def _(pe):
            pe.wait_ge(loaded.sem, all_loaded)

            def a(step, i, par):
                if step == 0:
                    pe.wait_ge(sig("film_out_ready").sem, sig("film_out_ready").count(i - 1))
                    before(pe, "ctx_copied", i)
                    for k in range(2):
                        pe.matmul(w.psum[:, 0, 0:NCTX], wk[:, k, :], ctx_b[:, k, :], start=(k == 0), stop=(k == 1))
                    for k in range(2):
                        last = pe.matmul(w.psum[0:NCTX, 0, P:P + D], ctx_b[:, k, :], wv[:, k, :],
                                         start=(k == 0), stop=(k == 1))
                    last.then_inc(c_["kv_ready"].sem, 1)
                    before(pe, "xl_ready", i)
                    for k in range(DK):
                        for s in range(LANES):
                            at = (k * LANES + s) * P
                            last = pe.transpose(w.psum[:, 1, at:at + P], xl[par][:, s, k * P:(k + 1) * P],
                                                w.ident[:, :])
                    last.then_inc(c_["xl_t_psum"].sem, 1)
                if step == 1:
                    before(pe, "xl_t_ready", i)
                    for k in range(DK):
                        last = pe.matmul(w.psum[:, 2, 0:LANES * P], wq[:, k, :], xl_t[:, k, :, :],
                                         start=(k == 0), stop=(k == DK - 1))
                    last.then_inc(c_["q_psum"].sem, 1)
                if step == 2:
                    before(pe, "kv_copied", i)
                    before(pe, "q_ready", i)
                    for s in range(LANES):
                        for hd in range(heads):
                            part = slice(hd * dim, (hd + 1) * dim)
                            last = pe.matmul(w.psum[:, hd, s * NCTX:(s + 1) * NCTX], q_t[part, s, :],
                                             k_t[part, :], start=True, stop=True)
                    last.then_inc(c_["scores_psum"].sem, 1)
                if step == 4:
                    before(pe, "mean_ready", i)
                    for s in range(LANES):
                        last = pe.transpose(w.psum[0:NCTX, 0, s * P:(s + 1) * P], mean[:, s, :], w.ident[:, :])
                    last.then_inc(c_["mean_t_psum"].sem, 1)
                    before(pe, "mean_t_ready", i)
                    for k in range(DK):
                        last = pe.matmul(w.psum[:, 1, k * LANES * P:(k + 1) * LANES * P],
                                         v[:, k * P:(k + 1) * P], mean_t[:, :, :], start=True, stop=True)
                    last.then_inc(c_["c_psum"].sem, 1)
                    before(pe, "c_ready", i)
                    for n in range(2):
                        for s in range(LANES):
                            bank = w.psum[:, 2 * n + s, :]
                            for k in range(DK):
                                pe.matmul(bank, c_t[:, k, s, :], film[n][:, k, :], start=(k == 0), stop=False)
                            last = pe.matmul(bank, w.ones[0:1, :], film_b[n][:, :], start=False, stop=True)
                    last.then_inc(c_["film_psum"].sem, 1)

            def b(step, i, par):
                if step == 0:
                    before(pe, "u_ready", i)
                    before(pe, "x_updated", i - 1)
                    for f in range(4):
                        for s in range(LANES):
                            last = pe.matmul(w.psum[:, 4 + f // 2, (f % 2) * D:(f % 2 + 1) * D],
                                             forward[:, s, f * P:(f + 1) * P], u_in[par][:, s, :],
                                             start=(s == 0), stop=(s == LANES - 1))
                    last.then_inc(c_["freq_psum"].sem, 1)
                if step == 1:
                    before(pe, "spec_ready", i)
                    for s in range(LANES):
                        for f in range(4):
                            last = pe.matmul(w.psum[:, 6, s * D:(s + 1) * D], backward[:, f, s, :],
                                             spectrum[:, f, :], start=(f == 0), stop=(f == 3))
                    last.then_inc(c_["y_psum"].sem, 1)
                if step == 2:
                    before(pe, "h_affine", i)
                    for k in range(DK):
                        for s in range(LANES):
                            at = (k * LANES + s) * P
                            last = pe.transpose(w.psum[:, 7, at:at + P], h[:, s, k * P:(k + 1) * P],
                                                w.ident[:, :])
                    last.then_inc(c_["h_t_psum"].sem, 1)
                if step == 3:
                    before(pe, "h_t_ready", i)
                    for c in range(4):
                        for m in range(2):
                            j = 2 * c + m
                            for k in range(DK):
                                last = pe.matmul(w.psum[:, 4 + c, m * D:(m + 1) * D],
                                                 w1[:, k, j * P:(j + 1) * P], h_t[:, k, :, :],
                                                 start=(k == 0), stop=(k == DK - 1))
                        last.then_inc(sig("hid_psum").sem, 1)
                if step == 4:
                    for c in range(4):
                        pe.wait_ge(sig("hid_ready").sem, sig("hid_ready").count(i * 4 + c))
                    for s in range(LANES):
                        for j in range(HT):
                            last = pe.matmul(w.psum[:, 4, s * D:(s + 1) * D], hid[:, j, s, :], w2[:, j, :],
                                             start=(j == 0), stop=(j == HT - 1))
                    last.then_inc(c_["ffn_psum"].sem, 1)

            over_batches(pe, a, b)

    loaded.base = all_loaded
    w.advance(**{name: B for name in once})
    w.advance(film_out_ready=B, hid_psum=4 * B, hid_ready=4 * B, stats_a=2 * B, rstd_a=2 * B, stats_b=2 * B,
              rstd_b=2 * B)



def chosen_attention_stage(nc, w, ctx):
    experts, slots, hp, rotate = 8, 32, 128, 64
    scale = float(hp) ** -0.5
    HALF = experts // 2
    GROUPS = 2
    io = w.io
    N = B * slots

    def sb(name, shape, dt=F32):
        return ctx.enter_context(nc.sbuf_tensor(f"cho_{name}", shape, dt))

    xn_all = sb("xn_all", [P, TILES, D])
    gathered = sb("gathered", [P, DK, experts, B, slots])
    rope = sb("rope", [P, 2, experts, B, slots])
    wr = sb("wr", [P, DK, experts])
    wqkv = sb("wqkv", [P, DK, experts, 3 * hp])
    wo = sb("wo", [P, experts, D])
    table = sb("table", [P, LANES, 2, P])
    upto = sb("upto", [P, P])
    mask = sb("mask", [P, P])
    iota = sb("iota", [P, slots])
    score_t = sb("score_t", [P, LANES, B * experts])
    chosen_t = sb("chosen_t", [P, LANES, B * experts])
    slot_t = sb("slot_t", [P, LANES, B * experts])
    score = sb("score", [P, S])
    rest = sb("rest", [P, S])
    best = sb("best", [P, 8])
    xn = sb("xn", [P, LANES, D])
    xn_t = sb("xn_t", [P, LANES, DK, P])
    hot = sb("hot", [P, LANES, experts, slots])
    swapped = sb("swapped", [rotate, 2, N])
    v_all = xn_all[:, 0:experts * N // D, :].rearrange("p (e x) d -> p e (x d)", e=experts) \
                                            .rearrange("p e (b j) -> p e b j", j=slots)

    sig = w.counter
    loaded = sig("weights_loaded")
    loads = [(wr[:, :, :], io["wr_t"].rearrange("(k p) e -> p k e", p=P))]
    loads += [(wqkv[:, k, :, :], io["L3_ffn_Wqkv"][:, k * P:(k + 1) * P, :].rearrange("e p n -> p e n"))
              for k in range(DK)]
    loads += [(wo[:, :, :], io["L3_ffn_Wo"].rearrange("e p n -> p e n")),
              (table[:, :, :, :], io["rotary"].rearrange("(l p) c d -> p l c d", p=P)),
              (upto[:, :], io["upto"]), (mask[:, :], io["slot_mask"]),
              (iota[:, :], io["iota"][1:1 + slots].partition_broadcast(P))]
    all_loaded = loaded.base + 16 * len(loads)
    xn_ready, xn_t_psum, xn_t_ready = sig("xn_ready"), sig("xn_t_psum"), sig("xn_t_ready")
    gate_psum, exped = sig("scores_psum"), sig("exped")
    stepped, turned = sig("choice_step"), sig("choice_turned")

    with nc.Block() as block:
        @block.sync
        def _(sp):
            for dst, src in loads:
                sp.dma_start(dst, src).then_inc(loaded.sem, 16)

        @block.gpsimd
        def _(pool):
            chain = Chain(pool, w.chains["pool"])
            with pool.Fori(0, B) as i:
                chain.restart_always()
                for s in range(LANES):
                    layernorm_rstd(pool, w, chain, i * LANES + s, s)
                for s in range(LANES):
                    u = i * LANES + s
                    pool.wait_ge(xn_ready.sem, xn_ready.count(u))
                    pool.tensor_copy(xn_all[:, u, :], xn[:, s, :]).then_inc(sig("xn_kept").sem, 1)

        @block.vector
        def _(dve):
            chain = Chain(dve, w.chains["dve"])
            dve.wait_ge(loaded.sem, all_loaded)
            with dve.Fori(0, B) as i:
                chain.restart_always()
                for s in range(LANES):
                    layernorm_stats(dve, w, chain, i * LANES + s, s)
                for s in range(LANES):
                    u = i * LANES + s
                    dve.wait_ge(sig("xn_kept").sem, sig("xn_kept").count(i * LANES - 1))
                    dve.wait_ge(xn_t_psum.sem, xn_t_psum.count(i * LANES - 1))
                    layernorm_apply(dve, w, xn[:, s, :], u, s).then_inc(xn_ready.sem, 1)
            dve.wait_ge(exped.sem, exped.count(TILES - 1))
            chain.restart_always()
            chain.link(dve.tensor_scalar(score_t[:, :, :], score_t[:, :, :], 1.0, None, ALU.add))
            chain.link(dve.reciprocal(score_t[:, :, :], score_t[:, :, :]))
            dve.engine_nop().then_inc(stepped.sem, 1)
            dve.wait_ge(turned.sem, turned.count(0))
            chain.link(dve.tensor_copy(score[:, :], w.psum[:, 0, 0:S]))
            for n in range(slots // 8):
                src = score if n == 0 else rest
                chain.link(dve.max(best[:, :], src[:, :]))
                chain.link(dve.match_replace(rest[:, :], best[:, :], src[:, :], -1.0))
            chain.link(dve.tensor_scalar(rest[:, :], rest[:, :], 0.0, None, ALU.is_lt))
            dve.engine_nop().then_inc(stepped.sem, 1)
            dve.wait_ge(turned.sem, turned.count(1))
            chain.link(dve.tensor_copy(chosen_t[:, :, :], w.psum[:, 1, 0:S].rearrange("p (l x) -> p l x", l=LANES)))
            dve.engine_nop().then_inc(stepped.sem, 1)
            dve.wait_ge(turned.sem, turned.count(2))
            chain.link(dve.tensor_tensor(slot_t[:, :, :], w.psum[:, 2, 0:S].rearrange("p (l x) -> p l x", l=LANES),
                                         chosen_t[:, :, :], ALU.mult))

        @block.scalar
        def _(act):
            with act.Fori(0, B) as i:
                for s in range(LANES):
                    u = i * LANES + s
                    act.wait_ge(xn_t_psum.sem, xn_t_psum.count(u))
                    act.activation(xn_t[:, s, :, :], w.lane(s)[:, 0, 0:D].rearrange("p (k t) -> p k t", t=P),
                                   ACT.Copy).then_inc(xn_t_ready.sem, 1)
                for s in range(LANES):
                    u = i * LANES + s
                    act.wait_ge(gate_psum.sem, gate_psum.count(u))
                    act.activation(score_t[:, s, bass.ds(i * experts, experts)], w.lane(s)[:, 1, 0:experts],
                                   ACT.Exp, scale=-1.0).then_inc(exped.sem, 1)

        @block.tensor
        def _(pe):
            pe.wait_ge(loaded.sem, all_loaded)
            with pe.Fori(0, B) as i:
                for s in range(LANES):
                    pe.wait_ge(xn_ready.sem, xn_ready.count(i * LANES + s))
                    transpose_tile(pe, w, xn[:, s, :], w.lane(s)[:, 0, :],
                                   w.ident[:, :]).then_inc(xn_t_psum.sem, 1)
                for s in range(LANES):
                    pe.wait_ge(xn_t_ready.sem, xn_t_ready.count(i * LANES + s))
                    pe.wait_ge(exped.sem, exped.count(i * LANES - 1))
                    for k in range(DK):
                        last = pe.matmul(w.lane(s)[:, 1, 0:experts], xn_t[:, s, k, :], wr[:, k, :],
                                         start=(k == 0), stop=(k == DK - 1))
                    last.then_inc(gate_psum.sem, 1)
            pe.wait_ge(stepped.sem, stepped.count(0))
            for s in range(LANES):
                last = pe.transpose(w.psum[:, 0, s * P:(s + 1) * P], score_t[:, s, :], w.ident[:, :])
            last.then_inc(turned.sem, 1)
            pe.wait_ge(stepped.sem, stepped.count(1))
            for s in range(LANES):
                last = pe.transpose(w.psum[:, 1, s * P:(s + 1) * P], rest[:, s * P:(s + 1) * P], w.ident[:, :])
            last.then_inc(turned.sem, 1)
            pe.wait_ge(stepped.sem, stepped.count(2))
            pe.matmul(w.psum[:, 2, 0:P], upto[:, :], chosen_t[:, 0, :], start=True, stop=True)
            pe.matmul(w.psum[:, 2, P:2 * P], w.ones[:, :], chosen_t[:, 0, :], start=True, stop=False)
            pe.matmul(w.psum[:, 2, P:2 * P], upto[:, :], chosen_t[:, 1, :], start=False,
                      stop=True).then_inc(turned.sem, 1)

    loaded.base = all_loaded
    w.advance(choice_step=3, choice_turned=3)
    w.advance(**{name: TILES for name in ("stats_ready", "rstd_ready", "xn_ready", "xn_kept", "xn_t_psum",
                                          "xn_t_ready", "scores_psum", "exped")})

    hot_ready, gather_psum, gather_kept = sig("hot_ready"), sig("gather_psum"), sig("gather_kept")
    with nc.Block() as block:
        @block.gpsimd
        def _(pool):
            with pool.Fori(0, B) as i:
                pool.wait_ge(gather_psum.sem, gather_psum.count(i - 1))
                pool.tensor_copy(xn[:, :, :], xn_all[:, bass.ds(i * LANES, LANES), :]
                                 ).then_inc(sig("xn_kept").sem, 1)

        @block.vector
        def _(dve):
            with dve.Fori(0, B) as i:
                dve.wait_ge(gather_psum.sem, gather_psum.count(i - 1))
                for s in range(LANES):
                    dve.tensor_tensor(hot[:, s, :, :],
                                      slot_t[:, s, bass.ds(i * experts, experts)].unsqueeze(2)
                                      .to_broadcast([P, experts, slots]),
                                      iota[:, :].unsqueeze(1).to_broadcast([P, experts, slots]),
                                      ALU.is_equal).then_inc(hot_ready.sem, 1)
                dve.wait_ge(gather_psum.sem, gather_psum.count(i))
                for k in range(DK):
                    dve.tensor_copy(gathered[:, k, :, i, :],
                                    w.psum[:, k, 0:D].rearrange("p (e j) -> p e j", j=slots)
                                    ).then_inc(gather_kept.sem, 1)

        @block.scalar
        def _(act):
            with act.Fori(0, B) as i:
                act.wait_ge(gather_psum.sem, gather_psum.count(i))
                for c in range(2):
                    act.activation(rope[:, c, :, i, :], w.psum[:, 2 + c, 0:D].rearrange("p (e j) -> p e j", j=slots),
                                   ACT.Copy).then_inc(sig("rope_kept").sem, 1)

        @block.tensor
        def _(pe):
            with pe.Fori(0, B) as i:
                pe.wait_ge(sig("xn_kept").sem, sig("xn_kept").count(i))
                pe.wait_ge(hot_ready.sem, hot_ready.count(i * LANES + LANES - 1))
                pe.wait_ge(gather_kept.sem, gather_kept.count(i * 2 - 1))
                pe.wait_ge(sig("rope_kept").sem, sig("rope_kept").count(i * 2 - 1))
                for n in range(4):
                    for s in range(LANES):
                        lhs = xn[:, s, n * P:(n + 1) * P] if n < DK else table[:, s, n - DK, :]
                        last = pe.matmul(w.psum[:, n, 0:D], lhs, hot[:, s, :, :], start=(s == 0),
                                         stop=(s == LANES - 1))
                last.then_inc(gather_psum.sem, 1)
    w.advance(xn_kept=B, hot_ready=TILES, gather_psum=B, gather_kept=2 * B, rope_kept=2 * B)

    qkv_psum, qkv_kept, half_swapped = sig("qkv_psum"), sig("qkv_kept"), sig("half_swapped")
    with nc.Block() as block:
        @block.tensor
        def _(pe):
            for e in range(experts):
                base = 3 * (e % 2)
                if e >= 2:
                    pe.wait_ge(qkv_kept.sem, qkv_kept.count(e - 2))
                    pe.wait_ge(half_swapped.sem, half_swapped.count(2 * (e - 2) + 1))
                    pe.wait_ge(sig("v_kept").sem, sig("v_kept").count(e - 2))
                for n in range(3):
                    for k in range(DK):
                        last = pe.matmul(w.psum[:, base + n, :], wqkv[:, k, e, n * hp:(n + 1) * hp],
                                         gathered[:, k, e, :, :], start=(k == 0), stop=(k == DK - 1))
                last.then_inc(qkv_psum.sem, 1)

        @block.scalar
        def _(act):
            for e in range(experts):
                base = 3 * (e % 2)
                act.wait_ge(qkv_psum.sem, qkv_psum.count(e))
                for n in range(2):
                    if e >= 1:
                        act.wait_ge(qkv_kept.sem, qkv_kept.count(e - 1))
                    for c in range(2):
                        ins = act.activation(swapped[32 * (1 - c):32 * (2 - c), n, :],
                                             w.psum[32 * c:32 * (c + 1), base + n, :], ACT.Copy)
                    ins.then_inc(half_swapped.sem, 1)
                act.activation(v_all[:, e, :, :], w.psum[:, base + 2, :].rearrange("p (b j) -> p b j", j=slots),
                               ACT.Copy).then_inc(sig("v_kept").sem, 1)

        @block.vector
        def _(dve):
            chain = Chain(dve, w.chains["dve"])
            chain.restart_always()
            for e in range(experts):
                base = 3 * (e % 2)
                dve.wait_ge(qkv_psum.sem, qkv_psum.count(e))
                for n in range(2):
                    kept = gathered[:, n, e, :, :]
                    dve.wait_ge(half_swapped.sem, half_swapped.count(2 * e + n))
                    chain.link(dve.tensor_tensor(kept, w.psum[:, base + n, :]
                                                 .rearrange("p (b j) -> p b j", j=slots),
                                                 rope[:, 0, e, :, :], ALU.mult))
                    turned_half = swapped[:, n, :].rearrange("p (b j) -> p b j", j=slots)
                    chain.link(dve.tensor_tensor(turned_half, turned_half, rope[0:rotate, 1, e, :, :], ALU.mult))
                    chain.link(dve.tensor_tensor(kept[0:rotate], kept[0:rotate], turned_half, ALU.add))
                dve.engine_nop().then_inc(qkv_kept.sem, 1)
    w.advance(qkv_psum=experts, half_swapped=2 * experts, qkv_kept=experts, v_kept=experts)

    q_b = sb("q_b", [P, experts, slots])
    v_b = sb("v_b", [P, experts, slots])
    masked = sb("masked", [P, GROUPS, P])
    top = sb("top", [P, GROUPS])
    total = sb("total", [P, GROUPS])
    prob_t = sb("prob_t", [P, GROUPS, P])
    v_rows = sb("v_rows", [P, GROUPS, P])
    attn = sb("attn", [P, GROUPS, P])
    put = sb("put", [P, GROUPS, D])
    hot_t = sb("hot_t", [P, GROUPS, S])

    staged, scores_psum, shifted = sig("staged"), sig("scores_psum"), sig("shifted")
    prob_t_psum, prob_t_ready = sig("prob_t_psum"), sig("prob_t_ready")
    attn_psum, attn_ready, put_psum, put_ready = (sig(n) for n in ("attn_psum", "attn_ready", "put_psum",
                                                                  "put_ready"))
    hot_t_psum, hot_t_ready, out_psum, x_updated = (sig(n) for n in ("hot_t_psum", "hot_t_ready", "out_psum",
                                                                    "x_updated"))
    inverse_ready = sig("inverse_ready")

    with nc.Block() as block:
        @block.gpsimd
        def _(pool):
            with pool.Fori(0, B) as i:
                pool.wait_ge(prob_t_psum.sem, prob_t_psum.count(i * GROUPS - 1))
                pool.tensor_copy(q_b[:, :, :], gathered[:, 0, :, i, :])
                pool.tensor_copy(v_b[:, :, :], v_all[:, :, i, :]).then_inc(staged.sem, 1)

        @block.vector
        def _(dve):
            chain = Chain(dve, w.chains["dve"])
            with dve.Fori(0, B) as i:
                chain.restart_always()
                for g in range(GROUPS):
                    n = i * GROUPS + g
                    dve.wait_ge(scores_psum.sem, scores_psum.count(n))
                    chain.link(dve.tensor_tensor(masked[:, g, :], w.psum[:, g, 0:P], mask[:, :], ALU.add))
                    chain.link(dve.tensor_reduce(top[:, g:g + 1], masked[:, g, :], AX.X, ALU.max))
                    dve.tensor_scalar(masked[:, g, :], masked[:, g, :], top[:, g:g + 1], None,
                                      ALU.subtract).then_inc(shifted.sem, 1)
                for s in range(LANES):
                    part = slot_t[:, s, bass.ds(i * experts, experts)].unsqueeze(2).to_broadcast(
                        [P, experts, slots])
                    value = score_t[:, s, bass.ds(i * experts, experts)].unsqueeze(2).to_broadcast(
                        [P, experts, slots])
                    chain.link(dve.tensor_tensor(hot[:, s, :, :], part, iota[:, :].unsqueeze(1).to_broadcast(
                        [P, experts, slots]), ALU.is_equal))
                    dve.tensor_tensor(hot[:, s, :, :], hot[:, s, :, :], value,
                                      ALU.mult).then_inc(hot_ready.sem, 1)
                for g in range(GROUPS):
                    n = i * GROUPS + g
                    dve.wait_ge(exped.sem, exped.count(n))
                    dve.reciprocal(total[:, g:g + 1], total[:, g:g + 1]).then_inc(inverse_ready.sem, 1)
                for g in range(GROUPS):
                    n = i * GROUPS + g
                    dve.wait_ge(prob_t_psum.sem, prob_t_psum.count(n))
                    dve.tensor_copy(prob_t[:, g, :], w.psum[:, 2 + g, 0:P])
                    dve.tensor_copy(v_rows[:, g, :], w.psum[:, 2 + g, P:2 * P]).then_inc(prob_t_ready.sem, 1)
                for g in range(GROUPS):
                    n = i * GROUPS + g
                    dve.wait_ge(hot_t_psum.sem, hot_t_psum.count(n))
                    dve.tensor_copy(hot_t[:, g, :], w.psum[:, g, 0:S]).then_inc(hot_t_ready.sem, 1)
                for s in range(LANES):
                    u = i * LANES + s
                    dve.wait_ge(out_psum.sem, out_psum.count(u))
                    dve.tensor_tensor(w.x_res[:, u, :], w.x_res[:, u, :], w.psum[:, 4 + s, 0:D],
                                      ALU.add).then_inc(x_updated.sem, 1)

        @block.scalar
        def _(act):
            with act.Fori(0, B) as i:
                for g in range(GROUPS):
                    n = i * GROUPS + g
                    act.wait_ge(shifted.sem, shifted.count(n))
                    act.activation(masked[:, g, :], masked[:, g, :], ACT.Exp, scale=scale,
                                   accum_out=total[:, g:g + 1]).then_inc(exped.sem, 1)
                for g in range(GROUPS):
                    n = i * GROUPS + g
                    act.wait_ge(attn_psum.sem, attn_psum.count(n))
                    act.activation(attn[:, g, :], w.psum[:, 4 + g, 0:P], ACT.Copy).then_inc(attn_ready.sem, 1)
                for g in range(GROUPS):
                    n = i * GROUPS + g
                    act.wait_ge(inverse_ready.sem, inverse_ready.count(n))
                    act.wait_ge(put_psum.sem, put_psum.count(n))
                    act.activation(put[:, g, :], w.psum[:, 6 + g, 0:D], ACT.Copy,
                                   scale=total[:, g:g + 1]).then_inc(put_ready.sem, 1)

        @block.tensor
        def _(pe):
            with pe.Fori(0, B) as i:
                pe.wait_ge(staged.sem, staged.count(i))
                pe.wait_ge(x_updated.sem, x_updated.count(i * LANES - 1))
                for g in range(GROUPS):
                    es = slice(g * HALF, (g + 1) * HALF)
                    pe.matmul(w.psum[:, g, 0:P], q_b[:, es, :], gathered[:, 1, es, i, :], start=True,
                              stop=True).then_inc(scores_psum.sem, 1)
                for g in range(GROUPS):
                    es = slice(g * HALF, (g + 1) * HALF)
                    pe.wait_ge(exped.sem, exped.count(i * GROUPS + g))
                    pe.transpose(w.psum[:, 2 + g, 0:P], masked[:, g, :], w.ident[:, :])
                    pe.transpose(w.psum[:, 2 + g, P:2 * P], v_b[:, es, :],
                                 w.ident[:, :]).then_inc(prob_t_psum.sem, 1)
                pe.wait_ge(hot_ready.sem, hot_ready.count(i * LANES + LANES - 1))
                for g in range(GROUPS):
                    es = slice(g * HALF, (g + 1) * HALF)
                    for s in range(LANES):
                        last = pe.transpose(w.psum[:, g, s * P:(s + 1) * P], hot[:, s, es, :], w.ident[:, :])
                    last.then_inc(hot_t_psum.sem, 1)
                for g in range(GROUPS):
                    pe.wait_ge(prob_t_ready.sem, prob_t_ready.count(i * GROUPS + g))
                    pe.matmul(w.psum[:, 4 + g, 0:P], v_rows[:, g, :], prob_t[:, g, :], start=True,
                              stop=True).then_inc(attn_psum.sem, 1)
                for g in range(GROUPS):
                    pe.wait_ge(attn_ready.sem, attn_ready.count(i * GROUPS + g))
                    for x in range(HALF):
                        rows = slice(x * slots, (x + 1) * slots)
                        last = pe.matmul(w.psum[rows, 6 + g, 0:D], attn[:, g, rows], wo[:, g * HALF + x, :],
                                         start=True, stop=True)
                    last.then_inc(put_psum.sem, 1)
                pe.wait_ge(put_ready.sem, put_ready.count(i * GROUPS + GROUPS - 1))
                pe.wait_ge(hot_t_ready.sem, hot_t_ready.count(i * GROUPS + GROUPS - 1))
                for s in range(LANES):
                    for g in range(GROUPS):
                        last = pe.matmul(w.psum[:, 4 + s, 0:D], hot_t[:, g, s * P:(s + 1) * P], put[:, g, :],
                                         start=(g == 0), stop=(g == GROUPS - 1))
                    last.then_inc(out_psum.sem, 1)

    w.advance(staged=B)
    w.advance(**{name: TILES for name in (
        "scores_psum", "shifted", "exped", "inverse_ready", "prob_t_psum", "prob_t_ready", "attn_psum",
        "attn_ready", "put_psum", "put_ready", "hot_ready", "hot_t_psum", "hot_t_ready", "out_psum",
        "x_updated")})



STAGES = [
    attention_stage("self0", 8, 64, "L0_xattn_Wq", "L0_xattn_Wk", "L0_xattn_Wv", "L0_xattn_Wo", "L0_xattn_bo"),
    quantised_stage("int8", prepare_int8),
    attention_stage("self1", 16, 16, "L1_xattn_w_q", "L1_xattn_w_k", "L1_xattn_w_v", "L1_xattn_w_o",
                    "L1_xattn_b_o", "L1_xattn_b_q", "L1_xattn_b_k", "L1_xattn_b_v"),
    experts_stage,
    global_attention_stage,
    quantised_stage("ternary", prepare_ternary),
    selective_stage,
    chosen_attention_stage,
]



def shape_tables():
    turn = 2.0 * np.pi / FREQ
    f = np.arange(S)
    t = np.arange(S)
    cos = np.cos(turn * np.outer(t, f))
    sin = np.sin(turn * np.outer(t, f))
    last = np.cos(np.pi * t)
    with_last = sin.copy()
    with_last[:, 0] = last
    weight = np.where(f == 0, 1.0, 2.0) / FREQ
    e = cos[:, 0:P].copy()
    e[:, 0] = last
    lag = 2.0 * np.concatenate([cos, sin, e], axis=1).reshape(SEQ_A, SEQ_B, 5 * P)
    half = np.repeat([0, 1], N_STATE)
    phase = np.zeros((P, 4))
    phase[:, 0] = np.where(half, 0.0, 0.25)
    phase[:, 1] = np.where(half, 0.25, 0.5)
    phase[:, 2] = np.where(half, 0.5, 0.25)
    inv_freq = 10000.0 ** -(np.arange(32) / 32.0)
    angle = np.outer(t, inv_freq)
    rotary = np.zeros((S, 2, P))
    rotary[:, 0, :] = np.concatenate([np.cos(angle), np.cos(angle), np.ones((S, 64))], axis=1)
    rotary[:, 1, 0:64] = np.concatenate([-np.sin(angle), np.sin(angle)], axis=1)
    n = np.arange(P)
    same = (n[:, None] // 32) == (n[None, :] // 32)
    tables = {"rotary": rotary, "upto": n[:, None] <= n[None, :],
              "slot_mask": np.where(same & (n[:, None] >= n[None, :]), 0.0, -1.0e30),
              "forward": np.concatenate([cos, with_last], axis=1),
              "backward": np.concatenate([(cos * weight).T, (with_last * weight).T], axis=0),
              "lag_transform": lag, "phase": phase,
              "steps": np.stack([SEQ_B * np.arange(SEQ_A), np.arange(SEQ_B)])}
    return {name: np.ascontiguousarray(a, dtype=np.float32) for name, a in tables.items()}


def lay_out(inputs):
    def array(name):
        return np.ascontiguousarray(inputs[name])

    def turned(name, *axes):
        return np.ascontiguousarray(np.transpose(array(name), axes or None))

    skip = {"ctx_768", "mask_BxS_bf1", "mask_BxS2_bf1", "L3_xattn_A_re", "L3_xattn_A_im", "L3_xattn_C_re",
            "L3_xattn_C_im", "L3_xattn_mod_gate", "L3_ffn_Wr", "L1_ffn_gate_w", "L1_ffn_expert_w", "L2_ffn_ternary_weight", "L2_ffn_act_scale"}
    arrays = {name: array(name) for name in inputs if name not in skip}
    arrays["ctx_t"] = np.ascontiguousarray(np.transpose(array("ctx_768"), (2, 0, 1)))
    arrays["gate_t"] = np.ascontiguousarray(array("L1_ffn_gate_w").T)
    arrays["expert_t"] = np.ascontiguousarray(np.transpose(array("L1_ffn_expert_w"), (2, 0, 1)))
    arrays["ternary_t"] = np.ascontiguousarray(array("L2_ffn_ternary_weight").T)
    arrays["act_scale"] = array("L2_ffn_act_scale").reshape(1)
    arrays["text_mask_t"] = np.ascontiguousarray(
        array("mask_BxS_bf1").view(np.uint8).reshape(TILES, P).T)
    arrays["vision_mask"] = array("mask_BxS2_bf1").view(np.uint8)
    arrays["wr_t"] = turned("L3_ffn_Wr")
    arrays["mod_gate"] = array("L3_xattn_mod_gate").reshape(1)
    for part in ("A_re", "A_im", "C_re", "C_im"):
        arrays[part.lower() + "_t"] = turned(f"L3_xattn_{part}")
    arrays.update(shape_tables())
    arrays["ident"] = np.eye(P, dtype=np.float32)
    arrays["iota"] = np.arange(P, dtype=np.float32)
    return arrays


def kernel(**inputs):
    import concourse.bacc as bacc
    from concourse.bass_utils import run_bass_kernel_spmd

    nc = bacc.Bacc("TRN2", target_bir_lowering=False, num_devices=1)
    arrays, io = {}, {}
    for name, a in lay_out(inputs).items():
        arrays[f"in_{name}"] = a
        io[name] = nc.dram_tensor(f"in_{name}", a.shape, mybir.dt.from_np(a.dtype), kind="ExternalInput").ap()
    out = nc.dram_tensor("out", (B, S, D), F32, kind="ExternalOutput").ap()
    program(nc, io, out, STAGES)
    result = run_bass_kernel_spmd(nc, [arrays], core_ids=[0])
    return result.results[0]["out"]
```

```python
from contextlib import ExitStack

import numpy as np

import concourse.bass as bass
from concourse import mybir

F32 = mybir.dt.float32
BF16 = mybir.dt.bfloat16
F32R = mybir.dt.float32r
I32 = mybir.dt.int32
U32 = mybir.dt.uint32
U8 = mybir.dt.uint8
ALU = mybir.AluOpType
ACT = mybir.ActivationFunctionType
AX = mybir.AxisListType

P = 128
B, S, D = 16, 256, 256
NCTX, DC = 120, 192
LANES = S // P
TILES = B * LANES
DK = D // P
CP = DC // 2
LN_EPS = 1e-5
ROUND = 1.5 * 2.0 ** 23


class Counter:

    def __init__(self, sem):
        self.sem, self.base = sem, 0

    def count(self, n):
        return self.base + n + 1


class Chain:

    def __init__(self, eng, sem):
        self.eng, self.sem, self.n = eng, sem, 0

    def restart(self):
        if self.n:
            self.eng.sem_clear(self.sem)
        self.n = 0

    def restart_always(self):
        self.eng.sem_clear(self.sem)
        self.n = 0

    def link(self, instruction):
        self.n += 1
        instruction.then_inc(self.sem, 1)
        self.eng.wait_ge(self.sem, self.n)


def program(nc, io, out, stages):
    with ExitStack() as ctx:
        whole = Whole(nc, io, ctx)
        load_x(nc, whole)
        for stage in stages:
            with ExitStack() as stage_ctx:
                stage(nc, whole, stage_ctx)
        store_x(nc, whole, out)


class Whole:

    def __init__(self, nc, io, ctx):
        self.nc, self.io = nc, io
        self.x_res = ctx.enter_context(nc.sbuf_tensor("x_res", [P, TILES + 1, D], F32))
        self.ident = ctx.enter_context(nc.sbuf_tensor("ident", [P, P], F32))
        self.ident16 = ctx.enter_context(nc.sbuf_tensor("ident16", [P, P], BF16))
        self.ones = ctx.enter_context(nc.sbuf_tensor("ones", [P, P], F32))
        self.neg_half = ctx.enter_context(nc.sbuf_tensor("neg_half", [P, LANES], F32))
        self.eps = ctx.enter_context(nc.sbuf_tensor("eps", [P, LANES], F32))
        self.stats = ctx.enter_context(nc.sbuf_tensor("stats", [P, LANES, 6], F32))
        self.mean_var = ctx.enter_context(nc.sbuf_tensor("mean_var", [P, LANES, 2], F32))
        self.rstd = ctx.enter_context(nc.sbuf_tensor("rstd", [P, LANES], F32))
        self.psum = ctx.enter_context(nc.psum_tensor("psum", [P, 8, 512], F32))
        self.counters = {}
        self.ctx = ctx
        self.chains = {e: ctx.enter_context(nc.semaphore(f"{e}_chain")) for e in ("dve", "pool", "act")}

    def counter(self, name):
        if name not in self.counters:
            self.counters[name] = Counter(self.ctx.enter_context(self.nc.semaphore(name)))
        return self.counters[name]

    def lane(self, s):
        return self.psum[:, 4 * s:4 * s + 4, :]

    def advance(self, **events):
        for name, n in events.items():
            self.counters[name].base += n


LOOKED_BACK = ("x_updated", "kv_ready", "exped", "attn_ready", "gated_used", "prob_t_psum", "prob_t_ready",
               "prob_t_ready2", "film_out_ready", "xn_kept", "xn_t_psum", "gather_psum", "gather_kept", "rope_kept")


def load_x(nc, w):
    loaded = w.counter("inputs_loaded")
    for name in LOOKED_BACK:
        w.counter(name).base = 1
    with nc.Block() as block:
        @block.sync
        def _(sp):
            for name in LOOKED_BACK:
                sp.sem_inc(w.counter(name).sem, 1)
            x_tiles = w.io["x"].rearrange("b (l p) d -> p (b l) d", p=P)
            step = TILES // 4
            for c in range(4):
                sp.dma_start(w.x_res[:, c * step:(c + 1) * step, :],
                             x_tiles[:, c * step:(c + 1) * step, :]).then_inc(loaded.sem, 16)
            sp.dma_start(w.ident[:, :], w.io["ident"]).then_inc(loaded.sem, 16)
            sp.wait_ge(loaded.sem, 16 * 5)

        @block.vector
        def _(dve):
            dve.memset(w.ones[:, :], 1.0)
            dve.memset(w.x_res[:, TILES, :], 0.0)
            dve.memset(w.neg_half[:, :], -0.5)
            dve.memset(w.eps[:, :], LN_EPS)
            dve.wait_ge(loaded.sem, 16 * 5)
            dve.tensor_copy(w.ident16[:, :], w.ident[:, :])
    loaded.base += 16 * 5


def store_x(nc, w, out):
    stored = w.counter("output_stored")
    with nc.Block() as block:
        @block.sync
        def _(sp):
            out_tiles = out.rearrange("b (l p) d -> p (b l) d", p=P)
            step = TILES // 4
            for c in range(4):
                sp.dma_start(out_tiles[:, c * step:(c + 1) * step, :],
                             w.x_res[:, c * step:(c + 1) * step, :]).then_inc(stored.sem, 16)
            sp.wait_ge(stored.sem, 16 * 4)



def layernorm_stats(dve, w, chain, u, s):
    chain.link(dve.bn_stats(w.stats[:, s, :], w.x_res[:, u, :]))
    dve.bn_aggr(w.mean_var[:, s, :], w.stats[:, s, :]).then_inc(w.counter("stats_ready").sem, 1)


def layernorm_rstd(pool, w, chain, u, s):
    pool.wait_ge(w.counter("stats_ready").sem, w.counter("stats_ready").count(u))
    chain.link(pool.tensor_tensor(w.rstd[:, s:s + 1], w.mean_var[:, s, 1:2], w.eps[:, 0:1], ALU.add))
    pool.tensor_tensor(w.rstd[:, s:s + 1], w.rstd[:, s:s + 1], w.neg_half[:, 0:1],
                       ALU.pow).then_inc(w.counter("rstd_ready").sem, 1)


def layernorm_apply(dve, w, xn, u, s):
    dve.wait_ge(w.counter("rstd_ready").sem, w.counter("rstd_ready").count(u))
    return dve.tensor_scalar(xn, w.x_res[:, u, :], w.mean_var[:, s, 0:1], w.rstd[:, s:s + 1],
                             ALU.subtract, ALU.mult)


def transpose_tile(pe, w, xn, bank, ident):
    for k in range(DK):
        last = pe.transpose(bank[:, k * P:(k + 1) * P], xn[:, k * P:(k + 1) * P], ident)
    return last



def attention_stage(tag, heads, dim, q_w, k_w, v_w, o_w, o_b, q_b=None, k_b=None, v_b=None):
    pad = max(dim, 32)
    inner = heads * pad
    parts = inner // P
    per = P // pad
    scale = float(dim) ** -0.5

    def stage(nc, w, ctx):
        io = w.io

        def sb(name, shape, dt=F32):
            return ctx.enter_context(nc.sbuf_tensor(f"{tag}_{name}", shape, dt))

        wq = sb("wq", [P, DK, inner])
        wk = sb("wk", [CP, 2, inner])
        wv = sb("wv", [CP, 2, inner])
        wo = sb("wo", [P, parts, D])
        bo = sb("bo", [2, D])
        bo_high = sb("bo_high", [2, D], F32R)
        bo_parts = sb("bo_parts", [2, D], F32R)
        bv_high = sb("bv_high", [2, inner], F32R)
        bv_parts = sb("bv_parts", [2, inner], F32R)
        is_low = sb("is_low", [2, 1])
        ones_r = sb("ones_r", [2, P], F32R)
        ctx_t = sb("ctx_t", [CP, 2, B, NCTX])
        ctx_b = sb("ctx_b", [CP, 2, NCTX])
        bq = sb("bq", [P, parts])
        bk = sb("bk", [P, parts])
        bv = sb("bv", [2, inner])
        k_t = sb("k_t", [P, parts, NCTX])
        v = sb("v", [NCTX, inner])
        xn = sb("xn", [P, LANES, D])
        xn_t = sb("xn_t", [P, DK, P])
        q_t = sb("q_t", [P, parts, P])
        top = sb("top", [P, per, parts])
        total = sb("total", [P, per, parts])
        prob = sb("prob", [P, LANES, per, parts, NCTX])
        prob_t = sb("prob_t", [NCTX, per, parts, P])
        attn_t = sb("attn_t", [P, parts, P])

        padded = pad != dim
        biased = q_b is not None
        cleared = w.counter("weights_cleared")
        loaded = w.counter("weights_loaded")
        loads = []
        if padded:
            for k in range(DK):
                loads.append((wq[:, k, :].rearrange("p (h e) -> p h e", e=pad)[:, :, 0:dim],
                              io[q_w][k * P:(k + 1) * P, :].rearrange("p (h e) -> p h e", e=dim)))
            for k in range(2):
                for dst, src in ((wk, io[k_w]), (wv, io[v_w])):
                    loads.append((dst[:, k, :].rearrange("p (h e) -> p h e", e=pad)[:, :, 0:dim],
                                  src[k * CP:(k + 1) * CP, :].rearrange("p (h e) -> p h e", e=dim)))
            for r in range(per):
                loads.append((wo[r * pad:r * pad + dim, :, :],
                              io[o_w].rearrange("(k r e) n -> r e k n", r=per, e=dim)[r]))
        else:
            loads.append((wq[:, :, :], io[q_w].rearrange("(k p) n -> p k n", p=P)))
            loads.append((wk[:, :, :], io[k_w].rearrange("(k p) n -> p k n", p=CP)))
            loads.append((wv[:, :, :], io[v_w].rearrange("(k p) n -> p k n", p=CP)))
            loads.append((wo[:, :, :], io[o_w].rearrange("(k p) n -> p k n", p=P)))
        if biased:
            for r in range(per):
                for dst, src in ((bq, io[q_b]), (bk, io[k_b])):
                    loads.append((dst[r * pad:r * pad + dim, :],
                                  src.rearrange("(k r e) -> r e k", r=per, e=dim)[r]))
            for row in range(2):
                loads.append((bv[row:row + 1, :].rearrange("p (h e) -> p h e", e=pad)[:, :, 0:dim],
                              io[v_b].rearrange("(a h e) -> a h e", a=1, e=dim)))
        loads.append((bo[:, :], io[o_b].partition_broadcast(2)))
        loads.append((ctx_t[:, :, :, :], io["ctx_t"].rearrange("(k p) b j -> p k b j", p=CP)))
        all_loaded = loaded.base + 16 * len(loads)

        sig = w.counter
        ctx_copied, k_psum, k_ready, v_psum, v_ready = (
            sig(n) for n in ("ctx_copied", "k_psum", "k_ready", "v_psum", "v_ready"))
        xn_ready, xn_t_psum, xn_t_ready = sig("xn_ready"), sig("xn_t_psum"), sig("xn_t_ready")
        q_psum, q_ready = sig("q_psum"), sig("q_ready")
        scores_psum, shifted, exped = sig("scores_psum"), sig("shifted"), sig("exped")
        normalised, rows_split = sig("normalised"), sig("rows_split")
        prob_t_psum, prob_t_ready = sig("prob_t_psum"), sig("prob_t_ready")
        attn_psum, attn_ready = sig("attn_psum"), sig("attn_ready")
        out_psum, x_updated = sig("out_psum"), sig("x_updated")

        scores = w.psum[:, 0:per, 0:parts * NCTX].rearrange("p r (k j) -> p r k j", j=NCTX)

        softmax_is_long = per > 2

        def turns(eng, turn):
            def some(t):
                return lambda ahead: 0 <= t + ahead < TILES

            for t in range(-3, 0):
                turn(t, t % LANES, t // LANES, some(t))
            with eng.Fori(0, B - 2) as i:
                for s in range(LANES):
                    turn(i * LANES + s, s, i, lambda ahead: True)
            for t in range(TILES - 4, TILES):
                turn(t, t % LANES, t // LANES, some(t))

        with nc.allow_non_contiguous_dma(reason="padded weights"), nc.Block() as block:
            @block.sync
            def _(sp):
                if padded:
                    sp.wait_ge(cleared.sem, cleared.count(0))
                for dst, src in loads:
                    sp.dma_start(dst, src).then_inc(loaded.sem, 16)
                sp.wait_ge(loaded.sem, all_loaded)

            @block.gpsimd
            def _(pool):
                chain = Chain(pool, w.chains["pool"])
                if padded:
                    for t in (wq, wk, wv, wo):
                        pool.memset(t[:, :, :], 0.0)
                    for t in (bq, bk):
                        pool.memset(t[:, :], 0.0)
                    pool.memset(bv[:, :], 0.0).then_inc(cleared.sem, 1)
                pool.wait_ge(loaded.sem, all_loaded)

                def turn(t, s, batch, exists):
                    if s == 0:
                        chain.restart_always()
                    if exists(3):
                        layernorm_rstd(pool, w, chain, t + 3, 1 - s)
                    if s == 0 and exists(2):
                        if exists(0):
                            pool.wait_ge(v_psum.sem, v_psum.count(batch))
                        pool.tensor_copy(ctx_b[:, :, :], ctx_t[:, :, batch + 1, :]).then_inc(ctx_copied.sem, 1)

                turns(pool, turn)
                chain.restart_always()

            @block.vector
            def _(dve):
                chain = Chain(dve, w.chains["dve"])
                dve.wait_ge(loaded.sem, all_loaded)
                dve.tensor_scalar(is_low[:, :], w.ident[0:2, 1:2], -1.0, None, ALU.mult)
                chain.link(dve.tensor_copy(ones_r[:, :], w.ones[0:2, :]))
                for raw, high, both in ((bo, bo_high, bo_parts),) + (((bv, bv_high, bv_parts),) if biased else ()):
                    chain.link(dve.tensor_copy(high[:, :], raw[:, :]))
                    chain.link(dve.scalar_tensor_tensor(both[:, :], high[:, :].bitcast(F32), is_low[:, :],
                                                        raw[:, :], ALU.mult, ALU.add))
                dve.engine_nop().then_inc(rows_split.sem, 1)

                def keep_queries(u):
                    dve.wait_ge(q_psum.sem, q_psum.count(u))
                    src = w.psum[:, 1, 0:parts * P].rearrange("p (k t) -> p k t", t=P)
                    if biased:
                        ins = dve.tensor_tensor(q_t[:, :, :], src,
                                                bq[:, :].unsqueeze(2).to_broadcast([P, parts, P]), ALU.add)
                    else:
                        ins = dve.tensor_copy(q_t[:, :, :], src)
                    ins.then_inc(q_ready.sem, 1)

                def turn(t, s, batch, exists):
                    if s == 0:
                        chain.restart_always()
                    p = 1 - s
                    all_keys = [P, per, parts, NCTX]
                    if exists(1):
                        dve.wait_ge(scores_psum.sem, scores_psum.count(t + 1))
                        chain.link(dve.tensor_reduce(top[:, :, :], scores, AX.X, ALU.max))
                        dve.tensor_tensor(prob[:, p, :, :, :], scores,
                                          top[:, :, :].unsqueeze(3).to_broadcast(all_keys),
                                          ALU.subtract).then_inc(shifted.sem, 1)
                    if exists(3):
                        layernorm_stats(dve, w, chain, t + 3, p)
                    if exists(2) and softmax_is_long:
                        keep_queries(t + 2)
                    if exists(1):
                        dve.wait_ge(exped.sem, exped.count(t + 1))
                        chain.link(dve.tensor_reduce(total[:, :, :], prob[:, p, :, :, :], AX.X, ALU.add))
                        chain.link(dve.reciprocal(total[:, :, :], total[:, :, :]))
                        dve.tensor_tensor(prob[:, p, :, :, :], prob[:, p, :, :, :],
                                          total[:, :, :].unsqueeze(3).to_broadcast(all_keys),
                                          ALU.mult).then_inc(normalised.sem, 1)
                    if exists(3):
                        layernorm_apply(dve, w, xn[:, p, :], t + 3, p).then_inc(xn_ready.sem, 1)
                    if exists(2) and not softmax_is_long:
                        keep_queries(t + 2)
                    if exists(0):
                        dve.wait_ge(out_psum.sem, out_psum.count(t))
                        dve.tensor_tensor(w.x_res[:, t, :], w.psum[:, 5, 0:D], w.x_res[:, t, :],
                                          ALU.add).then_inc(x_updated.sem, 1)

                turns(dve, turn)
                chain.restart_always()

            @block.scalar
            def _(act):
                act.wait_ge(loaded.sem, all_loaded)

                def turn(t, s, batch, exists):
                    if exists(0):
                        for r in range(per):
                            act.wait_ge(prob_t_psum.sem, prob_t_psum.count(t * per + r))
                            act.activation(prob_t[:, r, :, :], w.psum[0:NCTX, 4 + r, 0:parts * P]
                                           .rearrange("p (k t) -> p k t", t=P),
                                           ACT.Copy).then_inc(prob_t_ready.sem, 1)
                        act.wait_ge(attn_psum.sem, attn_psum.count(t))
                        act.activation(attn_t[:, :, :],
                                       w.psum[:, 4, 0:parts * P].rearrange("p (k t) -> p k t", t=P),
                                       ACT.Copy).then_inc(attn_ready.sem, 1)
                    if exists(2):
                        act.wait_ge(xn_t_psum.sem, xn_t_psum.count(t + 2))
                        act.activation(xn_t[:, :, :], w.psum[:, 0, 0:D].rearrange("p (k t) -> p k t", t=P),
                                       ACT.Copy).then_inc(xn_t_ready.sem, 1)
                    if exists(1):
                        act.wait_ge(shifted.sem, shifted.count(t + 1))
                        act.activation(prob[:, 1 - s, :, :, :], prob[:, 1 - s, :, :, :], ACT.Exp,
                                       scale=scale).then_inc(exped.sem, 1)
                    if s == 0 and exists(2):
                        act.wait_ge(k_psum.sem, k_psum.count(batch + 1))
                        for k in range(parts):
                            last = act.activation(k_t[:, k, :], w.psum[:, 3, k * NCTX:(k + 1) * NCTX],
                                                  ACT.Identity, bias=bk[:, k:k + 1] if biased else 0.0)
                        last.then_inc(k_ready.sem, 1)
                    if s == 1 and exists(1):
                        act.wait_ge(v_psum.sem, v_psum.count(batch + 1))
                        act.activation(v[:, :], w.psum[0:NCTX, 2, 0:inner], ACT.Copy).then_inc(v_ready.sem, 1)

                turns(act, turn)

            @block.tensor
            def _(pe):
                pe.wait_ge(loaded.sem, all_loaded)
                pe.wait_ge(rows_split.sem, rows_split.count(0))

                def turn(t, s, batch, exists):
                    if exists(1):
                        if s == 1:
                            pe.wait_ge(k_ready.sem, k_ready.count(batch + 1))
                        else:
                            pe.wait_ge(v_ready.sem, v_ready.count(batch))
                        pe.wait_ge(q_ready.sem, q_ready.count(t + 1))
                        for r in range(per):
                            for k in range(parts):
                                rows = slice(r * pad, (r + 1) * pad)
                                last = pe.matmul(w.psum[:, r, k * NCTX:(k + 1) * NCTX],
                                                 q_t[rows, k, :], k_t[rows, k, :], start=True, stop=True)
                        last.then_inc(scores_psum.sem, 1)
                    if exists(-1):
                        pe.wait_ge(x_updated.sem, x_updated.count(t - 1))
                    if exists(0):
                        pe.wait_ge(normalised.sem, normalised.count(t))
                        for r in range(per):
                            for k in range(parts):
                                last = pe.transpose(w.psum[0:NCTX, 4 + r, k * P:(k + 1) * P],
                                                    prob[:, s, r, k, :], w.ident[:, :])
                            last.then_inc(prob_t_psum.sem, 1)
                        for r in range(per):
                            pe.wait_ge(prob_t_ready.sem, prob_t_ready.count(t * per + r))
                            for k in range(parts):
                                h = k * per + r
                                last = pe.matmul(w.psum[r * pad:(r + 1) * pad, 4, k * P:(k + 1) * P],
                                                 v[:, h * pad:(h + 1) * pad], prob_t[:, r, k, :],
                                                 start=True, stop=True)
                        last.then_inc(attn_psum.sem, 1)
                    if exists(1):
                        pe.wait_ge(shifted.sem, shifted.count(t + 1))
                    if exists(2):
                        pe.wait_ge(xn_ready.sem, xn_ready.count(t + 2))
                        transpose_tile(pe, w, xn[:, s, :], w.psum[:, 0, :], w.ident[:, :]).then_inc(xn_t_psum.sem, 1)
                    if s == 0 and exists(2):
                        pe.wait_ge(ctx_copied.sem, ctx_copied.count(batch + 1))
                        for m in range(parts):
                            for k in range(2):
                                last = pe.matmul(w.psum[:, 3, m * NCTX:(m + 1) * NCTX],
                                                 wk[:, k, m * P:(m + 1) * P], ctx_b[:, k, :],
                                                 start=(k == 0), stop=(k == 1))
                        last.then_inc(k_psum.sem, 1)
                    if s == 1 and exists(1):
                        if biased:
                            pe.matmul(w.psum[0:NCTX, 2, 0:inner], ones_r[:, 0:NCTX], bv_parts[:, :], start=True,
                                      stop=False)
                        for k in range(2):
                            last = pe.matmul(w.psum[0:NCTX, 2, 0:inner], ctx_b[:, k, :], wv[:, k, :],
                                             start=(k == 0 and not biased), stop=(k == 1))
                        last.then_inc(v_psum.sem, 1)
                    if exists(2):
                        pe.wait_ge(xn_t_ready.sem, xn_t_ready.count(t + 2))
                        for m in range(parts):
                            for k in range(DK):
                                last = pe.matmul(w.psum[:, 1, m * P:(m + 1) * P],
                                                 wq[:, k, m * P:(m + 1) * P], xn_t[:, k, :],
                                                 start=(k == 0), stop=(k == DK - 1))
                        last.then_inc(q_psum.sem, 1)
                    if exists(0):
                        pe.wait_ge(attn_ready.sem, attn_ready.count(t))
                        pe.matmul(w.psum[:, 5, 0:D], ones_r[:, :], bo_parts[:, :], start=True, stop=False)
                        for k in range(parts):
                            last = pe.matmul(w.psum[:, 5, 0:D], attn_t[:, k, :], wo[:, k, :],
                                             start=False, stop=(k == parts - 1))
                        last.then_inc(out_psum.sem, 1)

                turns(pe, turn)

        loaded.base = all_loaded
        if padded:
            cleared.base += 1
        w.advance(**{name: B for name in ("ctx_copied", "k_psum", "k_ready", "v_psum", "v_ready")})
        w.advance(rows_split=1, **{name: TILES for name in (
            "stats_ready", "rstd_ready", "xn_ready", "xn_t_psum", "xn_t_ready", "q_psum", "q_ready",
            "scores_psum", "shifted", "exped", "normalised", "attn_psum", "attn_ready", "out_psum",
            "x_updated")})
        w.advance(prob_t_psum=TILES * per, prob_t_ready=TILES * per)

    return stage



def quantised_stage(tag, prepare):
    per_token = tag == "int8"

    def stage(nc, w, ctx):
        io = w.io

        def sb(name, shape, dt=F32):
            return ctx.enter_context(nc.sbuf_tensor(f"{tag}_{name}", shape, dt))

        w_t = sb("w_t", [P, DK, D], BF16)
        w_scale = sb("w_scale", [P, D])
        bias = sb("bias", [P, D])
        prepare(nc, w, sb, w_t, w_scale, bias)
        xn = sb("xn", [P, LANES, D])
        x_scale = sb("x_scale", [P, LANES])
        x_inv = sb("x_inv", [P, LANES])
        x_q = sb("x_q", [P, LANES, D], BF16)
        x_qt = sb("x_qt", [P, LANES, DK, P], BF16)
        x_bias = sb("x_bias", [P, LANES, D])
        scaled = sb("scaled", [P, LANES, D])

        sig = w.counter
        xn_ready, xn_t_psum, xn_t_ready = sig("xn_ready"), sig("xn_t_psum"), sig("xn_t_ready")
        out_psum, x_updated, x_biased = sig("out_psum"), sig("x_updated"), sig("x_biased")

        def turns(eng, turn):
            def some(t):
                return lambda ahead: 0 <= t + ahead < TILES

            for t in range(-2, 0):
                turn(t, t % LANES, some(t))
            with eng.Fori(0, B - 1) as i:
                for s in range(LANES):
                    turn(i * LANES + s, s, lambda ahead: True)
            for t in range(TILES - 2, TILES):
                turn(t, t % LANES, some(t))

        with nc.Block() as block:
            @block.gpsimd
            def _(pool):
                chain = Chain(pool, w.chains["pool"])

                def turn(t, s, exists):
                    if s == 0:
                        chain.restart_always()
                    if exists(2):
                        layernorm_rstd(pool, w, chain, t + 2, s)
                    if exists(1):
                        if exists(-1):
                            pool.wait_ge(x_updated.sem, x_updated.count(t - 1))
                        pool.tensor_tensor(x_bias[:, 1 - s, :], w.x_res[:, t + 1, :], bias[:, :],
                                           ALU.add).then_inc(x_biased.sem, 1)

                turns(pool, turn)
                chain.restart_always()

            @block.vector
            def _(dve):
                chain = Chain(dve, w.chains["dve"])
                low = -128.0 if per_token else -127.0

                def quantise(u, s):
                    chain.link(layernorm_apply(dve, w, xn[:, s, :], u, s))
                    inverse = w_scale[:, 1:2]
                    if per_token:
                        chain.link(dve.tensor_reduce(x_scale[:, s:s + 1], xn[:, s, :], AX.X, ALU.max,
                                                     apply_absolute_value=True))
                        chain.link(dve.tensor_scalar(x_scale[:, s:s + 1], x_scale[:, s:s + 1], 1e-8,
                                                     1.0 / 127.0, ALU.max, ALU.mult))
                        chain.link(dve.reciprocal(x_inv[:, s:s + 1], x_scale[:, s:s + 1]))
                        inverse = x_inv[:, s:s + 1]
                    chain.link(dve.tensor_scalar(xn[:, s, :], xn[:, s, :], inverse, ROUND, ALU.mult, ALU.add))
                    chain.link(dve.tensor_scalar(xn[:, s, :], xn[:, s, :], ROUND, low, ALU.subtract, ALU.max))
                    dve.tensor_scalar(x_q[:, s, :], xn[:, s, :], 127.0, None, ALU.min).then_inc(xn_ready.sem, 1)

                def turn(t, s, exists):
                    if s == 0:
                        chain.restart_always()
                    if exists(2):
                        layernorm_stats(dve, w, chain, t + 2, s)
                    if exists(1):
                        quantise(t + 1, 1 - s)
                    if exists(0):
                        y = w.lane(s)[:, 1, 0:D]
                        dve.wait_ge(out_psum.sem, out_psum.count(t))
                        dve.wait_ge(x_biased.sem, x_biased.count(t))
                        if per_token:
                            chain.link(dve.scalar_tensor_tensor(scaled[:, s, :], y, x_scale[:, s:s + 1],
                                                                w_scale[:, :], ALU.mult, ALU.mult))
                            dve.tensor_tensor(w.x_res[:, t, :], scaled[:, s, :], x_bias[:, s, :],
                                              ALU.add).then_inc(x_updated.sem, 1)
                        else:
                            dve.scalar_tensor_tensor(w.x_res[:, t, :], y, w_scale[:, 0:1], x_bias[:, s, :],
                                                     ALU.mult, ALU.add).then_inc(x_updated.sem, 1)

                turns(dve, turn)
                chain.restart_always()

            @block.scalar
            def _(act):
                def turn(t, s, exists):
                    if exists(1):
                        act.wait_ge(xn_t_psum.sem, xn_t_psum.count(t + 1))
                        act.activation(x_qt[:, 1 - s, :, :], w.lane(1 - s)[:, 0, 0:P].bitcast(BF16)
                                       .rearrange("p (k t) -> p k t", t=P), ACT.Copy).then_inc(xn_t_ready.sem, 1)

                turns(act, turn)

            @block.tensor
            def _(pe):
                def turn(t, s, exists):
                    if exists(1):
                        pe.wait_ge(xn_ready.sem, xn_ready.count(t + 1))
                        transpose_tile(pe, w, x_q[:, 1 - s, :], w.lane(1 - s)[:, 0, 0:P].bitcast(BF16),
                                       w.ident16[:, :]).then_inc(xn_t_psum.sem, 1)
                        if exists(-1):
                            pe.wait_ge(x_updated.sem, x_updated.count(t - 1))
                        pe.wait_ge(xn_t_ready.sem, xn_t_ready.count(t + 1))
                        for k in range(DK):
                            last = pe.matmul(w.lane(1 - s)[:, 1, 0:D], x_qt[:, 1 - s, k, :], w_t[:, k, :],
                                             start=(k == 0), stop=(k == DK - 1))
                        last.then_inc(out_psum.sem, 1)

                turns(pe, turn)

        w.advance(**{name: TILES for name in (
            "stats_ready", "rstd_ready", "xn_ready", "xn_t_psum", "xn_t_ready", "out_psum",
            "x_updated", "x_biased")})
    return stage


def prepare_int8(nc, w, sb, w_t, w_scale, bias):
    weight = sb("weight", [P, DK, D])
    amax = sb("amax", [P, DK])
    inverse = sb("inverse", [P, DK])
    w_q = sb("w_q", [P, DK, D], BF16)
    diag = sb("diag", [P, DK, P])
    loaded, quantised, turned = w.counter("weights_loaded"), w.counter("w_quantised"), w.counter("w_turned")
    all_loaded = loaded.base + 32
    with nc.Block() as block:
        @block.sync
        def _(sp):
            sp.dma_start(weight[:, :, :], w.io["L0_ffn_weight"].rearrange("(m p) n -> p m n", p=P)
                         ).then_inc(loaded.sem, 16)
            sp.dma_start(bias[:, :], w.io["L0_ffn_bias"].partition_broadcast(P)).then_inc(loaded.sem, 16)
            sp.wait_ge(loaded.sem, all_loaded)

        @block.vector
        def _(dve):
            chain = Chain(dve, w.chains["dve"])
            dve.wait_ge(loaded.sem, all_loaded)
            chain.link(dve.tensor_reduce(amax[:, :], weight[:, :, :], AX.X, ALU.max,
                                         apply_absolute_value=True))
            chain.link(dve.tensor_scalar(amax[:, :], amax[:, :], 1e-8, 1.0 / 127.0, ALU.max, ALU.mult))
            chain.link(dve.reciprocal(inverse[:, :], amax[:, :]))
            for m in range(DK):
                chain.link(dve.tensor_scalar(weight[:, m, :], weight[:, m, :], inverse[:, m:m + 1], ROUND,
                                             ALU.mult, ALU.add))
                chain.link(dve.tensor_scalar(weight[:, m, :], weight[:, m, :], ROUND, -128.0,
                                             ALU.subtract, ALU.max))
                chain.link(dve.tensor_scalar(w_q[:, m, :], weight[:, m, :], 127.0, None, ALU.min))
                chain.link(dve.tensor_scalar(diag[:, m, :], w.ident[:, :], amax[:, m:m + 1], None, ALU.mult))
            dve.engine_nop().then_inc(quantised.sem, 1)
            dve.wait_ge(turned.sem, turned.count(0))
            dve.tensor_copy(w_t[:, :, :], w.psum[:, 0, 0:D].bitcast(BF16).rearrange("p (k m) -> p k m", k=DK))
            dve.tensor_copy(w_scale[:, :], w.psum[:, 1, 0:D])
            chain.link(dve.engine_nop())
            chain.restart()

        @block.tensor
        def _(pe):
            pe.wait_ge(quantised.sem, quantised.count(0))
            weights_t = w.psum[:, 0, 0:D].bitcast(BF16).rearrange("p (k m) -> p k m", k=DK)
            for m in range(DK):
                for k in range(DK):
                    pe.transpose(weights_t[:, k, m * P:(m + 1) * P], w_q[:, m, k * P:(k + 1) * P],
                                 w.ident16[:, :])
            for m in range(DK):
                last = pe.matmul(w.psum[:, 1, m * P:(m + 1) * P], w.ones[:, :], diag[:, m, :],
                                 start=True, stop=True)
            last.then_inc(turned.sem, 1)
    loaded.base = all_loaded
    w.advance(w_quantised=1, w_turned=1)


def prepare_ternary(nc, w, sb, w_t, w_scale, bias):
    weight = sb("weight", [P, DK, D], I32)
    loaded = w.counter("weights_loaded")
    all_loaded = loaded.base + 48
    with nc.Block() as block:
        @block.sync
        def _(sp):
            sp.dma_start(weight[:, :, :], w.io["ternary_t"].rearrange("(k p) n -> p k n", p=P)
                         ).then_inc(loaded.sem, 16)
            sp.dma_start(bias[:, :], w.io["L2_ffn_bias"].partition_broadcast(P)).then_inc(loaded.sem, 16)
            sp.dma_start(w_scale[:, 0:1], w.io["act_scale"].partition_broadcast(P)).then_inc(loaded.sem, 16)
            sp.wait_ge(loaded.sem, all_loaded)

        @block.vector
        def _(dve):
            chain = Chain(dve, w.chains["dve"])
            dve.wait_ge(loaded.sem, all_loaded)
            chain.link(dve.tensor_scalar(w_scale[:, 0:1], w_scale[:, 0:1], 1e-5, None, ALU.max))
            chain.link(dve.reciprocal(w_scale[:, 1:2], w_scale[:, 0:1]))
            chain.link(dve.tensor_scalar(w_t[:, :, :], weight[:, :, :], -1.0, None, ALU.add))
            chain.restart()
    loaded.base = all_loaded



EXPERTS = 16
PAIRS = EXPERTS // 2


def experts_stage(nc, w, ctx):
    io = w.io

    def sb(name, shape, dt=F32):
        return ctx.enter_context(nc.sbuf_tensor(f"moe_{name}", shape, dt))

    gate = sb("gate", [P, DK, EXPERTS])
    we = sb("we", [P, DK, EXPERTS, D])
    we_high = sb("we_high", [P, DK, EXPERTS, D], F32R)
    we_low = sb("we_low", [P, DK, EXPERTS, D], F32R)
    be = sb("be", [2, EXPERTS, D])
    be_high = sb("be_high", [2, EXPERTS, D], F32R)
    be_parts = sb("be_parts", [2, EXPERTS, D], F32R)
    ones_r = sb("ones_r", [2, P], F32R)
    is_low = sb("is_low", [2, 1])
    iota = sb("iota", [P, EXPERTS])
    xn = sb("xn", [P, LANES, D])
    xn_t = sb("xn_t", [P, LANES, DK, P])
    xn_high = sb("xn_high", [P, LANES, DK, P], F32R)
    xn_low = sb("xn_low", [P, LANES, DK, P], F32R)
    top = sb("top", [P, LANES])
    e = sb("e", [P, LANES, EXPERTS])
    total = sb("total", [P, LANES])
    best = sb("best", [P, LANES, 8])
    best_at = sb("best_at", [P, LANES, 8], U32)
    at = sb("at", [P, LANES, 2])
    pick = sb("pick", [P, LANES, 2, EXPERTS])
    weight = sb("weight", [P, LANES, EXPERTS])
    RING = 3
    gated = sb("gated", [P, RING, 2, D])
    CUTS = 4
    EC = EXPERTS // CUTS

    sig = w.counter
    loaded = sig("weights_loaded")
    few_loaded = loaded.base + 16 * 4
    cut_loaded = [sig(f"cut{c}_loaded") for c in range(CUTS)]
    high_ready, low_ready = sig("we_high_ready"), sig("we_low_ready")
    bias_ready = sig("expert_bias_ready")
    xn_ready, xn_t_psum, xn_t_ready = sig("xn_ready"), sig("xn_t_psum"), sig("xn_t_ready")
    parts_ready = sig("xn_parts_ready")
    gate_psum, shifted, exped = sig("scores_psum"), sig("shifted"), sig("exped")
    weights_ready = sig("inverse_ready")
    expert_psum, gated_ready, gated_used = sig("expert_psum"), sig("gated_ready"), sig("gated_used")

    STATS_AT, NORM_AT, TURN_AT, GATE_AT, SHIFT_AT, EXP_AT, PICK_AT = 0, 0, 2, 3, 3, 4, 4

    with nc.Block() as block:
        @block.sync
        def _(sp):
            sp.dma_start(gate[:, :, :], io["gate_t"].rearrange("(k p) e -> p k e", p=P)).then_inc(loaded.sem, 16)
            sp.dma_start(iota[:, :], io["iota"][0:EXPERTS].partition_broadcast(P)).then_inc(loaded.sem, 16)
            for row in range(2):
                sp.dma_start(be[row:row + 1, :, :], io["L1_ffn_expert_b"].rearrange("(a e) n -> a e n", a=1)
                             ).then_inc(loaded.sem, 16)
            for c in range(CUTS):
                for k in range(DK):
                    sp.dma_start(we[:, k, c * EC:(c + 1) * EC, :],
                                 io["expert_t"][k * P:(k + 1) * P, c * EC:(c + 1) * EC, :]
                                 ).then_inc(cut_loaded[c].sem, 16)

        @block.gpsimd
        def _(pool):
            chain = Chain(pool, w.chains["pool"])

            def prepare(u, s):
                layernorm_rstd(pool, w, chain, u, s)
                pool.wait_ge(xn_t_ready.sem, xn_t_ready.count(u))
                pool.tensor_tensor(xn_low[:, s, :, :], xn_t[:, s, :, :], xn_high[:, s, :, :].bitcast(F32),
                                   ALU.subtract).then_inc(parts_ready.sem, 1)

            prepare(0, 0)
            with pool.Fori(0, B) as i:
                chain.restart_always()
                for s in range(LANES):
                    prepare(i * LANES + s + 1, 1 - s)
            chain.restart_always()

        @block.vector
        def _(dve):
            chain = Chain(dve, w.chains["dve"])
            dve.wait_ge(loaded.sem, few_loaded)

            def shift(u, s):
                logits = w.lane(s)[:, 0, 0:EXPERTS]
                dve.wait_ge(gate_psum.sem, gate_psum.count(u))
                chain.link(dve.tensor_reduce(top[:, s:s + 1], logits, AX.X, ALU.max))
                dve.tensor_scalar(e[:, s, :], logits, top[:, s:s + 1], None, ALU.subtract
                                  ).then_inc(shifted.sem, 1)

            def pick_two(u, s):
                dve.wait_ge(exped.sem, exped.count(u))
                chain.link(dve.tensor_reduce(total[:, s:s + 1], e[:, s, :], AX.X, ALU.add))
                chain.link(dve.reciprocal(total[:, s:s + 1], total[:, s:s + 1]))
                chain.link(dve.max(best[:, s, :], e[:, s, :]))
                chain.link(dve.max_index(best_at[:, s, :], best[:, s, :], e[:, s, :]))
                chain.link(dve.tensor_copy(at[:, s, :], best_at[:, s, 0:2]))
                for n in range(2):
                    chain.link(dve.tensor_scalar(pick[:, s, n, :], iota[:, :], at[:, s, n:n + 1],
                                                 best[:, s, n:n + 1], ALU.is_equal, ALU.mult))
                chain.link(dve.tensor_tensor(weight[:, s, :], pick[:, s, 0, :], pick[:, s, 1, :], ALU.add))
                dve.tensor_scalar(weight[:, s, :], weight[:, s, :], total[:, s:s + 1], None,
                                  ALU.mult).then_inc(weights_ready.sem, 1)

            def add_pair(u, s, p):
                n = u * PAIRS + p
                if p > 0:
                    dve.wait_ge(gated_used.sem, gated_used.count(n - 1))
                dve.wait_ge(gated_ready.sem, gated_ready.count(n))
                slot = (s * PAIRS + p) % RING
                chain.link(dve.tensor_tensor(w.x_res[:, u, :], w.x_res[:, u, :], gated[:, slot, 0, :], ALU.add))
                dve.tensor_tensor(w.x_res[:, u, :], w.x_res[:, u, :], gated[:, slot, 1, :],
                                  ALU.add).then_inc(gated_used.sem, 1)

            layernorm_stats(dve, w, chain, 0, 0)
            dve.tensor_scalar(is_low[:, :], w.ident[0:2, 1:2], -1.0, None, ALU.mult)
            dve.tensor_copy(ones_r[:, :], w.ones[0:2, :])
            chain.link(dve.tensor_copy(be_high[:, :, :], be[:, :, :]))
            dve.scalar_tensor_tensor(be_parts[:, :, :], be_high[:, :, :].bitcast(F32), is_low[:, :], be[:, :, :],
                                     ALU.mult, ALU.add).then_inc(bias_ready.sem, 1)
            layernorm_apply(dve, w, xn[:, 0, :], 0, 0).then_inc(xn_ready.sem, 1)
            shift(0, 0)
            for c in range(CUTS):
                dve.wait_ge(high_ready.sem, high_ready.count(c))
                part = (slice(None), slice(None), slice(c * EC, (c + 1) * EC), slice(None))
                dve.tensor_tensor(we_low[part], we[part], we_high[part].bitcast(F32), ALU.subtract
                                  ).then_inc(low_ready.sem, 1)
            pick_two(0, 0)
            chain.restart_always()
            with dve.Fori(0, B) as i:
                chain.restart_always()
                for s in range(LANES):
                    u = i * LANES + s
                    for p in range(PAIRS):
                        add_pair(u, s, p)
                        if p == STATS_AT:
                            layernorm_stats(dve, w, chain, u + 1, 1 - s)
                        if p == NORM_AT:
                            layernorm_apply(dve, w, xn[:, 1 - s, :], u + 1, 1 - s).then_inc(xn_ready.sem, 1)
                        if p == SHIFT_AT:
                            shift(u + 1, 1 - s)
                        if p == PICK_AT:
                            pick_two(u + 1, 1 - s)
            chain.restart_always()

        @block.scalar
        def _(act):
            def turned(u, s):
                act.wait_ge(xn_t_psum.sem, xn_t_psum.count(u))
                turned_xn = w.lane(s)[:, 0, 0:D].rearrange("p (k t) -> p k t", t=P)
                act.activation(xn_t[:, s, :, :], turned_xn, ACT.Copy)
                act.activation(xn_high[:, s, :, :], turned_xn, ACT.Copy).then_inc(xn_t_ready.sem, 1)

            def exponential(u, s):
                act.wait_ge(shifted.sem, shifted.count(u))
                act.activation(e[:, s, :], e[:, s, :], ACT.Exp).then_inc(exped.sem, 1)

            def gate_pair(u, s, p):
                n = u * PAIRS + p
                local = s * PAIRS + p
                act.wait_ge(expert_psum.sem, expert_psum.count(n))
                back = RING if local >= RING else local % RING + 1
                act.wait_ge(gated_used.sem, gated_used.count(n - back))
                for h in range(2):
                    x = 2 * p + h
                    last = act.activation(gated[:, local % RING, h, :],
                                          w.lane(s)[:, 1 + p % 3, h * D:(h + 1) * D], ACT.Relu,
                                          scale=weight[:, s, x:x + 1])
                last.then_inc(gated_ready.sem, 1)

            turned(0, 0)
            for c in range(CUTS):
                act.wait_ge(cut_loaded[c].sem, 16 * DK)
                part = (slice(None), slice(None), slice(c * EC, (c + 1) * EC), slice(None))
                act.activation(we_high[part], we[part], ACT.Copy).then_inc(high_ready.sem, 1)
            exponential(0, 0)
            with act.Fori(0, B) as i:
                for s in range(LANES):
                    u = i * LANES + s
                    act.wait_ge(weights_ready.sem, weights_ready.count(u))
                    for p in range(PAIRS):
                        gate_pair(u, s, p)
                        if p == TURN_AT:
                            turned(u + 1, 1 - s)
                        if p == EXP_AT:
                            exponential(u + 1, 1 - s)

        @block.tensor
        def _(pe):
            def normalised(u, s):
                pe.wait_ge(xn_ready.sem, xn_ready.count(u))
                transpose_tile(pe, w, xn[:, s, :], w.lane(s)[:, 0, :], w.ident[:, :]).then_inc(xn_t_psum.sem, 1)

            def logits(u, s):
                pe.wait_ge(xn_t_ready.sem, xn_t_ready.count(u))
                for k in range(DK):
                    last = pe.matmul(w.lane(s)[:, 0, 0:EXPERTS], xn_t[:, s, k, :], gate[:, k, :],
                                     start=(k == 0), stop=(k == DK - 1))
                last.then_inc(gate_psum.sem, 1)

            normalised(0, 0)
            pe.wait_ge(loaded.sem, few_loaded)
            logits(0, 0)
            pe.wait_ge(bias_ready.sem, bias_ready.count(0))
            pe.wait_ge(high_ready.sem, high_ready.count(CUTS - 1))
            pe.wait_ge(low_ready.sem, low_ready.count(CUTS - 1))
            with pe.Fori(0, B) as i:
                for s in range(LANES):
                    u = i * LANES + s
                    pe.wait_ge(parts_ready.sem, parts_ready.count(u))
                    for p in range(PAIRS):
                        bank = w.lane(s)[:, 1 + p % 3, :]
                        if p >= 3:
                            pe.wait_ge(gated_ready.sem, gated_ready.count(u * PAIRS + p - 3))
                        pe.matmul(bank, ones_r[:, :], be_parts[:, 2 * p:2 * p + 2, :], start=True, stop=False)
                        for k in range(DK):
                            pair = (slice(None), k, slice(2 * p, 2 * p + 2), slice(None))
                            pe.matmul(bank, xn_low[:, s, k, :], we_high[pair], start=False, stop=False)
                            pe.matmul(bank, xn_high[:, s, k, :], we_low[pair], start=False, stop=False)
                            last = pe.matmul(bank, xn_high[:, s, k, :], we_high[pair], start=False,
                                             stop=(k == DK - 1))
                        last.then_inc(expert_psum.sem, 1)
                        if p == TURN_AT:
                            normalised(u + 1, 1 - s)
                        if p == GATE_AT:
                            logits(u + 1, 1 - s)

    loaded.base = few_loaded
    w.advance(**{name: TILES + 1 for name in (
        "stats_ready", "rstd_ready", "xn_ready", "xn_t_psum", "xn_t_ready", "xn_parts_ready", "scores_psum",
        "shifted", "exped", "inverse_ready")})
    w.advance(expert_psum=TILES * PAIRS, gated_ready=TILES * PAIRS, gated_used=TILES * PAIRS,
              we_high_ready=CUTS, we_low_ready=CUTS, expert_bias_ready=1)



def global_attention_stage(nc, w, ctx):
    heads, dim = 8, 128
    inner = heads * dim
    scale = 1.5 * float(dim) ** -0.5
    chunk = 4 * NCTX
    chunks = B // 4
    TURN = 4
    NORM_AT, TURN_AT, QUERY_AT = 2, 3, 5
    io = w.io

    def sb(name, shape, dt=F32):
        return ctx.enter_context(nc.sbuf_tensor(f"global_{name}", shape, dt))

    KEYS = B * NCTX
    KT = KEYS // P
    k_t = sb("k_t", [P, heads, KEYS])
    v = sb("v", [P, KT, inner])
    sig = w.counter
    loaded, projected, copied = sig("weights_loaded"), sig("kv_ready"), sig("kv_copied")

    with ExitStack() as once, nc.Block() as block:
        wk = once.enter_context(nc.sbuf_tensor("global_wk", [CP, 2, inner], F32))
        wv = once.enter_context(nc.sbuf_tensor("global_wv", [CP, 2, inner], F32))
        ctx_t = once.enter_context(nc.sbuf_tensor("global_ctx_t", [CP, 2, KEYS], F32))
        all_loaded = loaded.base + 48
        groups = [("k", h, c) for h in range(heads) for c in range(chunks)]
        groups += [("v", t, c) for t in range(KT) for c in range(inner // 512)]

        @block.sync
        def _(sp):
            for dst, src in ((wk[:, :, :], io["L2_xattn_Wk"].rearrange("(k p) n -> p k n", p=CP)),
                             (ctx_t[:, :, :], io["ctx_t"].rearrange("(k p) b j -> p k (b j)", p=CP)),
                             (wv[:, :, :], io["L2_xattn_Wv"].rearrange("(k p) n -> p k n", p=CP))):
                sp.dma_start(dst, src).then_inc(loaded.sem, 16)

        @block.tensor
        def _(pe):
            pe.wait_ge(loaded.sem, all_loaded)
            for n, (what, a, c) in enumerate(groups):
                if n >= 8:
                    used = sig("kv_copied2") if n % 2 else copied
                    pe.wait_ge(used.sem, used.count((n - 8) // 2))
                for k in range(2):
                    if what == "k":
                        last = pe.matmul(w.psum[:, n % 8, 0:chunk], wk[:, k, a * dim:(a + 1) * dim],
                                         ctx_t[:, k, c * chunk:(c + 1) * chunk], start=(k == 0), stop=(k == 1))
                    else:
                        last = pe.matmul(w.psum[:, n % 8, :], ctx_t[:, k, a * P:(a + 1) * P],
                                         wv[:, k, c * 512:(c + 1) * 512], start=(k == 0), stop=(k == 1))
                last.then_inc(projected.sem, 1)

        def place(n):
            what, a, c = groups[n]
            if what == "k":
                return k_t[:, a, c * chunk:(c + 1) * chunk], w.psum[:, n % 8, 0:chunk]
            return v[:, a, c * 512:(c + 1) * 512], w.psum[:, n % 8, :]

        @block.vector
        def _(dve):
            for n in range(0, len(groups), 2):
                dve.wait_ge(projected.sem, projected.count(n))
                dve.tensor_copy(*place(n)).then_inc(copied.sem, 1)

        @block.scalar
        def _(act):
            for n in range(1, len(groups), 2):
                act.wait_ge(projected.sem, projected.count(n))
                act.activation(*place(n), ACT.Copy).then_inc(sig("kv_copied2").sem, 1)
    loaded.base = all_loaded
    w.advance(kv_ready=len(groups), kv_copied=(len(groups) + 1) // 2, kv_copied2=len(groups) // 2)

    wq = sb("wq", [P, DK, inner])
    wo = sb("wo", [P, heads, D])
    xn = sb("xn", [P, D])
    xn_t = sb("xn_t", [P, DK, P])
    q_t = sb("q_t", [P, heads, P])
    top = sb("top", [P, chunks])
    bias = sb("bias", [P, 2])
    part_sum = sb("part_sum", [P, heads, chunks])
    inverse = sb("inverse", [P, 2])
    prob = sb("prob", [P, 2, KEYS])
    prob_t = sb("prob_t", [P, 2, TURN, P])
    attn_t = sb("attn_t", [P, 2, P])
    all_loaded = loaded.base + 32

    turns = [list(range(t * TURN, min((t + 1) * TURN, KT))) for t in range(chunks)]

    xn_ready, xn_t_psum, xn_t_ready = sig("xn_ready"), sig("xn_t_psum"), sig("xn_t_ready")
    q_psum, q_ready = sig("q_psum"), sig("q_ready")
    scores_psum, bias_ready, exped = sig("scores_psum"), sig("shifted"), sig("exped")
    prob_t_psum, even_ready, odd_ready = sig("prob_t_psum"), sig("prob_t_ready"), sig("prob_t_ready2")
    attn_psum, attn_ready = sig("attn_psum"), sig("attn_ready")
    out_psum, x_updated = sig("out_psum"), sig("x_updated")


    with nc.Block() as block:
        @block.sync
        def _(sp):
            for dst, src in ((wq[:, :, :], io["L2_xattn_Wq"].rearrange("(k p) n -> p k n", p=P)),
                             (wo[:, :, :], io["L2_xattn_Wout"].rearrange("(h p) n -> p h n", p=P))):
                sp.dma_start(dst, src).then_inc(loaded.sem, 16)

        @block.gpsimd
        def _(pool):
            chain = Chain(pool, w.chains["pool"])
            with pool.Fori(0, TILES + 1) as u:
                chain.restart_always()
                layernorm_rstd(pool, w, chain, u, 0)
            chain.restart_always()

        @block.vector
        def _(dve):
            chain = Chain(dve, w.chains["dve"])
            dve.wait_ge(loaded.sem, all_loaded)

            def maximum(n, h):
                for c in range(chunks):
                    dve.wait_ge(scores_psum.sem, scores_psum.count(n * chunks + c))
                    ins = dve.tensor_reduce(top[:, c:c + 1], w.psum[:, c, 0:chunk], AX.X, ALU.max)
                chain.link(ins)
                chain.link(dve.tensor_reduce(bias[:, h % 2:h % 2 + 1], top[:, :], AX.X, ALU.max))
                dve.tensor_scalar(bias[:, h % 2:h % 2 + 1], bias[:, h % 2:h % 2 + 1], -scale, None,
                                  ALU.mult).then_inc(bias_ready.sem, 1)

            def turn(n, t):
                dve.wait_ge(prob_t_psum.sem, prob_t_psum.count(n * chunks + t))
                size = len(turns[t])
                dve.tensor_copy(prob_t[:, t % 2, 0:size, :],
                                w.psum[:, 4 + t % 2, 0:size * P].rearrange("p (k t) -> p k t", t=P)
                                ).then_inc((odd_ready if t % 2 else even_ready).sem, 1)

            def output(u, h):
                n = u * heads + h
                chain.link(dve.tensor_reduce(inverse[:, h % 2:h % 2 + 1], part_sum[:, h, :], AX.X, ALU.add))
                chain.link(dve.reciprocal(inverse[:, h % 2:h % 2 + 1], inverse[:, h % 2:h % 2 + 1]))
                if h > 0:
                    dve.wait_ge(x_updated.sem, x_updated.count(n - 1))
                dve.wait_ge(out_psum.sem, out_psum.count(n))
                dve.scalar_tensor_tensor(w.x_res[:, u, :], w.psum[:, 7, 0:D], inverse[:, h % 2:h % 2 + 1],
                                         w.x_res[:, u, :], ALU.mult, ALU.add).then_inc(x_updated.sem, 1)

            def queries(u, c):
                dve.wait_ge(q_psum.sem, q_psum.count(2 * u + c))
                dve.tensor_copy(q_t[:, 4 * c:4 * c + 4, :],
                                w.psum[:, 4, :].rearrange("p (k t) -> p k t", t=P)).then_inc(q_ready.sem, 1)

            def normalise(u):
                layernorm_stats(dve, w, chain, u, 0)
                layernorm_apply(dve, w, xn[:, :], u, 0).then_inc(xn_ready.sem, 1)

            chain.restart_always()
            normalise(0)
            queries(0, 0)
            queries(0, 1)
            maximum(0, 0)
            with dve.Fori(0, TILES) as u:
                for h in range(heads):
                    n = u * heads + h
                    if h == 0:
                        chain.restart_always()
                    turn(n, 0)
                    maximum(n + 1, h + 1)
                    if h == NORM_AT:
                        normalise(u + 1)
                    if h > 0:
                        output(u, h - 1)
                    turn(n, 2)
                    turn(n, 3)
                    if h == QUERY_AT:
                        queries(u + 1, 0)
                    if h == heads - 1:
                        queries(u + 1, 1)
                output(u, heads - 1)
            chain.restart_always()

        @block.scalar
        def _(act):
            act.wait_ge(loaded.sem, all_loaded)

            def exponential(n, h):
                act.wait_ge(bias_ready.sem, bias_ready.count(n))
                for c in range(chunks):
                    act.activation(prob[:, h % 2, c * chunk:(c + 1) * chunk], w.psum[:, c, 0:chunk], ACT.Exp,
                                   bias=bias[:, h % 2:h % 2 + 1], scale=scale,
                                   accum_out=part_sum[:, h % heads, c:c + 1]).then_inc(exped.sem, 1)

            def normalised(u):
                act.wait_ge(xn_t_psum.sem, xn_t_psum.count(u))
                act.activation(xn_t[:, :, :], w.psum[:, 4, 0:D].rearrange("p (k t) -> p k t", t=P),
                               ACT.Copy).then_inc(xn_t_ready.sem, 1)

            normalised(0)
            exponential(0, 0)
            with act.Fori(0, TILES) as u:
                for h in range(heads):
                    n = u * heads + h
                    act.wait_ge(prob_t_psum.sem, prob_t_psum.count(n * chunks + 1))
                    act.activation(prob_t[:, 1, :, :], w.psum[:, 5, :].rearrange("p (k t) -> p k t", t=P),
                                   ACT.Copy).then_inc(odd_ready.sem, 1)
                    exponential(n + 1, h + 1)
                    if h == TURN_AT:
                        normalised(u + 1)
                    act.wait_ge(attn_psum.sem, attn_psum.count(n))
                    act.activation(attn_t[:, h % 2, :], w.psum[:, 6, 0:P], ACT.Copy).then_inc(attn_ready.sem, 1)

        @block.tensor
        def _(pe):
            pe.wait_ge(loaded.sem, all_loaded)

            def scores(n, h, first=False):
                for c in range(chunks):
                    if not first:
                        pe.wait_ge(exped.sem, exped.count((n - 1) * chunks + c))
                    pe.matmul(w.psum[:, c, 0:chunk], q_t[:, h, :], k_t[:, h, c * chunk:(c + 1) * chunk],
                              start=True, stop=True).then_inc(scores_psum.sem, 1)

            def turn(n, h, t):
                if t == 0:
                    pe.wait_ge(exped.sem, exped.count(n * chunks + chunks - 1))
                ready = odd_ready if t % 2 else even_ready
                pe.wait_ge(ready.sem, ready.count(n * 2 + t // 2 - 1))
                for j, kt in enumerate(turns[t]):
                    last = pe.transpose(w.psum[:, 4 + t % 2, j * P:(j + 1) * P],
                                        prob[:, h % 2, kt * P:(kt + 1) * P], w.ident[:, :])
                last.then_inc(prob_t_psum.sem, 1)

            def weigh(n, h, t):
                if t == 0:
                    pe.wait_ge(attn_ready.sem, attn_ready.count(n - 1))
                ready = odd_ready if t % 2 else even_ready
                pe.wait_ge(ready.sem, ready.count(n * 2 + t // 2))
                for j, kt in enumerate(turns[t]):
                    last = pe.matmul(w.psum[:, 6, 0:P], v[:, kt, h * dim:(h + 1) * dim], prob_t[:, t % 2, j, :],
                                     start=(kt == 0), stop=(kt == KT - 1))
                if t == chunks - 1:
                    last.then_inc(attn_psum.sem, 1)

            def output(u, h):
                n = u * heads + h
                pe.wait_ge(attn_ready.sem, attn_ready.count(n))
                pe.wait_ge(x_updated.sem, x_updated.count(n - 1))
                pe.matmul(w.psum[:, 7, 0:D], attn_t[:, h % 2, :], wo[:, h, :], start=True,
                          stop=True).then_inc(out_psum.sem, 1)

            def normalised(u):
                pe.wait_ge(xn_ready.sem, xn_ready.count(u))
                transpose_tile(pe, w, xn[:, :], w.psum[:, 4, :], w.ident[:, :]).then_inc(xn_t_psum.sem, 1)

            def queries(u, c):
                pe.wait_ge(xn_t_ready.sem, xn_t_ready.count(u))
                if c == 1:
                    pe.wait_ge(q_ready.sem, q_ready.count(2 * u))
                for m in range(4):
                    h = 4 * c + m
                    for k in range(DK):
                        last = pe.matmul(w.psum[:, 4, m * P:(m + 1) * P], wq[:, k, h * dim:(h + 1) * dim],
                                         xn_t[:, k, :], start=(k == 0), stop=(k == DK - 1))
                last.then_inc(q_psum.sem, 1)

            normalised(0)
            queries(0, 0)
            queries(0, 1)
            pe.wait_ge(q_ready.sem, q_ready.count(1))
            scores(0, 0, first=True)
            with pe.Fori(0, TILES) as u:
                for h in range(heads):
                    n = u * heads + h
                    if h == TURN_AT + 1:
                        pe.wait_ge(xn_t_ready.sem, xn_t_ready.count(u + 1))
                    if h == QUERY_AT + 1:
                        pe.wait_ge(q_ready.sem, q_ready.count(2 * (u + 1)))
                    if h == 0:
                        pe.wait_ge(q_ready.sem, q_ready.count(2 * u + 1))
                    turn(n, h, 0)
                    turn(n, h, 1)
                    scores(n + 1, (h + 1) % heads)
                    weigh(n, h, 0)
                    if h > 0:
                        output(u, h - 1)
                    turn(n, h, 2)
                    weigh(n, h, 1)
                    turn(n, h, 3)
                    weigh(n, h, 2)
                    if h == TURN_AT:
                        normalised(u + 1)
                    if h == QUERY_AT:
                        queries(u + 1, 0)
                    if h == heads - 1:
                        queries(u + 1, 1)
                    weigh(n, h, 3)
                output(u, heads - 1)

    loaded.base = all_loaded
    n_heads = TILES * heads
    w.advance(**{name: TILES + 1 for name in ("stats_ready", "rstd_ready", "xn_ready", "xn_t_psum", "xn_t_ready")})
    w.advance(q_psum=2 * TILES + 2, q_ready=2 * TILES + 2, shifted=n_heads + 1)
    w.advance(scores_psum=(n_heads + 1) * chunks, exped=(n_heads + 1) * chunks)
    w.advance(**{name: n_heads for name in ("attn_psum", "attn_ready", "out_psum", "x_updated")})
    w.advance(prob_t_psum=n_heads * chunks, prob_t_ready=n_heads * 2, prob_t_ready2=n_heads * 2)

    bout = sb("bout", [P, D])
    with nc.Block() as block:
        @block.sync
        def _(sp):
            sp.dma_start(bout[:, :], io["L2_xattn_bout"].partition_broadcast(P)).then_inc(loaded.sem, 16)

        @block.vector
        def _(dve):
            dve.wait_ge(loaded.sem, loaded.base + 16)
            dve.tensor_tensor(w.x_res[:, 0:TILES, :], w.x_res[:, 0:TILES, :],
                              bout[:, :].unsqueeze(1).to_broadcast([P, TILES, D]), ALU.add)
    loaded.base += 16



N_STATE = 64
SEQ_A, SEQ_B = 16, 16
FREQ = 2 * S
GROUP = P // SEQ_A
TWO_PI = 6.283185


def spectral_kernel(nc, w, ctx):
    io = w.io

    def keep(name, shape):
        return ctx.enter_context(nc.sbuf_tensor(f"ssm_{name}", shape, F32))

    by_cos, by_sin, by_last = (keep(n, [P, DK, D]) for n in ("by_cos", "by_sin", "by_last"))
    sig = w.counter
    loaded, gathered = sig("weights_loaded"), sig("lags_gathered")
    made, turned, spectra = sig("states_made"), sig("states_tanh"), sig("spectra_psum")
    lag_psum, lag_copied = sig("lag_psum"), sig("lag_copied")
    dve_done, act_done = sig("ssm_dve"), sig("ssm_act")

    with ExitStack() as once, nc.Block() as block:
        def sb(name, shape):
            return once.enter_context(nc.sbuf_tensor(f"ssm_{name}", shape, F32))

        a_re, a_im, c_re, c_im, log_dt = (sb(n, [P, D]) for n in ("a_re", "a_im", "c_re", "c_im", "log_dt"))
        phase = sb("phase", [P, 4])
        steps = sb("steps", [P, 2, SEQ_A])
        transform = sb("transform", [SEQ_A, SEQ_B, 5 * P])
        r, turn, tan, cos, sin, half = (sb(n, [P, D]) for n in ("r", "turn", "tan", "cos", "sin", "half"))
        e_re, e_im, n_re, n_im, t1, t2 = (sb(n, [P, D]) for n in ("e_re", "e_im", "n_re", "n_im", "t1", "t2"))
        angle = sb("angle", [P, 3, D])
        whole = sb("whole", [P, 3, D])
        big = [sb(f"big{n}", [P, D, SEQ_A]) for n in range(5)]
        lags = sb("lags", [SEQ_A, GROUP, D // GROUP, SEQ_B])
        n_loads = 12
        all_loaded = loaded.base + 16 * n_loads

        @block.sync
        def _(sp):
            for dst, name in ((a_re, "a_re_t"), (a_im, "a_im_t"), (c_re, "c_re_t"), (c_im, "c_im_t")):
                for c in range(2):
                    sp.dma_start(dst[c * N_STATE:(c + 1) * N_STATE, :], io[name]).then_inc(loaded.sem, 16)
            sp.dma_start(log_dt[:, :], io["L3_xattn_log_dt"].partition_broadcast(P)).then_inc(loaded.sem, 16)
            sp.dma_start(phase[:, :], io["phase"]).then_inc(loaded.sem, 16)
            sp.dma_start(steps[:, :, :], io["steps"].partition_broadcast(P)).then_inc(loaded.sem, 16)
            sp.dma_start(transform[:, :, :], io["lag_transform"]).then_inc(loaded.sem, 16)
            sp.wait_ge(lag_copied.sem, lag_copied.count(0))
            blocks = big[0][:, :, :].rearrange("p (g e) b -> p g e b", e=GROUP)
            for e in range(GROUP):
                sp.dma_start(lags[:, e, :, :], blocks[e * SEQ_A:(e + 1) * SEQ_A, :, e, :]
                             ).then_inc(gathered.sem, 16)

        @block.scalar
        def _(act):
            chain = Chain(act, w.chains["act"])
            chain.restart()
            act.wait_ge(loaded.sem, all_loaded)
            act.activation(log_dt[:, :], log_dt[:, :], ACT.Exp).then_inc(act_done.sem, 1)
            act.wait_ge(dve_done.sem, dve_done.count(0))
            act.activation(tan[:, :], r[:, :], ACT.Tanh, scale=0.5).then_inc(act_done.sem, 1)
            act.activation(big[1][:, :, :], big[1][:, :, :], ACT.Exp)
            act.activation(big[2][:, :, :], big[2][:, :, :], ACT.Exp).then_inc(act_done.sem, 1)
            for n, t in enumerate((sin, cos, half)):
                ins = act.activation(t[:, :], angle[:, n, :], ACT.Sin, scale=TWO_PI)
            ins.then_inc(act_done.sem, 1)
            for n in range(3):
                act.wait_ge(dve_done.sem, dve_done.count(1 + n))
                t = (big[0], big[3], big[4])[n]
                act.activation(t[:, :, :], t[:, :, :], ACT.Sin, scale=TWO_PI).then_inc(act_done.sem, 1)

        @block.vector
        def _(dve):
            chain = Chain(dve, w.chains["dve"])
            chain.restart()
            dve.wait_ge(loaded.sem, all_loaded)
            dve.wait_ge(act_done.sem, act_done.count(0))
            link = chain.link

            def wide(t):
                return t.unsqueeze(2).to_broadcast([P, D, SEQ_A])

            def stepped(n):
                return steps[:, n, :].unsqueeze(1).to_broadcast([P, D, SEQ_A])

            def fraction(x, whole_part):
                link(dve.tensor_scalar(whole_part, x, ROUND, -ROUND, ALU.add, ALU.add))
                return dve.tensor_tensor(x, x, whole_part, ALU.subtract)

            link(dve.tensor_tensor(r[:, :], log_dt[:, :], a_re[:, :], ALU.mult))
            link(dve.tensor_tensor(turn[:, :], log_dt[:, :], a_im[:, :], ALU.mult))
            link(dve.tensor_scalar(turn[:, :], turn[:, :], 1.0 / (2.0 * np.pi), None, ALU.mult))
            for n in range(2):
                link(dve.tensor_tensor(big[1 + n][:, :, :], wide(r[:, :]), stepped(n), ALU.mult))
            link(dve.tensor_copy(angle[:, 0, :], turn[:, :]))
            link(dve.tensor_scalar(angle[:, 1, :], turn[:, :], 0.25, None, ALU.add))
            link(dve.tensor_scalar(angle[:, 2, :], turn[:, :], 0.5, None, ALU.mult))
            link(fraction(angle[:, :, :], whole[:, :, :]))
            dve.engine_nop().then_inc(dve_done.sem, 1)
            link(dve.tensor_copy(turn[:, :], angle[:, 0, :]))
            for n, (t, step) in enumerate(((big[0], 0), (big[3], 0), (big[4], 1))):
                link(dve.tensor_tensor(t[:, :, :], wide(turn[:, :]), stepped(step), ALU.mult))
                link(dve.tensor_scalar(t[:, :, :], t[:, :, :], phase[:, n:n + 1], None, ALU.add))
                scratch = (big[3], big[4], None)[n]
                if scratch is None:
                    break
                link(fraction(t[:, :, :], scratch[:, :, :]))
                dve.engine_nop().then_inc(dve_done.sem, 1)
            dve.wait_ge(act_done.sem, act_done.count(3))
            link(dve.tensor_scalar(t1[:, :], tan[:, :], -1.0, 1.0, ALU.mult, ALU.add))
            link(dve.reciprocal(t1[:, :], t1[:, :]))
            link(dve.scalar_tensor_tensor(t1[:, :], tan[:, :], 2.0, t1[:, :], ALU.mult, ALU.mult))
            link(dve.tensor_tensor(e_re[:, :], t1[:, :], cos[:, :], ALU.mult))
            link(dve.scalar_tensor_tensor(e_im[:, :], t1[:, :], 1.0, sin[:, :], ALU.add, ALU.mult))
            link(dve.scalar_tensor_tensor(t2[:, :], half[:, :], 2.0, half[:, :], ALU.mult, ALU.mult))
            link(dve.tensor_tensor(e_re[:, :], e_re[:, :], t2[:, :], ALU.subtract))

            def complex_product(re, im, x_re, x_im, y_re, y_im, sign):
                link(dve.tensor_tensor(t1[:, :], x_re[:, :], y_re[:, :], ALU.mult))
                link(dve.tensor_tensor(t2[:, :], x_im[:, :], y_im[:, :], ALU.mult))
                link(dve.scalar_tensor_tensor(re[:, :], t2[:, :], -sign, t1[:, :], ALU.mult, ALU.add))
                link(dve.tensor_tensor(t1[:, :], x_im[:, :], y_re[:, :], ALU.mult))
                link(dve.tensor_tensor(t2[:, :], x_re[:, :], y_im[:, :], ALU.mult))
                link(dve.scalar_tensor_tensor(im[:, :], t2[:, :], sign, t1[:, :], ALU.mult, ALU.add))

            complex_product(n_re, n_im, c_re, c_im, e_re, e_im, 1.0)
            complex_product(e_re, e_im, n_re, n_im, a_re, a_im, -1.0)
            link(dve.tensor_tensor(t1[:, :], a_re[:, :], a_re[:, :], ALU.mult))
            link(dve.tensor_tensor(t2[:, :], a_im[:, :], a_im[:, :], ALU.mult))
            link(dve.tensor_tensor(t1[:, :], t1[:, :], t2[:, :], ALU.add))
            link(dve.reciprocal(t1[:, :], t1[:, :]))
            link(dve.tensor_tensor(e_re[:, :], e_re[:, :], t1[:, :], ALU.mult))
            link(dve.tensor_tensor(e_im[:, :], e_im[:, :], t1[:, :], ALU.mult))
            dve.wait_ge(act_done.sem, act_done.count(5))
            link(dve.tensor_tensor(big[0][:, :, :], big[0][:, :, :], wide(e_re[:, :]), ALU.mult))
            link(dve.tensor_tensor(big[3][:, :, :], big[3][:, :, :], wide(e_im[:, :]), ALU.mult))
            link(dve.tensor_tensor(big[0][:, :, :], big[0][:, :, :], big[3][:, :, :], ALU.add))
            link(dve.tensor_tensor(big[1][:, :, :], big[1][:, :, :], big[0][:, :, :], ALU.mult))
            link(fraction(big[4][:, :, :], big[3][:, :, :]))
            dve.engine_nop().then_inc(dve_done.sem, 1)
            dve.wait_ge(act_done.sem, act_done.count(6))
            link(dve.tensor_tensor(big[2][:, :, :], big[2][:, :, :], big[4][:, :, :], ALU.mult))
            dve.engine_nop().then_inc(made.sem, 1)
            dve.wait_ge(lag_psum.sem, lag_psum.count(0))
            dve.tensor_copy(big[0][:, :, :].rearrange("p (g e) b -> p g (e b)", g=8),
                            w.psum[:, :, :]).then_inc(lag_copied.sem, 1)
            dve.wait_ge(spectra.sem, spectra.count(0))
            dve.tensor_copy(by_cos[:, :, :], w.psum[:, 0, :].rearrange("p (k d) -> p k d", d=D))
            dve.tensor_copy(by_sin[:, :, :], w.psum[:, 1, :].rearrange("p (k d) -> p k d", d=D))
            dve.tensor_copy(by_last[:, 0, :], w.psum[:, 2, 0:D])
            dve.tensor_copy(by_last[:, 1, :], w.psum[:, 0, D:2 * D])

        @block.tensor
        def _(pe):
            pe.wait_ge(made.sem, made.count(0))
            for g in range(D // GROUP):
                lanes = slice(g * GROUP, (g + 1) * GROUP)
                last = pe.matmul(w.psum[:, g // 4, (g % 4) * P:(g % 4 + 1) * P], big[1][:, lanes, :],
                                 big[2][:, lanes, :], start=True, stop=True)
            last.then_inc(lag_psum.sem, 1)
            pe.wait_ge(gathered.sem, gathered.base + 16 * GROUP)
            for t in range(5):
                for b in range(SEQ_B):
                    last = pe.matmul(w.psum[:, t // 2, (t % 2) * D:(t % 2 + 1) * D],
                                     transform[:, b, t * P:(t + 1) * P],
                                     lags[:, :, :, b].rearrange("a e g -> a g e"),
                                     start=(b == 0), stop=(b == SEQ_B - 1))
            last.then_inc(spectra.sem, 1)

    loaded.base = all_loaded
    gathered.base += 16 * GROUP
    w.advance(ssm_dve=4, ssm_act=7, states_made=1, lag_psum=1, lag_copied=1, spectra_psum=1)
    return by_cos, by_sin, by_last


def selective_stage(nc, w, ctx):
    heads, dim, top_k = 4, 32, 32
    hidden = 4 * D
    HT = hidden // P
    scale = float(dim) ** -0.5
    io = w.io
    by_cos, by_sin, by_last = spectral_kernel(nc, w, ctx)

    def sb(name, shape, dt=F32):
        return ctx.enter_context(nc.sbuf_tensor(f"sel_{name}", shape, dt))

    wq = sb("wq", [P, DK, heads * dim])
    wk = sb("wk", [CP, 2, heads * dim])
    wv = sb("wv", [CP, 2, D])
    film = [sb(f"film{n}", [P, DK, 2 * D]) for n in range(2)]
    film_b = sb("film_b", [2, 2, 2 * D])
    film_b_high = sb("film_b_high", [2, 2, 2 * D], F32R)
    film_b_parts = sb("film_b_parts", [2, 2, 2 * D], F32R)
    is_low = sb("is_low", [2, 1])
    ones_r = sb("ones_r", [2, P], F32R)
    rows = {n: sb(n, [P, D]) for n in ("g_norm_in", "b_norm_in", "g_ffn", "b_ffn", "g_norm_out", "b_norm_out",
                                       "b2", "D_skip")}
    gate = sb("gate", [P, 1])
    w1 = sb("w1", [P, DK, hidden])
    b1 = sb("b1", [P, HT])
    w2 = sb("w2", [P, HT, D])
    forward = sb("forward", [P, LANES, 4 * P])
    backward = sb("backward", [P, 4, LANES, P])
    text_u8 = sb("text_u8", [P, TILES], U8)
    text = sb("text", [P, TILES])
    vision_u8 = sb("vision_u8", [P, B, NCTX], U8)
    vision = sb("vision", [P, B, NCTX])
    ctx_t = sb("ctx_t", [CP, 2, B, NCTX])
    ctx_b = sb("ctx_b", [CP, 2, NCTX])
    k_t = sb("k_t", [P, NCTX])
    v = sb("v", [NCTX, D])
    xl_t = sb("xl_t", [P, DK, LANES, P])
    q_t = sb("q_t", [P, LANES, P])
    score = sb("score", [P, heads, LANES, NCTX])
    rest = sb("rest", [P, heads, LANES, NCTX])
    top = sb("top", [P, heads, LANES])
    best = sb("best", [P, heads, LANES, 8])
    total = sb("total", [P, heads, LANES])
    mean = sb("mean", [P, LANES, NCTX])
    mean_t = sb("mean_t", [NCTX, LANES, P])
    c_t = sb("c_t", [P, DK, LANES, P])
    mods_in = sb("mods_in", [P, LANES, 2 * D])
    xl = [sb(f"xl{n}", [P, LANES, D]) for n in range(2)]
    u_in = [sb(f"u_in{n}", [P, LANES, D]) for n in range(2)]
    xt_base = [sb(f"xt_base{n}", [P, LANES, D]) for n in range(2)]
    mods_out = [sb(f"mods_out{n}", [P, LANES, 2 * D]) for n in range(2)]
    prod = [sb(f"prod{n}", [P, DK, D]) for n in range(4)]
    spectrum = sb("spectrum", [P, 2 * DK, D])
    y = sb("y", [P, LANES, D])
    xt = sb("xt", [P, LANES, D])
    h = sb("h", [P, LANES, D])
    h_t = sb("h_t", [P, DK, LANES, P])
    hid = sb("hid", [P, HT, LANES, P])
    norms = {half: (sb(f"stats_{half}", [P, LANES, 6]), sb(f"mean_var_{half}", [P, LANES, 2]),
                    sb(f"rstd_{half}", [P, LANES])) for half in "ab"}

    sig = w.counter
    loaded = sig("weights_loaded")
    film_b_ready, spec_ready = sig("film_b_ready"), sig("spec_ready")
    loads = [(wq[:, :, :], io["L3_xattn_Wq"].rearrange("(k p) n -> p k n", p=P)),
             (wk[:, :, :], io["L3_xattn_Wk"].rearrange("(k p) n -> p k n", p=CP)),
             (wv[:, :, :], io["L3_xattn_Wv"].rearrange("(k p) n -> p k n", p=CP)),
             (ctx_t[:, :, :, :], io["ctx_t"].rearrange("(k p) b j -> p k b j", p=CP)),
             (text_u8[:, :], io["text_mask_t"]),
             (vision_u8[:, :, :], io["vision_mask"].partition_broadcast(P)),
             (gate[:, :], io["mod_gate"].partition_broadcast(P)),
             (w1[:, :, :], io["L3_xattn_W1"].rearrange("(k p) n -> p k n", p=P)),
             (b1[:, :], io["L3_xattn_b1"].rearrange("(k p) -> p k", p=P)),
             (w2[:, :, :], io["L3_xattn_W2"].rearrange("(k p) n -> p k n", p=P)),
             (forward[:, :, :], io["forward"].rearrange("(k p) n -> p k n", p=P)),
             (backward[:, :, :, :], io["backward"].rearrange("(k p) (l t) -> p k l t", p=P, t=P))]
    for n, end in enumerate(("in", "out")):
        loads.append((film[n][:, :, :], io[f"L3_xattn_W_film_{end}"].rearrange("(k p) n -> p k n", p=P)))
        loads.append((film_b[:, n, :], io[f"L3_xattn_b_film_{end}"].partition_broadcast(2)))
    for name, t in rows.items():
        loads.append((t[:, :], io[f"L3_xattn_{name}"].partition_broadcast(P)))
    all_loaded = loaded.base + 16 * len(loads)

    once = ("ctx_copied", "kv_ready", "kv_copied", "xl_ready", "xl_t_psum", "xl_t_ready", "q_psum", "q_ready",
            "u_normed", "u_affine", "scores_psum", "struck", "shifted", "exped", "mean_ready", "mean_t_psum",
            "mean_t_ready", "c_psum", "c_ready", "film_in_psum", "film_out_psum", "film_in_ready", "u_ready",
            "base_ready", "freq_psum", "y_psum", "h_affine", "h_t_psum", "h_t_ready", "ffn_psum", "x_updated")
    c_ = {n: sig(n) for n in once}

    def before(eng, name, n):
        eng.wait_ge(c_[name].sem, c_[name].count(n))

    def norm_events(half, i, which):
        n = 2 * i + which
        return sig(f"stats_{half}"), sig(f"rstd_{half}"), n

    ORDER = {"pe": "b0 a0 a1 b1 a2 b2 b3 b4 a4", "dve": "a0 b0 a1 a2 b1 b2 a3 a4 b4 a5",
             "act": "a1 b2 b3 a4", "pool": "a0 a1 b0 b1 a2 b4"}

    def over_batches(eng, name, a, b):
        def run(nxt, now):
            for half, step in ORDER[name].split():
                if half == "b" and now is not None:
                    b(int(step), *now)
                if half == "a" and nxt is not None:
                    a(int(step), *nxt)

        run((0, 0), None)
        with eng.Fori(0, B // 2 - 1) as t:
            run((2 * t + 1, 1), (2 * t, 0))
            run((2 * t + 2, 0), (2 * t + 1, 1))
        run((B - 1, 1), (B - 2, 0))
        run(None, (B - 1, 1))

    def scale_rows(pool, chain, half, i, which):
        stats, rstd, n = norm_events(half, i, which)
        _, mean_var, r = norms[half]
        pool.wait_ge(stats.sem, stats.count(n))
        chain.link(pool.tensor_tensor(r[:, :], mean_var[:, :, 1], w.eps[:, :], ALU.add))
        pool.tensor_tensor(r[:, :], r[:, :], w.neg_half[:, :], ALU.pow).then_inc(rstd.sem, 1)

    def affine(eng, chain, t, gain, shift):
        chain.link(eng.tensor_tensor(t[:, :, :], t[:, :, :],
                                     rows[gain][:, :].unsqueeze(1).to_broadcast([P, LANES, D]), ALU.mult))
        return eng.tensor_tensor(t[:, :, :], t[:, :, :],
                                 rows[shift][:, :].unsqueeze(1).to_broadcast([P, LANES, D]), ALU.add)

    with nc.allow_non_contiguous_dma(reason="biases by partition"), nc.Block() as block:
        @block.sync
        def _(sp):
            for dst, src in loads:
                sp.dma_start(dst, src).then_inc(loaded.sem, 16)

        @block.gpsimd
        def _(pool):
            chain = Chain(pool, w.chains["pool"])
            pool.wait_ge(loaded.sem, all_loaded)

            def a(step, i, par):
                if step == 0:
                    chain.restart_always()
                    before(pool, "kv_ready", i - 1)
                    pool.tensor_copy(ctx_b[:, :, :], ctx_t[:, :, i, :]).then_inc(c_["ctx_copied"].sem, 1)
                    scale_rows(pool, chain, "a", i, 0)
                if step == 1:
                    scale_rows(pool, chain, "a", i, 1)
                if step == 2:
                    before(pool, "u_normed", i)
                    affine(pool, chain, u_in[par], "g_norm_in", "b_norm_in").then_inc(c_["u_affine"].sem, 1)

            def b(step, i, par):
                if step == 0:
                    base = xt_base[par][:, :, :]
                    before(pool, "u_ready", i)
                    chain.link(pool.tensor_tensor(base, u_in[par][:, :, :],
                                                  rows["D_skip"][:, :].unsqueeze(1).to_broadcast([P, LANES, D]),
                                                  ALU.mult))
                    pool.wait_ge(sig("film_out_ready").sem, sig("film_out_ready").count(i))
                    chain.link(pool.tensor_tensor(base, base, mods_out[par][:, :, 0:D], ALU.mult))
                    chain.link(pool.tensor_tensor(base, base, mods_out[par][:, :, D:2 * D], ALU.add))
                    pool.tensor_tensor(base, base, xl[par][:, :, :], ALU.add).then_inc(c_["base_ready"].sem, 1)
                if step == 1:
                    scale_rows(pool, chain, "b", i, 0)
                if step == 4:
                    scale_rows(pool, chain, "b", i, 1)

            over_batches(pool, "pool", a, b)
            chain.restart_always()

        @block.vector
        def _(dve):
            chain = Chain(dve, w.chains["dve"])
            dve.wait_ge(loaded.sem, all_loaded)
            dve.tensor_copy(text[:, :], text_u8[:, :])
            chain.restart_always()
            chain.link(dve.tensor_scalar(vision[:, :, :], vision_u8[:, :, :], -1.0, 3.0e38, ALU.add, ALU.mult))
            chain.link(dve.tensor_scalar(vision[:, :, :], vision[:, :, :], 3.0e38, None, ALU.mult))
            chain.link(dve.tensor_scalar(text[:, :], text[:, :], 1.0 / heads, None, ALU.mult))
            link = chain.link
            dve.tensor_scalar(is_low[:, :], w.ident[0:2, 1:2], -1.0, None, ALU.mult)
            dve.tensor_copy(ones_r[:, :], w.ones[0:2, :])
            link(dve.tensor_copy(film_b_high[:, :, :], film_b[:, :, :]))
            dve.scalar_tensor_tensor(film_b_parts[:, :, :], film_b_high[:, :, :].bitcast(F32), is_low[:, :],
                                     film_b[:, :, :], ALU.mult, ALU.add).then_inc(film_b_ready.sem, 1)

            def stats(half, i, which, x):
                st, mean_var, _ = norms[half]
                for s in range(LANES):
                    ins = dve.bn_stats(st[:, s, :], x(s))
                link(ins)
                for s in range(LANES):
                    ins = dve.bn_aggr(mean_var[:, s, :], st[:, s, :])
                ins.then_inc(norm_events(half, i, which)[0].sem, 1)

            def normalise(half, i, which, x, to):
                _, mean_var, r = norms[half]
                _, rstd, n = norm_events(half, i, which)
                dve.wait_ge(rstd.sem, rstd.count(n))
                for s in range(LANES):
                    ins = dve.tensor_scalar(to[:, s, :], x(s), mean_var[:, s, 0:1], r[:, s:s + 1],
                                            ALU.subtract, ALU.mult)
                return ins

            def a(step, i, par):
                if step == 0:
                    chain.restart_always()
                    stats("a", i, 0, lambda s: w.x_res[:, i * LANES + s, :])
                    link(normalise("a", i, 0, lambda s: w.x_res[:, i * LANES + s, :], xl[par]))
                    dve.engine_nop().then_inc(c_["xl_ready"].sem, 1)
                    stats("a", i, 1, lambda s: xl[par][:, s, :])
                if step == 1:
                    normalise("a", i, 1, lambda s: xl[par][:, s, :], u_in[par]).then_inc(c_["u_normed"].sem, 1)
                    before(dve, "kv_ready", i)
                    dve.tensor_copy(k_t[:, :], w.psum[:, 0, 0:NCTX])
                    dve.tensor_copy(v[:, :], w.psum[0:NCTX, 0, P:P + D]).then_inc(c_["kv_copied"].sem, 1)
                if step == 2:
                    before(dve, "q_psum", i)
                    dve.tensor_copy(q_t[:, :, :], w.psum[:, 2, 0:LANES * P].rearrange(
                        "p (l t) -> p l t", t=P)).then_inc(c_["q_ready"].sem, 1)
                if step == 3:
                    before(dve, "scores_psum", i)
                    shape = [P, heads, LANES, NCTX]
                    for s in range(LANES):
                        ins = dve.tensor_tensor(score[:, :, s, :], w.psum[:, 0:heads, s * NCTX:(s + 1) * NCTX],
                                                vision[:, i, :].unsqueeze(1).to_broadcast([P, heads, NCTX]),
                                                ALU.add)
                    link(ins)
                    link(dve.tensor_reduce(top[:, :, :], score[:, :, :, :], AX.X, ALU.max))
                    link(dve.tensor_tensor(score[:, :, :, :], score[:, :, :, :],
                                           top[:, :, :].unsqueeze(3).to_broadcast(shape), ALU.subtract))
                    lanes = [(hd, s) for hd in range(heads) for s in range(LANES)]
                    for turn in range(top_k // 8):
                        src = score if turn == 0 else rest
                        for hd, s in lanes:
                            ins = dve.max(best[:, hd, s, :], src[:, hd, s, :])
                        link(ins)
                        for hd, s in lanes:
                            ins = dve.match_replace(rest[:, hd, s, :], best[:, hd, s, :], src[:, hd, s, :],
                                                    -1.0e30)
                        link(ins)
                        if turn == 0:
                            dve.engine_nop().then_inc(c_["struck"].sem, 1)
                    dve.engine_nop().then_inc(c_["shifted"].sem, 1)
                if step == 4:
                    before(dve, "exped", i)
                    link(dve.tensor_tensor(score[:, :, :, :], score[:, :, :, :], rest[:, :, :, :],
                                           ALU.subtract))
                    link(dve.tensor_reduce(total[:, :, :], score[:, :, :, :], AX.X, ALU.add))
                    link(dve.reciprocal(total[:, :, :], total[:, :, :]))
                    link(dve.tensor_tensor(total[:, :, :], total[:, :, :],
                                           text[:, bass.ds(i * LANES, LANES)].unsqueeze(1)
                                           .to_broadcast([P, heads, LANES]), ALU.mult))
                    for s in range(LANES):
                        ins = dve.tensor_scalar(mean[:, s, :], score[:, 0, s, :], total[:, 0, s:s + 1], None,
                                                ALU.mult)
                    link(ins)
                    for hd in range(1, heads):
                        for s in range(LANES):
                            ins = dve.scalar_tensor_tensor(mean[:, s, :], score[:, hd, s, :],
                                                           total[:, hd, s:s + 1], mean[:, s, :],
                                                           ALU.mult, ALU.add)
                        if hd < heads - 1:
                            link(ins)
                    ins.then_inc(c_["mean_ready"].sem, 1)
                if step == 5:
                    before(dve, "u_affine", i)
                    before(dve, "film_in_ready", i)
                    link(dve.tensor_tensor(u_in[par][:, :, :], u_in[par][:, :, :], mods_in[:, :, 0:D], ALU.mult))
                    dve.tensor_tensor(u_in[par][:, :, :], u_in[par][:, :, :], mods_in[:, :, D:2 * D],
                                      ALU.add).then_inc(c_["u_ready"].sem, 1)

            def b(step, i, par):
                if step == 0:
                    before(dve, "freq_psum", i)
                    x_cos = w.psum[:, 4, :].rearrange("p (k d) -> p k d", d=D)
                    x_sin = w.psum[:, 5, :].rearrange("p (k d) -> p k d", d=D)
                    dve.tensor_tensor(prod[0][:, :, :], x_cos, by_cos[:, :, :], ALU.mult)
                    link(dve.tensor_tensor(prod[1][:, :, :], x_sin, by_sin[:, :, :], ALU.mult))
                    dve.tensor_tensor(spectrum[:, 0:DK, :], prod[0][:, :, :], prod[1][:, :, :],
                                      ALU.subtract).then_inc(spec_ready.sem, 1)
                    dve.tensor_tensor(prod[2][:, :, :], x_cos, by_sin[:, :, :], ALU.mult)
                    link(dve.tensor_tensor(prod[3][:, :, :], x_sin, by_last[:, :, :], ALU.mult))
                    dve.tensor_tensor(spectrum[:, DK:2 * DK, :], prod[2][:, :, :], prod[3][:, :, :],
                                      ALU.add).then_inc(spec_ready.sem, 1)
                if step == 1:
                    dve.wait_ge(sig("film_out_ready").sem, sig("film_out_ready").count(i))
                    before(dve, "y_psum", i)
                    link(dve.tensor_tensor(xt[:, :, :], w.psum[:, 6:8, 0:D], mods_out[par][:, :, 0:D], ALU.mult))
                    before(dve, "base_ready", i)
                    link(dve.tensor_tensor(xt[:, :, :], xt[:, :, :], xt_base[par][:, :, :], ALU.add))
                    stats("b", i, 0, lambda s: xt[:, s, :])
                if step == 2:
                    link(normalise("b", i, 0, lambda s: xt[:, s, :], h))
                    affine(dve, chain, h, "g_ffn", "b_ffn").then_inc(c_["h_affine"].sem, 1)
                    link(dve.tensor_tensor(xt[:, :, :], xt[:, :, :],
                                           rows["b2"][:, :].unsqueeze(1).to_broadcast([P, LANES, D]), ALU.add))
                if step == 4:
                    before(dve, "ffn_psum", i)
                    link(dve.tensor_tensor(xt[:, :, :], w.psum[:, 4, :].rearrange("p (l d) -> p l d", d=D),
                                           xt[:, :, :], ALU.add))
                    stats("b", i, 1, lambda s: xt[:, s, :])
                    link(normalise("b", i, 1, lambda s: xt[:, s, :], y))
                    link(affine(dve, chain, y, "g_norm_out", "b_norm_out"))
                    tiles = w.x_res[:, bass.ds(i * LANES, LANES), :]
                    dve.tensor_tensor(tiles, tiles, y[:, :, :], ALU.add).then_inc(c_["x_updated"].sem, 1)

            over_batches(dve, "dve", a, b)
            chain.restart_always()

        @block.scalar
        def _(act):
            act.wait_ge(loaded.sem, all_loaded)

            def a(step, i, par):
                if step == 1:
                    before(act, "xl_t_psum", i)
                    act.activation(xl_t[:, :, :, :], w.psum[:, 1, :].rearrange("p (k l t) -> p k l t", k=DK, t=P),
                                   ACT.Copy).then_inc(c_["xl_t_ready"].sem, 1)
                if step == 4:
                    before(act, "struck", i)
                    act.activation(score[:, :, :, :], score[:, :, :, :], ACT.Exp, scale=scale)
                    before(act, "shifted", i)
                    act.activation(rest[:, :, :, :], rest[:, :, :, :], ACT.Exp,
                                   scale=scale).then_inc(c_["exped"].sem, 1)
                    before(act, "mean_t_psum", i)
                    act.activation(mean_t[:, :, :], w.psum[0:NCTX, 0, 0:LANES * P].rearrange(
                        "p (l t) -> p l t", t=P), ACT.Copy).then_inc(c_["mean_t_ready"].sem, 1)
                    before(act, "c_psum", i)
                    act.activation(c_t[:, :, :, :], w.psum[:, 1, :].rearrange("p (k l t) -> p k l t", k=DK, t=P),
                                   ACT.Copy).then_inc(c_["c_ready"].sem, 1)
                    for at, mods, psum_ready, ready in (
                            (0, mods_in, c_["film_in_psum"], c_["film_in_ready"]),
                            (2, mods_out[par], c_["film_out_psum"], sig("film_out_ready"))):
                        act.wait_ge(psum_ready.sem, psum_ready.count(i))
                        act.activation(mods[:, :, 0:D], w.psum[:, at:at + 2, 0:D], ACT.Identity,
                                       scale=gate[:, 0:1], bias=w.ones[:, 0:1])
                        act.activation(mods[:, :, D:2 * D], w.psum[:, at:at + 2, D:2 * D], ACT.Copy,
                                       scale=gate[:, 0:1]).then_inc(ready.sem, 1)

            def b(step, i, par):
                if step == 2:
                    before(act, "h_t_psum", i)
                    act.activation(h_t[:, :, :, :], w.psum[:, 7, :].rearrange("p (k l t) -> p k l t", k=DK, t=P),
                                   ACT.Copy).then_inc(c_["h_t_ready"].sem, 1)
                if step == 3:
                    for c in range(4):
                        act.wait_ge(sig("hid_psum").sem, sig("hid_psum").count(i * 4 + c))
                        for m in range(2):
                            j = 2 * c + m
                            ins = act.activation(hid[:, j, :, :], w.psum[:, 4 + c, m * D:(m + 1) * D]
                                                 .rearrange("p (l t) -> p l t", t=P),
                                                 ACT.Gelu, bias=b1[:, j:j + 1])
                        ins.then_inc(sig("hid_ready").sem, 1)

            over_batches(act, "act", a, b)

        @block.tensor
        def _(pe):
            pe.wait_ge(loaded.sem, all_loaded)
            pe.wait_ge(film_b_ready.sem, film_b_ready.count(0))

            def a(step, i, par):
                if step == 0:
                    pe.wait_ge(sig("film_out_ready").sem, sig("film_out_ready").count(i - 1))
                    before(pe, "ctx_copied", i)
                    for k in range(2):
                        pe.matmul(w.psum[:, 0, 0:NCTX], wk[:, k, :], ctx_b[:, k, :], start=(k == 0), stop=(k == 1))
                    for k in range(2):
                        last = pe.matmul(w.psum[0:NCTX, 0, P:P + D], ctx_b[:, k, :], wv[:, k, :],
                                         start=(k == 0), stop=(k == 1))
                    last.then_inc(c_["kv_ready"].sem, 1)
                    before(pe, "xl_ready", i)
                    for k in range(DK):
                        for s in range(LANES):
                            at = (k * LANES + s) * P
                            last = pe.transpose(w.psum[:, 1, at:at + P], xl[par][:, s, k * P:(k + 1) * P],
                                                w.ident[:, :])
                    last.then_inc(c_["xl_t_psum"].sem, 1)
                if step == 1:
                    before(pe, "xl_t_ready", i)
                    for k in range(DK):
                        last = pe.matmul(w.psum[:, 2, 0:LANES * P], wq[:, k, :], xl_t[:, k, :, :],
                                         start=(k == 0), stop=(k == DK - 1))
                    last.then_inc(c_["q_psum"].sem, 1)
                if step == 2:
                    before(pe, "kv_copied", i)
                    before(pe, "q_ready", i)
                    for s in range(LANES):
                        for hd in range(heads):
                            part = slice(hd * dim, (hd + 1) * dim)
                            last = pe.matmul(w.psum[:, hd, s * NCTX:(s + 1) * NCTX], q_t[part, s, :],
                                             k_t[part, :], start=True, stop=True)
                    last.then_inc(c_["scores_psum"].sem, 1)
                if step == 4:
                    before(pe, "mean_ready", i)
                    for s in range(LANES):
                        last = pe.transpose(w.psum[0:NCTX, 0, s * P:(s + 1) * P], mean[:, s, :], w.ident[:, :])
                    last.then_inc(c_["mean_t_psum"].sem, 1)
                    before(pe, "mean_t_ready", i)
                    for k in range(DK):
                        last = pe.matmul(w.psum[:, 1, k * LANES * P:(k + 1) * LANES * P],
                                         v[:, k * P:(k + 1) * P], mean_t[:, :, :], start=True, stop=True)
                    last.then_inc(c_["c_psum"].sem, 1)
                    before(pe, "c_ready", i)
                    for n in range(2):
                        for s in range(LANES):
                            bank = w.psum[:, 2 * n + s, :]
                            pe.matmul(bank, ones_r[:, :], film_b_parts[:, n, :], start=True, stop=False)
                            for k in range(DK):
                                last = pe.matmul(bank, c_t[:, k, s, :], film[n][:, k, :], start=False,
                                                 stop=(k == DK - 1))
                        last.then_inc(c_[("film_in_psum", "film_out_psum")[n]].sem, 1)

            def b(step, i, par):
                if step == 0:
                    before(pe, "u_ready", i)
                    before(pe, "x_updated", i - 1)
                    for f in range(4):
                        for s in range(LANES):
                            last = pe.matmul(w.psum[:, 4 + f // 2, (f % 2) * D:(f % 2 + 1) * D],
                                             forward[:, s, f * P:(f + 1) * P], u_in[par][:, s, :],
                                             start=(s == 0), stop=(s == LANES - 1))
                    last.then_inc(c_["freq_psum"].sem, 1)
                if step == 1:
                    for f in range(4):
                        if f % 2 == 0:
                            pe.wait_ge(spec_ready.sem, spec_ready.count(2 * i + f // 2))
                        for s in range(LANES):
                            last = pe.matmul(w.psum[:, 6 + s, 0:D], backward[:, f, s, :],
                                             spectrum[:, f, :], start=(f == 0), stop=(f == 3))
                    last.then_inc(c_["y_psum"].sem, 1)
                if step == 2:
                    before(pe, "h_affine", i)
                    for k in range(DK):
                        for s in range(LANES):
                            at = (k * LANES + s) * P
                            last = pe.transpose(w.psum[:, 7, at:at + P], h[:, s, k * P:(k + 1) * P],
                                                w.ident[:, :])
                    last.then_inc(c_["h_t_psum"].sem, 1)
                if step == 3:
                    before(pe, "h_t_ready", i)
                    for c in range(4):
                        for m in range(2):
                            j = 2 * c + m
                            for k in range(DK):
                                last = pe.matmul(w.psum[:, 4 + c, m * D:(m + 1) * D],
                                                 w1[:, k, j * P:(j + 1) * P], h_t[:, k, :, :],
                                                 start=(k == 0), stop=(k == DK - 1))
                        last.then_inc(sig("hid_psum").sem, 1)
                if step == 4:
                    for c in range(4):
                        pe.wait_ge(sig("hid_ready").sem, sig("hid_ready").count(i * 4 + c))
                    for s in range(LANES):
                        for j in range(HT):
                            last = pe.matmul(w.psum[:, 4, s * D:(s + 1) * D], hid[:, j, s, :], w2[:, j, :],
                                             start=(j == 0), stop=(j == HT - 1))
                    last.then_inc(c_["ffn_psum"].sem, 1)

            over_batches(pe, "pe", a, b)

    loaded.base = all_loaded
    w.advance(**{name: B for name in once})
    w.advance(film_b_ready=1, spec_ready=2 * B, film_out_ready=B, hid_psum=4 * B, hid_ready=4 * B, stats_a=2 * B, rstd_a=2 * B, stats_b=2 * B,
              rstd_b=2 * B)



def chosen_attention_stage(nc, w, ctx):
    experts, slots, hp, rotate = 8, 32, 128, 64
    scale = float(hp) ** -0.5
    HALF = experts // 2
    GROUPS = 2
    io = w.io
    N = B * slots

    def sb(name, shape, dt=F32):
        return ctx.enter_context(nc.sbuf_tensor(f"cho_{name}", shape, dt))

    xn_all = sb("xn_all", [P, TILES, D])
    gathered = sb("gathered", [P, DK, experts, B, slots])
    rope = sb("rope", [P, 2, experts, B, slots])
    wr = sb("wr", [P, DK, experts])
    wqkv = sb("wqkv", [P, DK, experts, 3 * hp])
    wo = sb("wo", [P, experts, D])
    table = sb("table", [P, LANES, 2, P])
    upto = sb("upto", [P, P])
    mask = sb("mask", [P, P])
    iota = sb("iota", [P, slots])
    score_t = sb("score_t", [P, LANES, B * experts])
    chosen_t = sb("chosen_t", [P, LANES, B * experts])
    slot_t = sb("slot_t", [P, LANES, B * experts])
    score = sb("score", [P, S])
    rest = sb("rest", [P, S])
    best = sb("best", [P, 8])
    xn = sb("xn", [P, LANES, D])
    xn_t = sb("xn_t", [P, LANES, DK, P])
    hot = sb("hot", [P, LANES, experts, slots])
    swapped = sb("swapped", [rotate, 2, N])
    v_all = xn_all[:, 0:experts * N // D, :].rearrange("p (e x) d -> p e (x d)", e=experts) \
                                            .rearrange("p e (b j) -> p e b j", j=slots)

    sig = w.counter
    loaded = sig("weights_loaded")
    loads = [(wr[:, :, :], io["wr_t"].rearrange("(k p) e -> p k e", p=P))]
    loads += [(wqkv[:, k, :, :], io["L3_ffn_Wqkv"][:, k * P:(k + 1) * P, :].rearrange("e p n -> p e n"))
              for k in range(DK)]
    loads += [(wo[:, :, :], io["L3_ffn_Wo"].rearrange("e p n -> p e n")),
              (table[:, :, :, :], io["rotary"].rearrange("(l p) c d -> p l c d", p=P)),
              (upto[:, :], io["upto"]), (mask[:, :], io["slot_mask"]),
              (iota[:, :], io["iota"][1:1 + slots].partition_broadcast(P))]
    all_loaded = loaded.base + 16 * len(loads)
    xn_ready, xn_t_psum, xn_t_ready = sig("xn_ready"), sig("xn_t_psum"), sig("xn_t_ready")
    gate_psum, exped = sig("scores_psum"), sig("exped")
    stepped, turned = sig("choice_step"), sig("choice_turned")

    with nc.Block() as block:
        @block.sync
        def _(sp):
            for dst, src in loads:
                sp.dma_start(dst, src).then_inc(loaded.sem, 16)

        @block.gpsimd
        def _(pool):
            chain = Chain(pool, w.chains["pool"])
            with pool.Fori(0, B) as i:
                chain.restart_always()
                for s in range(LANES):
                    layernorm_rstd(pool, w, chain, i * LANES + s, s)
                for s in range(LANES):
                    u = i * LANES + s
                    pool.wait_ge(xn_ready.sem, xn_ready.count(u))
                    pool.tensor_copy(xn_all[:, u, :], xn[:, s, :]).then_inc(sig("xn_kept").sem, 1)

        @block.vector
        def _(dve):
            chain = Chain(dve, w.chains["dve"])
            dve.wait_ge(loaded.sem, all_loaded)
            with dve.Fori(0, B) as i:
                chain.restart_always()
                for s in range(LANES):
                    layernorm_stats(dve, w, chain, i * LANES + s, s)
                for s in range(LANES):
                    u = i * LANES + s
                    dve.wait_ge(sig("xn_kept").sem, sig("xn_kept").count(i * LANES - 1))
                    dve.wait_ge(xn_t_psum.sem, xn_t_psum.count(i * LANES - 1))
                    layernorm_apply(dve, w, xn[:, s, :], u, s).then_inc(xn_ready.sem, 1)
            dve.wait_ge(exped.sem, exped.count(TILES - 1))
            chain.restart_always()
            chain.link(dve.tensor_scalar(score_t[:, :, :], score_t[:, :, :], 1.0, None, ALU.add))
            chain.link(dve.reciprocal(score_t[:, :, :], score_t[:, :, :]))
            dve.engine_nop().then_inc(stepped.sem, 1)
            dve.wait_ge(turned.sem, turned.count(0))
            chain.link(dve.tensor_copy(score[:, :], w.psum[:, 0, 0:S]))
            for n in range(slots // 8):
                src = score if n == 0 else rest
                chain.link(dve.max(best[:, :], src[:, :]))
                chain.link(dve.match_replace(rest[:, :], best[:, :], src[:, :], -1.0))
            chain.link(dve.tensor_scalar(rest[:, :], rest[:, :], 0.0, None, ALU.is_lt))
            dve.engine_nop().then_inc(stepped.sem, 1)
            dve.wait_ge(turned.sem, turned.count(1))
            chain.link(dve.tensor_copy(chosen_t[:, :, :], w.psum[:, 1, 0:S].rearrange("p (l x) -> p l x", l=LANES)))
            dve.engine_nop().then_inc(stepped.sem, 1)
            dve.wait_ge(turned.sem, turned.count(2))
            chain.link(dve.tensor_tensor(slot_t[:, :, :], w.psum[:, 2, 0:S].rearrange("p (l x) -> p l x", l=LANES),
                                         chosen_t[:, :, :], ALU.mult))

        @block.scalar
        def _(act):
            with act.Fori(0, B) as i:
                for s in range(LANES):
                    u = i * LANES + s
                    act.wait_ge(xn_t_psum.sem, xn_t_psum.count(u))
                    act.activation(xn_t[:, s, :, :], w.lane(s)[:, 0, 0:D].rearrange("p (k t) -> p k t", t=P),
                                   ACT.Copy).then_inc(xn_t_ready.sem, 1)
                for s in range(LANES):
                    u = i * LANES + s
                    act.wait_ge(gate_psum.sem, gate_psum.count(u))
                    act.activation(score_t[:, s, bass.ds(i * experts, experts)], w.lane(s)[:, 1, 0:experts],
                                   ACT.Exp, scale=-1.0).then_inc(exped.sem, 1)

        @block.tensor
        def _(pe):
            pe.wait_ge(loaded.sem, all_loaded)
            with pe.Fori(0, B) as i:
                for s in range(LANES):
                    pe.wait_ge(xn_ready.sem, xn_ready.count(i * LANES + s))
                    transpose_tile(pe, w, xn[:, s, :], w.lane(s)[:, 0, :],
                                   w.ident[:, :]).then_inc(xn_t_psum.sem, 1)
                for s in range(LANES):
                    pe.wait_ge(xn_t_ready.sem, xn_t_ready.count(i * LANES + s))
                    pe.wait_ge(exped.sem, exped.count(i * LANES - 1))
                    for k in range(DK):
                        last = pe.matmul(w.lane(s)[:, 1, 0:experts], xn_t[:, s, k, :], wr[:, k, :],
                                         start=(k == 0), stop=(k == DK - 1))
                    last.then_inc(gate_psum.sem, 1)
            pe.wait_ge(stepped.sem, stepped.count(0))
            for s in range(LANES):
                last = pe.transpose(w.psum[:, 0, s * P:(s + 1) * P], score_t[:, s, :], w.ident[:, :])
            last.then_inc(turned.sem, 1)
            pe.wait_ge(stepped.sem, stepped.count(1))
            for s in range(LANES):
                last = pe.transpose(w.psum[:, 1, s * P:(s + 1) * P], rest[:, s * P:(s + 1) * P], w.ident[:, :])
            last.then_inc(turned.sem, 1)
            pe.wait_ge(stepped.sem, stepped.count(2))
            pe.matmul(w.psum[:, 2, 0:P], upto[:, :], chosen_t[:, 0, :], start=True, stop=True)
            pe.matmul(w.psum[:, 2, P:2 * P], w.ones[:, :], chosen_t[:, 0, :], start=True, stop=False)
            pe.matmul(w.psum[:, 2, P:2 * P], upto[:, :], chosen_t[:, 1, :], start=False,
                      stop=True).then_inc(turned.sem, 1)

    loaded.base = all_loaded
    w.advance(choice_step=3, choice_turned=3)
    w.advance(**{name: TILES for name in ("stats_ready", "rstd_ready", "xn_ready", "xn_kept", "xn_t_psum",
                                          "xn_t_ready", "scores_psum", "exped")})

    hot_ready, gather_psum, gather_kept = sig("hot_ready"), sig("gather_psum"), sig("gather_kept")
    with nc.Block() as block:
        @block.gpsimd
        def _(pool):
            with pool.Fori(0, B) as i:
                pool.wait_ge(gather_psum.sem, gather_psum.count(i - 1))
                pool.tensor_copy(xn[:, :, :], xn_all[:, bass.ds(i * LANES, LANES), :]
                                 ).then_inc(sig("xn_kept").sem, 1)

        @block.vector
        def _(dve):
            with dve.Fori(0, B) as i:
                dve.wait_ge(gather_psum.sem, gather_psum.count(i - 1))
                for s in range(LANES):
                    dve.tensor_tensor(hot[:, s, :, :],
                                      slot_t[:, s, bass.ds(i * experts, experts)].unsqueeze(2)
                                      .to_broadcast([P, experts, slots]),
                                      iota[:, :].unsqueeze(1).to_broadcast([P, experts, slots]),
                                      ALU.is_equal).then_inc(hot_ready.sem, 1)
                dve.wait_ge(gather_psum.sem, gather_psum.count(i))
                for k in range(DK):
                    dve.tensor_copy(gathered[:, k, :, i, :],
                                    w.psum[:, k, 0:D].rearrange("p (e j) -> p e j", j=slots)
                                    ).then_inc(gather_kept.sem, 1)

        @block.scalar
        def _(act):
            with act.Fori(0, B) as i:
                act.wait_ge(gather_psum.sem, gather_psum.count(i))
                for c in range(2):
                    act.activation(rope[:, c, :, i, :], w.psum[:, 2 + c, 0:D].rearrange("p (e j) -> p e j", j=slots),
                                   ACT.Copy).then_inc(sig("rope_kept").sem, 1)

        @block.tensor
        def _(pe):
            with pe.Fori(0, B) as i:
                pe.wait_ge(sig("xn_kept").sem, sig("xn_kept").count(i))
                pe.wait_ge(hot_ready.sem, hot_ready.count(i * LANES + LANES - 1))
                pe.wait_ge(gather_kept.sem, gather_kept.count(i * 2 - 1))
                pe.wait_ge(sig("rope_kept").sem, sig("rope_kept").count(i * 2 - 1))
                for n in range(4):
                    for s in range(LANES):
                        lhs = xn[:, s, n * P:(n + 1) * P] if n < DK else table[:, s, n - DK, :]
                        last = pe.matmul(w.psum[:, n, 0:D], lhs, hot[:, s, :, :], start=(s == 0),
                                         stop=(s == LANES - 1))
                last.then_inc(gather_psum.sem, 1)
    w.advance(xn_kept=B, hot_ready=TILES, gather_psum=B, gather_kept=2 * B, rope_kept=2 * B)

    qkv_psum, qkv_kept, half_swapped = sig("qkv_psum"), sig("qkv_kept"), sig("half_swapped")
    with nc.Block() as block:
        @block.tensor
        def _(pe):
            for e in range(experts):
                base = 3 * (e % 2)
                if e >= 2:
                    pe.wait_ge(qkv_kept.sem, qkv_kept.count(e - 2))
                    pe.wait_ge(half_swapped.sem, half_swapped.count(2 * (e - 2) + 1))
                    pe.wait_ge(sig("v_kept").sem, sig("v_kept").count(e - 2))
                for n in range(3):
                    for k in range(DK):
                        last = pe.matmul(w.psum[:, base + n, :], wqkv[:, k, e, n * hp:(n + 1) * hp],
                                         gathered[:, k, e, :, :], start=(k == 0), stop=(k == DK - 1))
                last.then_inc(qkv_psum.sem, 1)

        @block.scalar
        def _(act):
            for e in range(experts):
                base = 3 * (e % 2)
                act.wait_ge(qkv_psum.sem, qkv_psum.count(e))
                for n in range(2):
                    if e >= 1:
                        act.wait_ge(qkv_kept.sem, qkv_kept.count(e - 1))
                    for c in range(2):
                        ins = act.activation(swapped[32 * (1 - c):32 * (2 - c), n, :],
                                             w.psum[32 * c:32 * (c + 1), base + n, :], ACT.Copy)
                    ins.then_inc(half_swapped.sem, 1)
                act.activation(v_all[:, e, :, :], w.psum[:, base + 2, :].rearrange("p (b j) -> p b j", j=slots),
                               ACT.Copy).then_inc(sig("v_kept").sem, 1)

        @block.vector
        def _(dve):
            chain = Chain(dve, w.chains["dve"])
            chain.restart_always()
            for e in range(experts):
                base = 3 * (e % 2)
                dve.wait_ge(qkv_psum.sem, qkv_psum.count(e))
                for n in range(2):
                    kept = gathered[:, n, e, :, :]
                    dve.wait_ge(half_swapped.sem, half_swapped.count(2 * e + n))
                    chain.link(dve.tensor_tensor(kept, w.psum[:, base + n, :]
                                                 .rearrange("p (b j) -> p b j", j=slots),
                                                 rope[:, 0, e, :, :], ALU.mult))
                    turned_half = swapped[:, n, :].rearrange("p (b j) -> p b j", j=slots)
                    chain.link(dve.tensor_tensor(turned_half, turned_half, rope[0:rotate, 1, e, :, :], ALU.mult))
                    chain.link(dve.tensor_tensor(kept[0:rotate], kept[0:rotate], turned_half, ALU.add))
                dve.engine_nop().then_inc(qkv_kept.sem, 1)
    w.advance(qkv_psum=experts, half_swapped=2 * experts, qkv_kept=experts, v_kept=experts)

    q_b = sb("q_b", [P, experts, slots])
    v_b = sb("v_b", [P, experts, slots])
    masked = sb("masked", [P, GROUPS, P])
    top = sb("top", [P, GROUPS])
    total = sb("total", [P, GROUPS])
    prob_t = sb("prob_t", [P, GROUPS, P])
    v_rows = sb("v_rows", [P, GROUPS, P])
    attn = sb("attn", [P, GROUPS, P])
    put = sb("put", [P, GROUPS, D])
    hot_t = sb("hot_t", [P, GROUPS, S])

    staged, scores_psum, shifted = sig("staged"), sig("scores_psum"), sig("shifted")
    prob_t_psum, prob_t_ready = sig("prob_t_psum"), sig("prob_t_ready")
    attn_psum, attn_ready, put_psum, put_ready = (sig(n) for n in ("attn_psum", "attn_ready", "put_psum",
                                                                  "put_ready"))
    hot_t_psum, hot_t_ready, out_psum, x_updated = (sig(n) for n in ("hot_t_psum", "hot_t_ready", "out_psum",
                                                                    "x_updated"))
    inverse_ready = sig("inverse_ready")

    with nc.Block() as block:
        @block.gpsimd
        def _(pool):
            with pool.Fori(0, B) as i:
                pool.wait_ge(prob_t_psum.sem, prob_t_psum.count(i * GROUPS - 1))
                pool.tensor_copy(q_b[:, :, :], gathered[:, 0, :, i, :])
                pool.tensor_copy(v_b[:, :, :], v_all[:, :, i, :]).then_inc(staged.sem, 1)

        @block.vector
        def _(dve):
            chain = Chain(dve, w.chains["dve"])
            with dve.Fori(0, B) as i:
                chain.restart_always()
                for g in range(GROUPS):
                    n = i * GROUPS + g
                    dve.wait_ge(scores_psum.sem, scores_psum.count(n))
                    chain.link(dve.tensor_tensor(masked[:, g, :], w.psum[:, g, 0:P], mask[:, :], ALU.add))
                    chain.link(dve.tensor_reduce(top[:, g:g + 1], masked[:, g, :], AX.X, ALU.max))
                    dve.tensor_scalar(masked[:, g, :], masked[:, g, :], top[:, g:g + 1], None,
                                      ALU.subtract).then_inc(shifted.sem, 1)
                for s in range(LANES):
                    part = slot_t[:, s, bass.ds(i * experts, experts)].unsqueeze(2).to_broadcast(
                        [P, experts, slots])
                    value = score_t[:, s, bass.ds(i * experts, experts)].unsqueeze(2).to_broadcast(
                        [P, experts, slots])
                    chain.link(dve.tensor_tensor(hot[:, s, :, :], part, iota[:, :].unsqueeze(1).to_broadcast(
                        [P, experts, slots]), ALU.is_equal))
                    dve.tensor_tensor(hot[:, s, :, :], hot[:, s, :, :], value,
                                      ALU.mult).then_inc(hot_ready.sem, 1)
                for g in range(GROUPS):
                    n = i * GROUPS + g
                    dve.wait_ge(exped.sem, exped.count(n))
                    dve.reciprocal(total[:, g:g + 1], total[:, g:g + 1]).then_inc(inverse_ready.sem, 1)
                for g in range(GROUPS):
                    n = i * GROUPS + g
                    dve.wait_ge(prob_t_psum.sem, prob_t_psum.count(n))
                    dve.tensor_copy(prob_t[:, g, :], w.psum[:, 2 + g, 0:P])
                    dve.tensor_copy(v_rows[:, g, :], w.psum[:, 2 + g, P:2 * P]).then_inc(prob_t_ready.sem, 1)
                for g in range(GROUPS):
                    n = i * GROUPS + g
                    dve.wait_ge(hot_t_psum.sem, hot_t_psum.count(n))
                    dve.tensor_copy(hot_t[:, g, :], w.psum[:, g, 0:S]).then_inc(hot_t_ready.sem, 1)
                for s in range(LANES):
                    u = i * LANES + s
                    dve.wait_ge(out_psum.sem, out_psum.count(u))
                    dve.tensor_tensor(w.x_res[:, u, :], w.x_res[:, u, :], w.psum[:, 4 + s, 0:D],
                                      ALU.add).then_inc(x_updated.sem, 1)

        @block.scalar
        def _(act):
            with act.Fori(0, B) as i:
                for g in range(GROUPS):
                    n = i * GROUPS + g
                    act.wait_ge(shifted.sem, shifted.count(n))
                    act.activation(masked[:, g, :], masked[:, g, :], ACT.Exp, scale=scale,
                                   accum_out=total[:, g:g + 1]).then_inc(exped.sem, 1)
                for g in range(GROUPS):
                    n = i * GROUPS + g
                    act.wait_ge(attn_psum.sem, attn_psum.count(n))
                    act.activation(attn[:, g, :], w.psum[:, 4 + g, 0:P], ACT.Copy).then_inc(attn_ready.sem, 1)
                for g in range(GROUPS):
                    n = i * GROUPS + g
                    act.wait_ge(inverse_ready.sem, inverse_ready.count(n))
                    act.wait_ge(put_psum.sem, put_psum.count(n))
                    act.activation(put[:, g, :], w.psum[:, 6 + g, 0:D], ACT.Copy,
                                   scale=total[:, g:g + 1]).then_inc(put_ready.sem, 1)

        @block.tensor
        def _(pe):
            with pe.Fori(0, B) as i:
                pe.wait_ge(staged.sem, staged.count(i))
                pe.wait_ge(x_updated.sem, x_updated.count(i * LANES - 1))
                for g in range(GROUPS):
                    es = slice(g * HALF, (g + 1) * HALF)
                    pe.matmul(w.psum[:, g, 0:P], q_b[:, es, :], gathered[:, 1, es, i, :], start=True,
                              stop=True).then_inc(scores_psum.sem, 1)
                for g in range(GROUPS):
                    es = slice(g * HALF, (g + 1) * HALF)
                    pe.wait_ge(exped.sem, exped.count(i * GROUPS + g))
                    pe.transpose(w.psum[:, 2 + g, 0:P], masked[:, g, :], w.ident[:, :])
                    pe.transpose(w.psum[:, 2 + g, P:2 * P], v_b[:, es, :],
                                 w.ident[:, :]).then_inc(prob_t_psum.sem, 1)
                pe.wait_ge(hot_ready.sem, hot_ready.count(i * LANES + LANES - 1))
                for g in range(GROUPS):
                    es = slice(g * HALF, (g + 1) * HALF)
                    for s in range(LANES):
                        last = pe.transpose(w.psum[:, g, s * P:(s + 1) * P], hot[:, s, es, :], w.ident[:, :])
                    last.then_inc(hot_t_psum.sem, 1)
                for g in range(GROUPS):
                    pe.wait_ge(prob_t_ready.sem, prob_t_ready.count(i * GROUPS + g))
                    pe.matmul(w.psum[:, 4 + g, 0:P], v_rows[:, g, :], prob_t[:, g, :], start=True,
                              stop=True).then_inc(attn_psum.sem, 1)
                for g in range(GROUPS):
                    pe.wait_ge(attn_ready.sem, attn_ready.count(i * GROUPS + g))
                    for x in range(HALF):
                        rows = slice(x * slots, (x + 1) * slots)
                        last = pe.matmul(w.psum[rows, 6 + g, 0:D], attn[:, g, rows], wo[:, g * HALF + x, :],
                                         start=True, stop=True)
                    last.then_inc(put_psum.sem, 1)
                pe.wait_ge(put_ready.sem, put_ready.count(i * GROUPS + GROUPS - 1))
                pe.wait_ge(hot_t_ready.sem, hot_t_ready.count(i * GROUPS + GROUPS - 1))
                for s in range(LANES):
                    for g in range(GROUPS):
                        last = pe.matmul(w.psum[:, 4 + s, 0:D], hot_t[:, g, s * P:(s + 1) * P], put[:, g, :],
                                         start=(g == 0), stop=(g == GROUPS - 1))
                    last.then_inc(out_psum.sem, 1)

    w.advance(staged=B)
    w.advance(**{name: TILES for name in (
        "scores_psum", "shifted", "exped", "inverse_ready", "prob_t_psum", "prob_t_ready", "attn_psum",
        "attn_ready", "put_psum", "put_ready", "hot_ready", "hot_t_psum", "hot_t_ready", "out_psum",
        "x_updated")})



STAGES = [
    attention_stage("self0", 8, 64, "L0_xattn_Wq", "L0_xattn_Wk", "L0_xattn_Wv", "L0_xattn_Wo", "L0_xattn_bo"),
    quantised_stage("int8", prepare_int8),
    attention_stage("self1", 16, 16, "L1_xattn_w_q", "L1_xattn_w_k", "L1_xattn_w_v", "L1_xattn_w_o",
                    "L1_xattn_b_o", "L1_xattn_b_q", "L1_xattn_b_k", "L1_xattn_b_v"),
    experts_stage,
    global_attention_stage,
    quantised_stage("ternary", prepare_ternary),
    selective_stage,
    chosen_attention_stage,
]



def shape_tables():
    turn = 2.0 * np.pi / FREQ
    f = np.arange(S)
    t = np.arange(S)
    cos = np.cos(turn * np.outer(t, f))
    sin = np.sin(turn * np.outer(t, f))
    last = np.cos(np.pi * t)
    with_last = sin.copy()
    with_last[:, 0] = last
    weight = np.where(f == 0, 1.0, 2.0) / FREQ
    e = cos[:, 0:P].copy()
    e[:, 0] = last
    lag = 2.0 * np.concatenate([cos, sin, e], axis=1).reshape(SEQ_A, SEQ_B, 5 * P)
    half = np.repeat([0, 1], N_STATE)
    phase = np.zeros((P, 4))
    phase[:, 0] = np.where(half, 0.0, 0.25)
    phase[:, 1] = np.where(half, 0.25, 0.5)
    phase[:, 2] = np.where(half, 0.5, 0.25)
    inv_freq = 10000.0 ** -(np.arange(32) / 32.0)
    angle = np.outer(t, inv_freq)
    rotary = np.zeros((S, 2, P))
    rotary[:, 0, :] = np.concatenate([np.cos(angle), np.cos(angle), np.ones((S, 64))], axis=1)
    rotary[:, 1, 0:64] = np.concatenate([-np.sin(angle), np.sin(angle)], axis=1)
    n = np.arange(P)
    same = (n[:, None] // 32) == (n[None, :] // 32)
    tables = {"rotary": rotary, "upto": n[:, None] <= n[None, :],
              "slot_mask": np.where(same & (n[:, None] >= n[None, :]), 0.0, -1.0e30),
              "forward": np.concatenate([cos, with_last], axis=1),
              "backward": np.concatenate([(cos * weight).T, (with_last * weight).T], axis=0),
              "lag_transform": lag, "phase": phase,
              "steps": np.stack([SEQ_B * np.arange(SEQ_A), np.arange(SEQ_B)])}
    return {name: np.ascontiguousarray(a, dtype=np.float32) for name, a in tables.items()}


def lay_out(inputs):
    def array(name):
        return np.ascontiguousarray(inputs[name])

    def turned(name, *axes):
        return np.ascontiguousarray(np.transpose(array(name), axes or None))

    skip = {"ctx_768", "mask_BxS_bf1", "mask_BxS2_bf1", "L3_xattn_A_re", "L3_xattn_A_im", "L3_xattn_C_re",
            "L3_xattn_C_im", "L3_xattn_mod_gate", "L3_ffn_Wr", "L1_ffn_gate_w", "L1_ffn_expert_w", "L2_ffn_ternary_weight", "L2_ffn_act_scale"}
    arrays = {name: array(name) for name in inputs if name not in skip}
    arrays["ctx_t"] = np.ascontiguousarray(np.transpose(array("ctx_768"), (2, 0, 1)))
    arrays["gate_t"] = np.ascontiguousarray(array("L1_ffn_gate_w").T)
    arrays["expert_t"] = np.ascontiguousarray(np.transpose(array("L1_ffn_expert_w"), (2, 0, 1)))
    arrays["ternary_t"] = np.ascontiguousarray(array("L2_ffn_ternary_weight").T)
    arrays["act_scale"] = array("L2_ffn_act_scale").reshape(1)
    arrays["text_mask_t"] = np.ascontiguousarray(
        array("mask_BxS_bf1").view(np.uint8).reshape(TILES, P).T)
    arrays["vision_mask"] = array("mask_BxS2_bf1").view(np.uint8)
    arrays["wr_t"] = turned("L3_ffn_Wr")
    arrays["mod_gate"] = array("L3_xattn_mod_gate").reshape(1)
    for part in ("A_re", "A_im", "C_re", "C_im"):
        arrays[part.lower() + "_t"] = turned(f"L3_xattn_{part}")
    arrays.update(shape_tables())
    arrays["ident"] = np.eye(P, dtype=np.float32)
    arrays["iota"] = np.arange(P, dtype=np.float32)
    return arrays


def kernel(**inputs):
    import concourse.bacc as bacc
    from concourse.bass_utils import run_bass_kernel_spmd

    nc = bacc.Bacc("TRN2", target_bir_lowering=False, num_devices=1)
    arrays, io = {}, {}
    for name, a in lay_out(inputs).items():
        arrays[f"in_{name}"] = a
        io[name] = nc.dram_tensor(f"in_{name}", a.shape, mybir.dt.from_np(a.dtype), kind="ExternalInput").ap()
    out = nc.dram_tensor("out", (B, S, D), F32, kind="ExternalOutput").ap()
    program(nc, io, out, STAGES)
    result = run_bass_kernel_spmd(nc, [arrays], core_ids=[0])
    return result.results[0]["out"]
```
